# Optimizing a Trainium2 kernel written in Bass

```python
import numpy as np
import jax
import jax.numpy as jnp

def _softmax(x, axis=-1):
    return jax.nn.softmax(x, axis=axis)

def _gelu(x):
    return jax.nn.gelu(x, approximate=True)

def _silu(x):
    return jax.nn.silu(x)

def _sigmoid(x):
    return jax.nn.sigmoid(x)

def _layernorm(x, axis=-1, eps=1e-05):
    m = jnp.mean(x, axis=axis, keepdims=True)
    v = jnp.var(x, axis=axis, keepdims=True)
    return (x - m) / jnp.sqrt(v + eps)

def _scatter_add(tgt, idx, src, axis=0):
    return tgt.at[idx].add(src)

def _segment_sum(src, seg, n):
    return jax.ops.segment_sum(src, seg, n)
kernel_name = 'mk_flamingo_gated_d2_seqx_r4_83875e'

def setup_inputs(seed: int=0):
    np.random.seed(seed)
    _w = jnp.asarray

    def _rec_inputs():
        import jax
        import jax.numpy as jnp
        _rk = jax.random.key(seed)
        x = -0.0002928 + 1 * jax.random.normal(jax.random.fold_in(_rk, 1), (4, 512, 256), jnp.float32)
        _lenS = 512 - jax.random.randint(jax.random.fold_in(_rk, 7), (4,), 0, max(1, 512 // 4) + 1, jnp.int32)
        _lenS2 = 512 - jax.random.randint(jax.random.fold_in(_rk, 8), (4,), 0, max(1, 512 // 4) + 1, jnp.int32)
        _ctx_1024P = jax.random.normal(jax.random.fold_in(_rk, 11), (4, 16, 256), jnp.float32)
        _ctx_1024c = jax.random.dirichlet(jax.random.fold_in(_rk, 511), 0.3 * jnp.ones((16,), jnp.float32), (4, 512))
        _ctx_1024t = jnp.einsum('bsk,bkd->bsd', _ctx_1024c, _ctx_1024P)
        _ctx_1024t = _ctx_1024t * jax.lax.rsqrt(jnp.mean(jnp.square(_ctx_1024t)) + 1e-12) * 0.953939
        ctx_1024 = -1.39393e-06 + 0.999914 * (_ctx_1024t + 0.3 * jax.random.normal(jax.random.fold_in(_rk, 611), (4, 512, 256), jnp.float32))
        fside_BxSxS2_0 = -4.48278e-06 + 1.00019 * jax.random.normal(jax.random.fold_in(_rk, 13), (4, 512, 512), jnp.float32)
        _validS = jnp.arange(512)[None, :] < _lenS[:, None]
        _validS2 = jnp.arange(512)[None, :] < _lenS2[:, None]
        _causal = jnp.tril(jnp.ones((512, 512), dtype=bool))
        mask_BxS2_ik0 = jnp.where(jnp.broadcast_to(_validS2[:, :], (4, 512)), 0, 1).astype(jnp.int32)
        _g = jax.random.normal(jax.random.fold_in(_rk, 9001), (2, 2), jnp.float32)
        _g = jnp.sign(_g) * jnp.maximum(jnp.abs(_g), 1.0) + (_g == 0) * 1.0
        g_xattn = _g[0]
        g_ffn = _g[1]
        return (x, ctx_1024, fside_BxSxS2_0, mask_BxS2_ik0, g_xattn, g_ffn)
    x, ctx_1024, fside_BxSxS2_0, mask_BxS2_ik0, g_xattn, g_ffn = _rec_inputs()

    def _L0_xattn_setup():
        import math
        import jax, jax.numpy as jnp
        import numpy as np
        B, S, E, H = (2, 512, 256, 16)
        DK = E // H
        key = jax.random.key(seed)
        ks = jax.random.split(key, 12)
        sc = 1.0 / math.sqrt(E)
        return {'x': jax.random.normal(ks[0], (B, S, E), jnp.float32), 'kv': jax.random.normal(ks[1], (B, S, E), jnp.float32), 'mask': jax.random.randint(ks[2], (B, S), 0, 2, jnp.int32), 'attn_bias': jax.random.normal(ks[3], (B, S, S), jnp.float32), 'WQ_w': jax.random.normal(ks[4], (E, E), jnp.float32) * sc, 'WQ_b': jnp.zeros((E,), jnp.float32), 'WK_w': jax.random.normal(ks[5], (E, E), jnp.float32) * sc, 'WK_b': jnp.zeros((E,), jnp.float32), 'WV_w': jax.random.normal(ks[6], (E, E), jnp.float32) * sc, 'WV_b': jnp.zeros((E,), jnp.float32), 'WO_w': jax.random.normal(ks[7], (E, E), jnp.float32) * sc, 'WO_b': jnp.zeros((E,), jnp.float32)}
    _L0_xattn_all = _L0_xattn_setup()
    _L0_xattn_in = {k: v for k, v in _L0_xattn_all.items() if k in ('WQ_w', 'WQ_b', 'WK_w', 'WK_b', 'WV_w', 'WV_b', 'WO_w', 'WO_b')}
    del _L0_xattn_all

    def _L0_ffn_setup():
        import jax, jax.numpy as jnp
        import numpy as np
        B, N, DIM = (2, 512, 256)
        HEADS, DIM_HEAD, EXPERTS = (8, 64, 8)
        SCALE = DIM_HEAD ** (-0.5)
        key = jax.random.key(seed)
        ks = jax.random.split(key, 6)
        dim_inner = HEADS * DIM_HEAD
        return {'x': jax.random.normal(ks[0], (B, N, DIM), jnp.float32), 'w_q': jax.random.normal(ks[1], (DIM, dim_inner), jnp.float32) * 0.02, 'w_k': jax.random.normal(ks[2], (DIM, dim_inner), jnp.float32) * 0.02, 'w_gate': jax.random.normal(ks[3], (DIM, HEADS * EXPERTS), jnp.float32) * 0.02, 'value_experts': jax.random.normal(ks[4], (EXPERTS, HEADS, DIM, DIM_HEAD), jnp.float32) * 0.02, 'output_experts': jax.random.normal(ks[5], (EXPERTS, HEADS, DIM_HEAD, DIM), jnp.float32) * 0.02}
    _L0_ffn_all = _L0_ffn_setup()
    _L0_ffn_in = {k: v for k, v in _L0_ffn_all.items() if k in ('w_q', 'w_k', 'w_gate', 'value_experts', 'output_experts')}
    del _L0_ffn_all

    def _L1_xattn_setup():
        import jax, jax.numpy as jnp
        import numpy as np
        DIM = 256
        NUM_HEADS = 16
        DIM_HEAD = 64
        INNER = NUM_HEADS * DIM_HEAD
        SCALE = DIM_HEAD ** (-0.5)

        def _layernorm(x, gamma, beta, eps=1e-05):
            mu = jnp.mean(x, axis=-1, keepdims=True)
            var = jnp.mean(jnp.square(x - mu), axis=-1, keepdims=True)
            return (x - mu) * jax.lax.rsqrt(var + eps) * gamma + beta
        key = jax.random.key(seed)
        ks = jax.random.split(key, 8)
        B, SQ, SK = (2, 512, 1024)
        x = jax.random.normal(ks[0], (B, SQ, DIM), dtype=jnp.float32)
        context = jax.random.normal(ks[1], (B, SK, DIM), dtype=jnp.float32)
        ln_gamma = jnp.ones((DIM,), jnp.float32)
        ln_beta = jnp.zeros((DIM,), jnp.float32)
        w_q = jax.random.normal(ks[2], (DIM, INNER), dtype=jnp.float32) / np.sqrt(DIM)
        w_kv = jax.random.normal(ks[3], (DIM, 2 * INNER), dtype=jnp.float32) / np.sqrt(DIM)
        w_out = jax.random.normal(ks[4], (INNER, DIM), dtype=jnp.float32) / np.sqrt(INNER)
        b_out = jnp.zeros((DIM,), jnp.float32)
        gate = jnp.array([0.5], jnp.float32)
        return {'x': x, 'context': context, 'ln_gamma': ln_gamma, 'ln_beta': ln_beta, 'w_q': w_q, 'w_kv': w_kv, 'w_out': w_out, 'b_out': b_out, 'gate': gate}
    _L1_xattn_all = _L1_xattn_setup()
    _L1_xattn_in = {k: v for k, v in _L1_xattn_all.items() if k in ('ln_gamma', 'ln_beta', 'w_q', 'w_kv', 'w_out', 'b_out', 'gate')}
    del _L1_xattn_all

    def _L1_ffn_setup():
        import jax, jax.numpy as jnp
        import numpy as np
        B, T, D = (2, 256, 256)
        H, DK, K = (8, 128, 8)
        NKEYS = 64
        NEXP = NKEYS * NKEYS

        def _rmsnorm(x, w, eps=1e-06):
            inv = jax.lax.rsqrt(jnp.mean(x * x, axis=-1, keepdims=True) + eps)
            return x * inv * w
        key = jax.random.key(seed)
        ks = jax.random.split(key, 5)
        return {'x': jax.random.normal(ks[0], (B, T, D), jnp.float32), 'w_q': jax.random.normal(ks[1], (H * 2 * DK, D), jnp.float32) * 0.02, 'keys': jax.random.normal(ks[2], (H, NKEYS, 2, DK), jnp.float32) * 0.02, 'expert_down': jax.random.normal(ks[3], (NEXP, D), jnp.float32) * 0.02, 'expert_up': jax.random.normal(ks[4], (NEXP, D), jnp.float32) * 0.02, 'norm_w': jnp.ones((D,), jnp.float32)}
    _L1_ffn_all = _L1_ffn_setup()
    _L1_ffn_in = {k: v for k, v in _L1_ffn_all.items() if k in ('w_q', 'keys', 'expert_down', 'expert_up', 'norm_w')}
    del _L1_ffn_all
    return {'x': x, 'ctx_1024': ctx_1024, 'fside_BxSxS2_0': fside_BxSxS2_0, 'mask_BxS2_ik0': mask_BxS2_ik0, 'g_xattn': g_xattn, 'g_ffn': g_ffn, 'L0_xattn_WQ_w': _L0_xattn_in['WQ_w'], 'L0_xattn_WQ_b': _L0_xattn_in['WQ_b'], 'L0_xattn_WK_w': _L0_xattn_in['WK_w'], 'L0_xattn_WK_b': _L0_xattn_in['WK_b'], 'L0_xattn_WV_w': _L0_xattn_in['WV_w'], 'L0_xattn_WV_b': _L0_xattn_in['WV_b'], 'L0_xattn_WO_w': _L0_xattn_in['WO_w'], 'L0_xattn_WO_b': _L0_xattn_in['WO_b'], 'L0_ffn_w_q': _L0_ffn_in['w_q'], 'L0_ffn_w_k': _L0_ffn_in['w_k'], 'L0_ffn_w_gate': _L0_ffn_in['w_gate'], 'L0_ffn_value_experts': _L0_ffn_in['value_experts'], 'L0_ffn_output_experts': _L0_ffn_in['output_experts'], 'L1_xattn_ln_gamma': _L1_xattn_in['ln_gamma'], 'L1_xattn_ln_beta': _L1_xattn_in['ln_beta'], 'L1_xattn_w_q': _L1_xattn_in['w_q'], 'L1_xattn_w_kv': _L1_xattn_in['w_kv'], 'L1_xattn_w_out': _L1_xattn_in['w_out'], 'L1_xattn_b_out': _L1_xattn_in['b_out'], 'L1_xattn_gate': _L1_xattn_in['gate'], 'L1_ffn_w_q': _L1_ffn_in['w_q'], 'L1_ffn_keys': _L1_ffn_in['keys'], 'L1_ffn_expert_down': _L1_ffn_in['expert_down'], 'L1_ffn_expert_up': _L1_ffn_in['expert_up'], 'L1_ffn_norm_w': _L1_ffn_in['norm_w']}

def reference(x, ctx_1024, fside_BxSxS2_0, mask_BxS2_ik0, g_xattn, g_ffn, L0_xattn_WQ_w, L0_xattn_WQ_b, L0_xattn_WK_w, L0_xattn_WK_b, L0_xattn_WV_w, L0_xattn_WV_b, L0_xattn_WO_w, L0_xattn_WO_b, L0_ffn_w_q, L0_ffn_w_k, L0_ffn_w_gate, L0_ffn_value_experts, L0_ffn_output_experts, L1_xattn_ln_gamma, L1_xattn_ln_beta, L1_xattn_w_q, L1_xattn_w_kv, L1_xattn_w_out, L1_xattn_b_out, L1_xattn_gate, L1_ffn_w_q, L1_ffn_keys, L1_ffn_expert_down, L1_ffn_expert_up, L1_ffn_norm_w):
    import jax
    import jax.numpy as jnp

    def _L0_xattn_ref(x, kv, mask, attn_bias, WQ_w, WQ_b, WK_w, WK_b, WV_w, WV_b, WO_w, WO_b):
        import math
        import jax, jax.numpy as jnp
        import numpy as np
        B, S, E, H = (2, 512, 256, 16)
        DK = E // H
        b, sq, _ = x.shape
        sk = kv.shape[1]
        Q = (x @ WQ_w.T + WQ_b).reshape(b, sq, H, DK).transpose(0, 2, 1, 3)
        K = (kv @ WK_w.T + WK_b).reshape(b, sk, H, DK).transpose(0, 2, 1, 3)
        V = (kv @ WV_w.T + WV_b).reshape(b, sk, H, DK).transpose(0, 2, 1, 3)
        T = jnp.einsum('bhqd,bhkd->bhqk', Q, K) / math.sqrt(DK)
        T = T + attn_bias[:, None, :, :]
        m2 = jnp.einsum('bi,bj->bij', mask.astype(T.dtype), mask.astype(T.dtype))
        T = jnp.where(m2[:, None, :, :] == 0, jnp.asarray(-1000000000.0, T.dtype), T)
        A = jax.nn.softmax(T, axis=-1)
        out = jnp.einsum('bhqk,bhkd->bhqd', A, V)
        out = out.transpose(0, 2, 1, 3).reshape(b, sq, E)
        return out @ WO_w.T + WO_b

    def _L0_ffn_ref(x, w_q, w_k, w_gate, value_experts, output_experts):
        import jax, jax.numpy as jnp
        import numpy as np
        B, N, DIM = (2, 512, 256)
        HEADS, DIM_HEAD, EXPERTS = (8, 64, 8)
        SCALE = DIM_HEAD ** (-0.5)
        b, n, _ = x.shape
        q = (x @ w_q).reshape(b, n, HEADS, DIM_HEAD).transpose(0, 2, 1, 3)
        k = (x @ w_k).reshape(b, n, HEADS, DIM_HEAD).transpose(0, 2, 1, 3)
        gates = jax.nn.sigmoid((x @ w_gate).reshape(b, n, HEADS, EXPERTS).transpose(0, 2, 1, 3))
        sel = jnp.argmax(gates, axis=-1)
        gm = jax.nn.one_hot(sel, EXPERTS, dtype=x.dtype) * gates
        values = jnp.einsum('bhne,ehdk,bnd->bhnk', gm, value_experts, x)
        sim = jnp.einsum('bhid,bhjd->bhij', q * SCALE, k)
        causal_mask = jnp.triu(jnp.ones((n, n), dtype=bool), 1)
        sim = jnp.where(causal_mask, jnp.finfo(sim.dtype).min, sim)
        attn = jax.nn.softmax(sim, axis=-1)
        out = jnp.einsum('bhij,bhjk->bhik', attn, values)
        out = jnp.einsum('bhne,ehkd,bhnk->bhnd', gm, output_experts, out)
        return out.sum(axis=1)

    def _L1_xattn_ref(x, context, ln_gamma, ln_beta, w_q, w_kv, w_out, b_out, gate):
        import jax, jax.numpy as jnp
        import numpy as np
        DIM = 256
        NUM_HEADS = 16
        DIM_HEAD = 64
        INNER = NUM_HEADS * DIM_HEAD
        SCALE = DIM_HEAD ** (-0.5)

        def _layernorm(x, gamma, beta, eps=1e-05):
            mu = jnp.mean(x, axis=-1, keepdims=True)
            var = jnp.mean(jnp.square(x - mu), axis=-1, keepdims=True)
            return (x - mu) * jax.lax.rsqrt(var + eps) * gamma + beta
        B, SQ, _ = x.shape
        SK = context.shape[1]
        xn = _layernorm(x, ln_gamma, ln_beta)
        q = (xn @ w_q).reshape(B, SQ, NUM_HEADS, DIM_HEAD)
        kv = context @ w_kv
        k, v = jnp.split(kv, 2, axis=-1)
        k = k.reshape(B, SK, NUM_HEADS, DIM_HEAD)
        v = v.reshape(B, SK, NUM_HEADS, DIM_HEAD)
        scores = jnp.einsum('bqhd,bkhd->bhqk', q * SCALE, k)
        attn = jax.nn.softmax(scores, axis=-1)
        out = jnp.einsum('bhqk,bkhd->bqhd', attn, v).reshape(B, SQ, INNER)
        out = out @ w_out + b_out
        return out * jnp.tanh(gate[0])

    def _L1_ffn_ref(x, w_q, keys, expert_down, expert_up, norm_w):
        import jax, jax.numpy as jnp
        import numpy as np
        B, T, D = (2, 256, 256)
        H, DK, K = (8, 128, 8)
        NKEYS = 64
        NEXP = NKEYS * NKEYS

        def _rmsnorm(x, w, eps=1e-06):
            inv = jax.lax.rsqrt(jnp.mean(x * x, axis=-1, keepdims=True) + eps)
            return x * inv * w
        b, t, d = x.shape
        xn = _rmsnorm(x, norm_w)
        q = (xn @ w_q.T).reshape(b, t, H, 2, DK)
        sim1 = jnp.einsum('bthd,hkd->bthk', q[..., 0, :], keys[:, :, 0, :])
        sim2 = jnp.einsum('bthd,hkd->bthk', q[..., 1, :], keys[:, :, 1, :])
        s1, i1 = jax.lax.top_k(sim1, K)
        s2, i2 = jax.lax.top_k(sim2, K)
        all_idx = (i1[..., :, None] * NKEYS + i2[..., None, :]).reshape(b, t, H, K * K)
        all_sc = (s1[..., :, None] + s2[..., None, :]).reshape(b, t, H, K * K)
        fs, pk = jax.lax.top_k(all_sc, K)
        fi = jnp.take_along_axis(all_idx, pk, axis=-1)
        wd = expert_down[fi]
        wu = expert_up[fi]
        hidden = jax.nn.gelu(jnp.einsum('btd,bthkd->bthk', xn, wd), approximate=False)
        hidden = hidden * jax.nn.relu(fs)
        return jnp.einsum('bthk,bthkd->btd', hidden, wu)
    x = x + jnp.tanh(g_xattn[0]) * _L0_xattn_ref(_layernorm(x, axis=-1), ctx_1024, mask_BxS2_ik0, fside_BxSxS2_0, L0_xattn_WQ_w, L0_xattn_WQ_b, L0_xattn_WK_w, L0_xattn_WK_b, L0_xattn_WV_w, L0_xattn_WV_b, L0_xattn_WO_w, L0_xattn_WO_b)
    x = x + jnp.tanh(g_ffn[0]) * _L0_ffn_ref(_layernorm(x, axis=-1), L0_ffn_w_q, L0_ffn_w_k, L0_ffn_w_gate, L0_ffn_value_experts, L0_ffn_output_experts)
    x = x + jnp.tanh(g_xattn[1]) * _L1_xattn_ref(_layernorm(x, axis=-1), ctx_1024, L1_xattn_ln_gamma, L1_xattn_ln_beta, L1_xattn_w_q, L1_xattn_w_kv, L1_xattn_w_out, L1_xattn_b_out, L1_xattn_gate)
    x = x + jnp.tanh(g_ffn[1]) * _L1_ffn_ref(_layernorm(x, axis=-1), L1_ffn_w_q, L1_ffn_keys, L1_ffn_expert_down, L1_ffn_expert_up, L1_ffn_norm_w)
    return x

_drawn_inputs = setup_inputs


def setup_inputs(seed=0):
    import zlib

    import numpy as np

    out = dict(_drawn_inputs(seed))
    spreads = {'g_ffn': (-1.0, 0.6),
     'L0_xattn_WQ_b': (0.0, 0.8),
     'L0_xattn_WK_b': (0.0, 0.8),
     'L0_xattn_WV_b': (0.0, 0.1),
     'L0_xattn_WO_b': (0.0, 0.1),
     'L1_xattn_ln_gamma': (1.0, 0.6),
     'L1_xattn_ln_beta': (0.0, 0.8),
     'L1_xattn_b_out': (0.0, 0.1),
     'L1_ffn_norm_w': (1.0, 0.6)}
    factors = {'L0_ffn_w_q': 8.0,
     'L0_ffn_w_k': 8.0,
     'L0_ffn_w_gate': 8.0,
     'L0_ffn_value_experts': 7.783,
     'L0_ffn_output_experts': 7.851,
     'L1_ffn_w_q': 7.749,
     'L1_ffn_keys': 7.57,
     'L1_ffn_expert_down': 7.771,
     'L1_ffn_expert_up': 7.542}
    for name, (base, spread) in spreads.items():
        noise = np.random.default_rng([zlib.crc32(name.encode()), seed]).standard_normal(out[name].shape)
        drawn = base * np.exp(spread * noise) if base else spread * noise
        out[name] = jnp.asarray(drawn.astype(out[name].dtype))
    for name, factor in factors.items():
        out[name] = (out[name] * factor).astype(out[name].dtype)
    return out
```

```python
from contextlib import ExitStack

import numpy as np

import concourse.bass as bass
from concourse import mybir

F32 = mybir.dt.float32
BF16 = mybir.dt.bfloat16
I32 = mybir.dt.int32
U32 = mybir.dt.uint32
ALU = mybir.AluOpType
ACT = mybir.ActivationFunctionType
AX = mybir.AxisListType

P = 128
B, S, D = 4, 512, 256
QT = S // P
KC = D // P
EPS = 1e-5
MASKED = 1e9
CAUSAL = 3.0e38


class Signal:

    def __init__(self, nc, ctx, name, per):
        self.sem = ctx.enter_context(nc.semaphore(name))
        self.per = per

    def wait(self, eng, turn, n):
        eng.wait_ge(self.sem, turn * self.per + n)


TICKS = 16


def apart(eng, m):
    m["ticks"] += 1
    n = m["ticks"] % TICKS
    if eng is m["pool"]:
        eng.tensor_tensor(m["tick"][:, n:n + 1], m["cst"][:, 0:1], m["cst"][:, 1:2], ALU.mult)
    else:
        eng.memset(m["tick"][:, TICKS + n:TICKS + n + 1], 0.0)


class Attention:

    def __init__(self, heads, dk, group, causal=False):
        self.heads, self.dk, self.group, self.causal = heads, dk, group, causal
        self.width = heads * dk
        self.per_tile = P // dk
        self.tiles = heads // self.per_tile
        self.groups = heads // group
        self.strip = P // group
        self.units = heads * QT
        self.tile_units = self.per_tile * QT
        self.group_units = group * QT

    def unit(self, u):
        g, r = divmod(u, self.group_units)
        qt, j = divmod(r, self.group)
        return g, qt, j, g * self.group + j

    def keys(self, qt):
        return qt + 1 if self.causal else QT

    def first_of_tile(self, s):
        return s % self.tile_units == 0 and 0 <= s < self.units


A_ = Attention(16, 16, 4)
B_ = Attention(8, 64, 2, causal=True)
C_ = Attention(16, 64, 2)

EB, HB = 8, 8
HD, NK, TOP = 8, 64, 8
NSEL = HD * TOP
EHI, ELO = 128, 32


def build(nc, a, out, phases="ABCD"):
    with ExitStack() as ctx:
        def sb(name, shape, dt=F32):
            return ctx.enter_context(nc.sbuf_tensor(name, shape, dt))

        def sem(name):
            return ctx.enter_context(nc.semaphore(name))

        bank = [ctx.enter_context(nc.psum_tensor(f"bank{i}", [P, 512], F32)) for i in range(8)]
        m = {}
        m["bank"] = bank
        m["x"] = sb("x", [P, B * QT, D])
        m["ident"] = sb("ident", [P, P])
        m["cst"] = sb("cst", [P, 64])
        m["gates"] = sb("gates", [P, 8])
        m["cols"] = sb("cols", [P, 32])
        m["tick"], m["ticks"] = sb("tick", [P, 2 * TICKS]), 0
        m["pool"] = nc.gpsimd
        m["big1"] = sb("big1", [P, 8192])
        m["big2"] = sb("big2", [P, 8192])
        m["wab"] = sb("wab", [P, 5248])
        m["wc"] = sb("wc", [P, 8192])
        m["work"] = sb("work", [P, 18800])
        s = {n: sem(n) for n in ("x_loaded", "identity_made", "wa_loaded", "wb_loaded", "wbig_loaded",
                                 "wc_loaded", "scalars_loaded", "scalars_ready", "wd_loaded")}
        m["s"] = s
        prologue(nc, a, m)
        if "A" in phases:
            cross_attention(nc, a, m, A_, "A")
        if "B" in phases:
            moe_attention(nc, a, m)
        if "C" in phases:
            cross_attention(nc, a, m, C_, "C")
        if "D" in phases:
            product_key_experts(nc, a, m)
        epilogue(nc, out, m)


def carve(m, key="work"):
    at = [0]
    region = m[key]

    def take(*shape):
        n = int(np.prod(shape))
        v = region[:, at[0]:at[0] + n]
        at[0] += n
        if len(shape) == 2:
            v = v.rearrange("p (a b) -> p a b", b=shape[1])
        elif len(shape) == 3:
            v = v.rearrange("p (a b c) -> p a b c", b=shape[1], c=shape[2])
        return v
    return take


def weight_views(m):
    ta = carve(m, "wab")
    v = {}
    v["A.wq"], v["A.wk"], v["A.wv"] = ta(KC, 256), ta(KC, 256), ta(KC, 256)
    v["A.wo"] = ta(4, 256)
    v["A.bv"], v["A.bo"] = ta(256), ta(256)
    v["B.gate"], v["B.wq"], v["B.wk"] = ta(KC, HB * EB), ta(KC, 512), ta(KC, 512)
    tc = carve(m, "wc")
    v["C.wq"], v["C.wk"], v["C.wv"] = tc(KC, 1024), tc(KC, 1024), tc(KC, 1024)
    v["C.wo"] = tc(8, 256)
    return v


def prologue(nc, a, m):
    s, v = m["s"], weight_views(m)
    with nc.Block() as block:
        @block.sync
        def _(eng):
            eng.dma_start(m["x"][:, :, :], a["x"].rearrange("b (t p) d -> p (b t) d", p=P)).then_inc(s["x_loaded"], 16)
            for n, name in enumerate(("g_xattn", "g_ffn")):
                eng.dma_start(m["gates"][:, 2 * n:2 * n + 2],
                              a[name].rearrange("(a n) -> a n", a=1).to_broadcast([P, 2])
                              ).then_inc(s["scalars_loaded"], 16)
            eng.dma_start(m["gates"][:, 4:5], a["L1_xattn_gate"].rearrange("(a n) -> a n", a=1).to_broadcast([P, 1])
                          ).then_inc(s["scalars_loaded"], 16)
            for n, name in enumerate(("L0_xattn_WQ_b", "L0_xattn_WK_b", "L1_xattn_ln_gamma", "L1_xattn_ln_beta",
                                      "L1_ffn_norm_w")):
                eng.dma_start(m["cols"][:, 2 * n:2 * n + 2], a[name + ".cols"]).then_inc(s["scalars_loaded"], 16)
            for name, key in (("A.wq", "A.wqT"), ("A.wk", "A.wkT"), ("A.wv", "A.wvT")):
                eng.dma_start(v[name], a[key].rearrange("(c p) n -> p c n", p=P)).then_inc(s["wa_loaded"], 16)
            for name, key in (("A.bv", "L0_xattn_WV_b"), ("A.bo", "L0_xattn_WO_b")):
                eng.dma_start(v[name], a[key].rearrange("(a n) -> a n", a=1).to_broadcast([P, 256])
                              ).then_inc(s["wa_loaded"], 16)
            for name, key in (("B.gate", "L0_ffn_w_gate"), ("B.wq", "L0_ffn_w_q"), ("B.wk", "L0_ffn_w_k")):
                eng.dma_start(v[name], a[key].rearrange("(c p) n -> p c n", p=P)).then_inc(s["wb_loaded"], 16)
            eng.wait_ge(s["identity_made"], 4)
            for j in range(4):
                eng.dma_start(v["A.wo"][32 * j:32 * j + 16, :, :],
                              a["A.woT"].rearrange("(g j r) n -> j r g n", j=4, r=16)[j]).then_inc(s["wa_loaded"], 16)

        @block.gpsimd
        def _(eng):
            eng.memset(m["ident"][:, :], 0.0).then_inc(s["identity_made"], 1)
            eng.wait_ge(s["identity_made"], 1)
            eng.affine_select(out=m["ident"][:, :], in_=m["ident"][:, :], compare_op=ALU.not_equal, fill=1.0,
                              base=0, pattern=[[-1, P]], channel_multiplier=1).then_inc(s["identity_made"], 1)
            eng.memset(m["cst"][:, :], 1.0).then_inc(s["identity_made"], 1)
            eng.memset(v["A.wo"], 0.0).then_inc(s["identity_made"], 1)
            eng.wait_ge(s["identity_made"], 4)
            n = 4
            for at, count, rows in ((0, 8, 16), (8, 2, 64)):
                part = m["cst"][:, at:at + count]
                eng.affine_select(out=part, in_=part, compare_op=ALU.is_ge, fill=0.0, base=0,
                                  pattern=[[-rows, count]], channel_multiplier=1).then_inc(s["identity_made"], 1)
                n += 1
                eng.wait_ge(s["identity_made"], n)
                eng.affine_select(out=part, in_=part, compare_op=ALU.is_ge, fill=0.0, base=rows - 1,
                                  pattern=[[rows, count]], channel_multiplier=-1).then_inc(s["identity_made"], 1)
                n += 1

        @block.scalar
        def _(eng):
            eng.wait_ge(s["scalars_loaded"], 8 * 16)
            eng.activation(m["gates"][:, 0:5], m["gates"][:, 0:5], ACT.Tanh).then_inc(s["scalars_ready"], 1)

        @block.vector
        def _(eng):
            eng.wait_ge(s["scalars_ready"], 1)
            eng.tensor_tensor(m["gates"][:, 5:6], m["gates"][:, 1:2], m["gates"][:, 4:5], ALU.mult
                              ).then_inc(s["scalars_ready"], 1)


def epilogue(nc, out, m):
    with ExitStack() as ctx:
        stored = ctx.enter_context(nc.semaphore("stored"))
        with nc.Block() as block:
            @block.sync
            def _(eng):
                eng.dma_start(out.rearrange("b (t p) d -> p (b t) d", p=P), m["x"][:, :, :]).then_inc(stored, 16)
                eng.wait_ge(stored, 16)


def layer_norm(nc, ctx, m, name, rounds, source, xn, scratch, affine=None):
    NT = B * QT
    stats, mv = scratch(NT, 6), scratch(NT, 2)
    std, rstd, t1, t2 = scratch(NT), scratch(NT), scratch(NT), scratch(NT)
    var_ready = ctx.enter_context(nc.semaphore(name + "_var_ready"))
    std_ready = ctx.enter_context(nc.semaphore(name + "_std_ready"))
    step = ctx.enter_context(nc.semaphore(name + "_stat_step"))
    done = ctx.enter_context(nc.semaphore(name + "_xn_ready"))

    def on_scalar(eng):
        for r in range(rounds):
            eng.wait_ge(var_ready, r + 1)
            eng.activation(std, mv[:, :, 1], ACT.Sqrt).then_inc(std_ready, 1)

    def on_vector(eng):
        n = 0
        for r in range(rounds):
            kind = "rms" if name[0] == "D" and r == rounds - 1 else "ln"
            src = source if r == 0 else xn
            if r:
                eng.wait_ge(done, NT * r)
            for t in range(NT):
                eng.bn_stats(stats[:, t, :], src[:, t, :]).then_inc(step, 1)
            n += NT
            for t in range(NT):
                eng.wait_ge(step, n - NT + t + 1)
                eng.bn_aggr(mv[:, t, :], stats[:, t, :]).then_inc(step, 1)
            n += NT
            eng.wait_ge(step, n)
            if kind == "rms":
                eng.tensor_tensor(t1, mv[:, :, 0], mv[:, :, 0], ALU.mult).then_inc(step, 1)
                eng.wait_ge(step, n + 1)
                eng.tensor_tensor(mv[:, :, 1], mv[:, :, 1], t1, ALU.add).then_inc(step, 1)
                n += 2
                eng.wait_ge(step, n)
            eng.tensor_scalar(mv[:, :, 1], mv[:, :, 1], 1e-6 if kind == "rms" else EPS, None, ALU.add
                              ).then_inc(var_ready, 1)
            eng.wait_ge(std_ready, r + 1)
            eng.reciprocal(rstd, std).then_inc(step, 1)
            eng.wait_ge(step, n + 1)
            eng.tensor_tensor(t1, rstd, rstd, ALU.mult).then_inc(step, 1)
            eng.wait_ge(step, n + 2)
            eng.tensor_tensor(t2, t1, mv[:, :, 1], ALU.mult).then_inc(step, 1)
            eng.wait_ge(step, n + 3)
            eng.tensor_scalar(t1, t2, -0.5, 1.5, ALU.mult, ALU.add).then_inc(step, 1)
            eng.wait_ge(step, n + 4)
            eng.tensor_tensor(rstd, rstd, t1, ALU.mult).then_inc(step, 1)
            n += 5
            eng.wait_ge(step, n)
            if affine:
                scale, shift = affine
                if r == 0:
                    eng.tensor_copy(scale, rstd).then_inc(step, 1)
                    eng.tensor_scalar(shift, mv[:, :, 0], -1.0, None, ALU.mult).then_inc(step, 1)
                    n += 2
                    eng.wait_ge(step, n)
                else:
                    eng.tensor_tensor(scale, scale, rstd, ALU.mult).then_inc(step, 1)
                    eng.wait_ge(step, n + 1)
                    eng.tensor_tensor(shift, shift, scale, ALU.mult).then_inc(done, 1)
                    n += 1
                    continue
            for t in range(NT):
                eng.tensor_scalar(xn[:, t, :], src[:, t, :], mv[:, t, 0:1], rstd[:, t:t + 1],
                                  ALU.subtract, ALU.mult).then_inc(done, 1)
    return on_scalar, on_vector, done, NT * rounds if affine is None else NT * (rounds - 1) + 1


def cross_attention(nc, a, m, A, name):
    masked = name == "A"
    s, v = m["s"], weight_views(m)
    bank, ident, x = m["bank"], m["ident"], m["x"]
    SB, TB, OB, MB = bank[0:2], bank[2:4], bank[4:6], bank[6:8]
    wq, wk, wv, wo = (v[f"{name}.{w}"] for w in ("wq", "wk", "wv", "wo"))
    GS, U, T = A.group_units, A.units, A.tiles
    headmask = m["cst"][:, 0:8] if name == "A" else m["cst"][:, 8:10]
    gate = m["gates"][:, 0:1] if name == "A" else m["gates"][:, 5:6]
    take, big1, big2 = carve(m), carve(m, "big1"), carve(m, "big2")
    NS, PTR = 3, 2 * A.group
    xn = big1(B * QT, D)
    ctxT = big2(KC, B * S)
    vtok = big1(QT, A.width)
    xstage = take(QT, D)
    xnT, ctxb = take(KC, S), take(KC, S)
    qT, kT = take(2, S), take(S)
    prob = take(NS, S)
    pT = take(PTR, QT * P)
    rbs = take(S)
    rmat = take(2 * GS, A.dk)
    low, rowsum, rinv = take(U), take(U), take(U)
    y = take(2, D)
    if masked:
        kz = carve(m, "wc")(2 * A.per_tile, S)
        bneg, onorm, braw = big1(QT, S), big2(A.groups, S), big2(QT, S)
        sneg = take(NS, S)
        mrow, qrow, mm, bt = take(S), take(S), take(S), take(S)
        mraw, mcraw, mcol = take(S).bitcast(I32), take(QT).bitcast(I32), take(QT)
    else:
        kz, onorm, bo = take(2 * A.per_tile, S), take(A.groups, S), take(D)

    with ExitStack() as ctx:
        def sig(what, per):
            return Signal(nc, ctx, f"{name}_{what}", per)

        turn_done = sig("x_updated", QT)
        ctx_loaded = ctx.enter_context(nc.semaphore(f"{name}_ctx_loaded"))
        bias_loaded = sig("bias_loaded", 48)
        bo_loaded = ctx.enter_context(nc.semaphore(f"{name}_bo_loaded"))
        bias_step = sig("bias_step", 4 + 4 * QT)
        cleared = ctx.enter_context(nc.semaphore(f"{name}_cleared"))
        rows_ready = sig("rows_ready", 1)
        staged = sig("x_and_ctx_staged", 2)
        xt_made = sig("xn_transposed", KC)
        xt_ready = sig("xnT_ready", KC)
        v_made, v_ready = sig("v_made", QT * max(1, A.width // 512)), sig("v_ready", QT * max(1, A.width // 512))
        qk_made, q_ready, k_ready = sig("qk_made", 2 * T), sig("q_ready", T), sig("k_ready", T)
        kz_ready = sig("kz_ready", T)
        s_made, low_ready = sig("scores_made", U), sig("low_ready", U)
        p_ready = sig("probs_ready", U)
        t_made = sig("probs_transposed", U)
        pt_even, pt_odd = sig("pT_even_ready", U // 2), sig("pT_odd_ready", U // 2)
        av_done = sig("av_done", A.groups * QT)
        rinv_ready = sig("rinv_ready", A.groups)
        rmat_ready = sig("rmat_ready", A.groups)
        rb_made, rb_copied = sig("rb_made", A.groups), sig("rb_copied", A.groups)
        on_ready = sig("onorm_ready", A.groups)
        out_made, y_ready = sig("out_made", QT), sig("y_ready", QT)
        ln_act, ln_dve, xn_done, xn_count = layer_norm(nc, ctx, m, name, 1 if name == "A" else 2, x, xn, take)

        STEPS = U + 7
        def vchunks():
            return [(kt, c) for kt in range(QT) for c in range(max(1, A.width // 512))]
        VW = min(512, A.width)

        def closes_pass(u):
            return 0 <= u < U and u % A.group == A.group - 1

        def closes_group(u):
            return 0 <= u < U and u % GS == GS - 1

        def tile_at(step):
            if step == 0:
                return 0
            u = step + 5
            return u // A.tile_units if u < U and u % A.tile_units == 0 and u > 5 else None

        def groups_before(step):
            return sum(closes_group(z - 6) for z in range(step))

        def tiles_until(step):
            return sum(tile_at(z) is not None for z in range(step + 1))

        with nc.Block() as block:
            @block.sync
            def _(eng):
                eng.dma_start(ctxT, a["ctxT"].rearrange("(c p) n -> p c n", p=P)).then_inc(ctx_loaded, 16)
                if name == "C":
                    for w, key in (("C.wq", "L1_xattn_w_q"), ("C.wk", "C.wk"), ("C.wv", "C.wv"), ("C.wo", "L1_xattn_w_out")):
                        eng.dma_start(v[w], a[key].rearrange("(c p) n -> p c n", p=P)).then_inc(s["wc_loaded"], 16)
                    eng.dma_start(bo, a["L1_xattn_b_out"].rearrange("(a n) -> a n", a=1).to_broadcast([P, D])
                                  ).then_inc(bo_loaded, 16)
                if masked:
                    with eng.Fori(0, B) as b:
                        bias_step.wait(eng, b, 0)
                        eng.dma_start(braw, a["bias"][b].rearrange("(t p) k -> p t k", p=P)).then_inc(bias_loaded.sem, 16)
                        eng.dma_start(mraw, a["mask"][b].rearrange("(a k) -> a k", a=1).to_broadcast([P, S])).then_inc(bias_loaded.sem, 16)
                        eng.dma_start(mcraw, a["mask.cols"][b]).then_inc(bias_loaded.sem, 16)

            @block.gpsimd
            def _(eng):
                with eng.Fori(0, B) as b:
                    turn_done.wait(eng, b, 0)
                    if masked:
                        bias_loaded.wait(eng, b, 48)
                        apart(eng, m)
                        eng.tensor_scalar(mrow, mraw, 0.0, None, ALU.is_equal).then_inc(bias_step.sem, 1)
                        eng.tensor_scalar(mcol, mcraw, 0.0, None, ALU.is_equal).then_inc(bias_step.sem, 1)
                        bias_step.wait(eng, b, 2)
                        apart(eng, m)
                        eng.tensor_scalar(qrow, mrow, A.dk ** -0.5, -(A.dk ** -0.5), ALU.mult, ALU.add
                                          ).then_inc(bias_step.sem, 1)
                        eng.tensor_scalar(mcol, mcol, -1.0, 1.0, ALU.mult, ALU.add).then_inc(bias_step.sem, 1)
                        bias_step.wait(eng, b, 4)
                        apart(eng, m)
                        eng.tensor_scalar(mrow, mrow, -1.0, 1.0, ALU.mult, ALU.add).then_inc(rows_ready.sem, 1)
                        rows_ready.wait(eng, b, 1)
                        for t in range(QT):
                            n = 4 + 4 * t
                            apart(eng, m)
                            eng.tensor_scalar(mm, mrow, mcol[:, t:t + 1], None, ALU.mult).then_inc(bias_step.sem, 1)
                            bias_step.wait(eng, b, n + 1)
                            eng.tensor_tensor(bt, braw[:, t, :], mm, ALU.mult).then_inc(bias_step.sem, 1)
                            eng.tensor_scalar(mm, mm, -MASKED, MASKED, ALU.mult, ALU.add).then_inc(bias_step.sem, 1)
                            bias_step.wait(eng, b, n + 3)
                            eng.tensor_tensor(bneg[:, t, :], mm, bt, ALU.subtract).then_inc(bias_step.sem, 1)
                            bias_step.wait(eng, b, n + 4)
                    for step in range(STEPS):
                        t = tile_at(step)
                        if t is not None:
                            k_ready.wait(eng, b, t + 1)
                            if t >= 2:
                                s_made.wait(eng, b, (t - 1) * A.tile_units)
                            apart(eng, m)
                            for j in range(A.per_tile):
                                last = eng.tensor_scalar(kz[:, (t % 2) * A.per_tile + j, :], kT, headmask[:, j:j + 1],
                                                         None, ALU.mult)
                            last.then_inc(kz_ready.sem, 1)
                        if closes_group(step - 5):
                            g = (step - 5) // GS
                            rinv_ready.wait(eng, b, g + 1)
                            if g >= 2:
                                rb_made.wait(eng, b, g - 1)
                            apart(eng, m)
                            eng.tensor_copy(rmat[:, (g % 2) * GS:(g % 2 + 1) * GS, :],
                                            rinv[:, g * GS:(g + 1) * GS].unsqueeze(2).to_broadcast([P, GS, A.dk])
                                            ).then_inc(rmat_ready.sem, 1)

            @block.tensor
            def _(eng):
                eng.wait_ge(s["identity_made"], 8)
                if masked:
                    eng.wait_ge(cleared, 2)
                eng.wait_ge(s["wa_loaded" if masked else "wc_loaded"], 16 * (9 if masked else 4))
                with eng.Fori(0, B) as b:
                    staged.wait(eng, b, 2)
                    for c in range(KC):
                        for t in range(QT):
                            last = eng.transpose(MB[c][:, t * P:(t + 1) * P], xstage[:, t, c * P:(c + 1) * P], ident[:, :])
                        last.then_inc(xt_made.sem, 1)
                    for n, (kt, c) in enumerate(vchunks()):
                        if n >= 2:
                            v_ready.wait(eng, b, n - 1)
                        for kc in range(KC):
                            last = eng.matmul(SB[n % 2][:, 0:VW], ctxb[:, kc, kt * P:(kt + 1) * P],
                                              wv[:, kc, c * VW:(c + 1) * VW], start=(kc == 0), stop=(kc == KC - 1))
                        last.then_inc(v_made.sem, 1)
                    for step in range(STEPS):
                        t = tile_at(step)
                        if t is not None:
                            if t == 0:
                                xt_ready.wait(eng, b, KC)
                            else:
                                k_ready.wait(eng, b, t)
                                if groups_before(step):
                                    rb_copied.wait(eng, b, groups_before(step))
                            for kc in range(KC):
                                last = eng.matmul(MB[0][:, :], wq[:, kc, t * P:(t + 1) * P], xnT[:, kc, :],
                                                  start=(kc == 0), stop=(kc == KC - 1))
                            last.then_inc(qk_made.sem, 1)
                            for kc in range(KC):
                                last = eng.matmul(MB[1][:, :], wk[:, kc, t * P:(t + 1) * P], ctxb[:, kc, :],
                                                  start=(kc == 0), stop=(kc == KC - 1))
                            last.then_inc(qk_made.sem, 1)
                        if step < U:
                            g, qt, j, h = A.unit(step)
                            tl, hj = divmod(h, A.per_tile)
                            if A.first_of_tile(step):
                                kz_ready.wait(eng, b, tl + 1)
                                q_ready.wait(eng, b, tl + 1)
                            if step >= 2:
                                (low_ready if masked else p_ready).wait(eng, b, step - 1)
                            else:
                                v_ready.wait(eng, b, len(vchunks()))
                            eng.matmul(SB[step % 2][:, :], qT[:, tl % 2, qt * P:(qt + 1) * P],
                                       kz[:, (tl % 2) * A.per_tile + hj, :], start=True, stop=True
                                       ).then_inc(s_made.sem, 1)
                        u = step - 2
                        if 0 <= u < U:
                            p_ready.wait(eng, b, u + 1)
                            if u >= 2:
                                (pt_even if u % 2 == 0 else pt_odd).wait(eng, b, u // 2)
                            for kt in range(QT):
                                last = eng.transpose(TB[u % 2][:, kt * P:(kt + 1) * P],
                                                     prob[:, u % NS, kt * P:(kt + 1) * P], ident[:, :])
                            last.then_inc(t_made.sem, 1)
                        u = step - 4
                        if closes_pass(u):
                            g, qt, _, _ = A.unit(u)
                            pt_even.wait(eng, b, (u + 1) // 2)
                            pt_odd.wait(eng, b, (u + 1) // 2)
                            if qt == 0 and g >= 2:
                                on_ready.wait(eng, b, g - 1)
                            for kt in range(QT):
                                for j in range(A.group):
                                    h = g * A.group + j
                                    un = u - A.group + 1 + j
                                    r = A.strip * j
                                    last = eng.matmul(OB[g % 2][r:r + A.dk, qt * P:(qt + 1) * P],
                                                      vtok[:, kt, h * A.dk:(h + 1) * A.dk],
                                                      pT[:, un % PTR, kt * P:(kt + 1) * P],
                                                      start=(kt == 0), stop=(kt == QT - 1))
                            last.then_inc(av_done.sem, 1)
                        u = step - 6
                        if closes_group(u):
                            g = u // GS
                            rmat_ready.wait(eng, b, g + 1)
                            k_ready.wait(eng, b, tiles_until(step))
                            if g >= 1:
                                rb_copied.wait(eng, b, g)
                            for qt in range(QT):
                                for j in range(A.group):
                                    r = A.strip * j
                                    last = eng.matmul(MB[1][r:r + A.dk, qt * P:(qt + 1) * P],
                                                      rmat[:, (g % 2) * GS + qt * A.group + j, 0:A.dk], ident[:, :],
                                                      start=True, stop=True)
                            last.then_inc(rb_made.sem, 1)
                    on_ready.wait(eng, b, A.groups)
                    for t in range(QT):
                        if t >= 2:
                            y_ready.wait(eng, b, t - 1)
                        NG = A.groups
                        for g in range(NG):
                            last = eng.matmul(SB[t % 2][:, 0:D], onorm[:, g, t * P:(t + 1) * P], wo[:, g, :],
                                              start=(g == 0), stop=(g == NG - 1))
                        last.then_inc(out_made.sem, 1)

            @block.scalar
            def _(eng):
                ln_act(eng)
                eng.wait_ge(xn_done, xn_count)
                eng.wait_ge(ctx_loaded, 16)
                with eng.Fori(0, B) as b:
                    turn_done.wait(eng, b, 0)
                    eng.activation(xstage, xn[:, bass.ts(b, QT), :], ACT.Copy).then_inc(staged.sem, 1)
                    eng.activation(ctxb, ctxT[:, :, bass.ts(b, S)], ACT.Copy).then_inc(staged.sem, 1)
                    for n, (kt, c) in enumerate(vchunks()):
                        if not masked:
                            v_made.wait(eng, b, n + 1)
                            eng.activation(vtok[:, kt, c * VW:(c + 1) * VW], SB[n % 2][:, 0:VW], ACT.Copy
                                           ).then_inc(v_ready.sem, 1)
                    for step in range(STEPS):
                        if step < U:
                            low_ready.wait(eng, b, step + 1)
                            if step >= NS:
                                t_made.wait(eng, b, step - NS + 1)
                            src = sneg[:, step % NS, :] if masked else SB[step % 2][:, :]
                            done = eng.activation(prob[:, step % NS, :], src, ACT.Exp, bias=low[:, step:step + 1],
                                                  scale=-1.0 if masked else 1.0, accum_out=rowsum[:, step:step + 1])
                            done.then_inc(p_ready.sem, 1)
                        u = step - 2
                        if 0 <= u < U and u % 2 == 1:
                            t_made.wait(eng, b, u + 1)
                            if u >= PTR:
                                av_done.wait(eng, b, u // A.group - 1)
                            eng.activation(pT[:, u % PTR, :], TB[u % 2][:, :], ACT.Copy).then_inc(pt_odd.sem, 1)
                        u = step - 6
                        if closes_group(u):
                            g = u // GS
                            rb_made.wait(eng, b, g + 1)
                            if g >= 1:
                                on_ready.wait(eng, b, g)
                            eng.activation(rbs, MB[1][:, :], ACT.Copy).then_inc(rb_copied.sem, 1)

            @block.vector
            def _(eng):
                eng.wait_ge(s["x_loaded"], 16)
                eng.wait_ge(s["scalars_ready"], 2)
                eng.wait_ge(s["identity_made"], 8)
                if masked:
                    for k in OB:
                        eng.memset(k[:, :], 0.0).then_inc(cleared, 1)
                    eng.wait_ge(s["wa_loaded"], 16 * 9)
                else:
                    eng.wait_ge(bo_loaded, 16)
                ln_dve(eng)
                with eng.Fori(0, B) as b:
                    for c in range(KC):
                        xt_made.wait(eng, b, c + 1)
                        if masked:
                            eng.tensor_copy(xnT[:, c, :], MB[c][:, :]).then_inc(xt_ready.sem, 1)
                        else:
                            eng.tensor_scalar(xnT[:, c, :], MB[c][:, :], m["cols"][:, 4 + c:5 + c],
                                              m["cols"][:, 6 + c:7 + c], ALU.mult, ALU.add).then_inc(xt_ready.sem, 1)
                    if masked:
                        for n, (kt, c) in enumerate(vchunks()):
                            v_made.wait(eng, b, n + 1)
                            eng.tensor_tensor(vtok[:, kt, :], SB[n % 2][:, 0:VW], v["A.bv"], ALU.add
                                              ).then_inc(v_ready.sem, 1)
                    for step in range(STEPS):
                        t = tile_at(step)
                        if t is not None:
                            qk_made.wait(eng, b, 2 * t + 1)
                            if t == 0 and masked:
                                rows_ready.wait(eng, b, 1)
                            if t >= 2:
                                s_made.wait(eng, b, (t - 1) * A.tile_units)
                            if masked:
                                eng.scalar_tensor_tensor(out=qT[:, t % 2, :], in0=MB[0][:, :],
                                                         scalar=m["cols"][:, t:t + 1], in1=qrow,
                                                         op0=ALU.add, op1=ALU.mult).then_inc(q_ready.sem, 1)
                            else:
                                eng.tensor_scalar(qT[:, t % 2, :], MB[0][:, :], A.dk ** -0.5, None, ALU.mult
                                                  ).then_inc(q_ready.sem, 1)
                            qk_made.wait(eng, b, 2 * t + 2)
                            if t >= 1:
                                kz_ready.wait(eng, b, t)
                            if masked:
                                eng.scalar_tensor_tensor(out=kT, in0=MB[1][:, :], scalar=m["cols"][:, 2 + t:3 + t],
                                                         in1=mrow, op0=ALU.add, op1=ALU.mult).then_inc(k_ready.sem, 1)
                            else:
                                eng.tensor_copy(kT, MB[1][:, :]).then_inc(k_ready.sem, 1)
                        if step < U:
                            g, qt, j, h = A.unit(step)
                            s_made.wait(eng, b, step + 1)
                            if masked:
                                if step < QT:
                                    bias_step.wait(eng, b, 4 + 4 * QT)
                                if step >= NS:
                                    p_ready.wait(eng, b, step - NS + 1)
                                apart(eng, m)
                                eng.tensor_tensor_reduce(sneg[:, step % NS, :], SB[step % 2][:, :], bneg[:, qt, :],
                                                         1.0, 3.0e38, ALU.add, ALU.min, low[:, step:step + 1]
                                                         ).then_inc(low_ready.sem, 1)
                            else:
                                eng.tensor_reduce(low[:, step:step + 1], SB[step % 2][:, :], AX.X, ALU.max,
                                                  negate=True).then_inc(low_ready.sem, 1)
                        u = step - 2
                        if 0 <= u < U and u % 2 == 0:
                            t_made.wait(eng, b, u + 1)
                            if u >= PTR:
                                av_done.wait(eng, b, u // A.group - 1)
                            eng.tensor_copy(pT[:, u % PTR, :], TB[u % 2][:, :]).then_inc(pt_even.sem, 1)
                        u = step - 4
                        if closes_group(u):
                            g = u // GS
                            p_ready.wait(eng, b, (g + 1) * GS)
                            eng.reciprocal(rinv[:, g * GS:(g + 1) * GS], rowsum[:, g * GS:(g + 1) * GS]
                                           ).then_inc(rinv_ready.sem, 1)
                        u = step - 6
                        if closes_group(u):
                            g = u // GS
                            rb_copied.wait(eng, b, g + 1)
                            av_done.wait(eng, b, (g + 1) * QT)
                            eng.tensor_tensor(onorm[:, g, :], OB[g % 2][:, :], rbs, ALU.mult).then_inc(on_ready.sem, 1)
                    for t in range(QT):
                        out_made.wait(eng, b, t + 1)
                        eng.tensor_tensor(y[:, t % 2, :], SB[t % 2][:, 0:D], v["A.bo"] if masked else bo, ALU.add
                                          ).then_inc(y_ready.sem, 1)
                        y_ready.wait(eng, b, t + 1)
                        xt = x[:, b * QT + t, :]
                        eng.scalar_tensor_tensor(out=xt, in0=y[:, t % 2, :], scalar=gate, in1=xt,
                                                 op0=ALU.mult, op1=ALU.add).then_inc(turn_done.sem, 1)


def moe_attention(nc, a, m):
    A = B_
    s, v = m["s"], weight_views(m)
    bank, ident, x = m["bank"], m["ident"], m["x"]
    SB, TB, OB, MB = bank[0:2], bank[2:4], bank[4:6], bank[6:8]
    wq, wk, wgate = v["B.wq"], v["B.wk"], v["B.gate"]
    GS, U, T, DK = A.group_units, A.units, A.tiles, A.dk
    headmask, gate = m["cst"][:, 8:10], m["gates"][:, 2:3]
    take, wide = carve(m), carve(m, "wc")
    NS, PTR, NG = 3, 2 * A.group, 3
    w_val = carve(m, "big1")(KC, HB * EB * DK)
    w_out = carve(m, "big2")(HB * EB // 2, D)
    xn, vtok, otok = wide(B * QT, D), wide(QT, A.width), wide(QT, A.width)
    xstage, xnT = take(QT, D), take(KC, S)
    qT, kT, kz = take(2, S), take(S), take(2 * A.per_tile, S)
    prob, sneg, pT = take(NS, S), take(NS, S), take(PTR, QT * P)
    low, rowsum, rinv = take(U), take(U), take(U)
    oT = take(S)
    gates, hit, gm, gmr = (take(QT * HB, EB) for _ in range(4))
    best, rev = take(QT * HB), take(EB)
    scaled, spread, spreadT = take(NG, EB * DK), take(NG, EB * DK), take(NG, EB * DK)
    cneg = take(S)
    VU = QT * HB

    with ExitStack() as ctx:
        def sig(what, per):
            return Signal(nc, ctx, f"B_{what}", per)

        turn_done = sig("x_updated", QT)
        val_loaded = ctx.enter_context(nc.semaphore("B_val_loaded"))
        out_loaded = ctx.enter_context(nc.semaphore("B_out_loaded"))
        consts = ctx.enter_context(nc.semaphore("B_consts_made"))
        staged, xt_made, xt_ready = sig("staged", 1), sig("xn_transposed", KC), sig("xnT_ready", KC)
        gate_made, gate_ready, pick = sig("gate_made", 1), sig("gate_ready", 1), sig("pick_step", 6)
        val_made, val_scaled, v_ready = sig("val_made", VU), sig("val_scaled", VU), sig("v_ready", VU)
        qk_made, q_ready, k_ready = sig("qk_made", 2 * T), sig("q_ready", T), sig("k_ready", T)
        kz_ready = sig("kz_ready", T)
        s_made, low_ready, p_ready = sig("scores_made", U), sig("low_ready", U), sig("probs_ready", U)
        t_made = sig("probs_transposed", U)
        pt_even, pt_odd = sig("pT_even_ready", U // 2), sig("pT_odd_ready", U // 2)
        av_done, rinv_ready, gmr_ready = sig("av_done", A.groups * QT), sig("rinv_ready", A.groups), sig("gmr_ready", A.groups)
        ot_ready, heads_made, otok_ready = sig("oT_ready", A.groups), sig("heads_made", A.groups), sig("otok_ready", A.groups)
        sp_ready, spt_made, spt_ready = sig("spread_ready", VU), sig("spread_transposed", VU), sig("spreadT_ready", VU)
        sp_used = sig("spread_used", VU)
        ln_act, ln_dve, xn_done, xn_count = layer_norm(nc, ctx, m, "B", 1, x, xn, take)

        STEPS = U + 8

        def closes_pass(u):
            return 0 <= u < U and u % A.group == A.group - 1

        def closes_group(u):
            return 0 <= u < U and u % GS == GS - 1

        def tile_at(step):
            u = step + 5
            return u // A.tile_units if u < U and u % A.tile_units == 0 and u > 5 else None

        def groups_before(step):
            return sum(closes_group(z - 7) for z in range(step))

        def tiles_until(step):
            return 1 + sum(tile_at(z) is not None for z in range(step + 1))

        with nc.Block() as block:
            @block.sync
            def _(eng):
                for c in range(KC):
                    for n in range(2):
                        half = HB * EB * DK // 2
                        eng.dma_start(w_val[:, c, n * half:(n + 1) * half],
                                      a["B.val"][c * P:(c + 1) * P, n * half:(n + 1) * half]).then_inc(val_loaded, 16)
                eng.dma_start(w_out, a["B.out"]).then_inc(out_loaded, 16)

            @block.gpsimd
            def _(eng):
                eng.memset(cneg, 0.0).then_inc(consts, 1)
                eng.wait_ge(consts, 1)
                eng.affine_select(out=cneg, in_=cneg, compare_op=ALU.is_ge, fill=CAUSAL, base=S - P,
                                  pattern=[[-1, S]], channel_multiplier=1).then_inc(consts, 1)
                eng.iota(rev, pattern=[[-1, EB]], base=EB, channel_multiplier=0,
                         allow_small_or_imprecise_dtypes=True).then_inc(consts, 1)
                with eng.Fori(0, B) as b:
                    for step in range(-1, STEPS):
                        t = 0 if step < 0 else tile_at(step)
                        if t is not None:
                            k_ready.wait(eng, b, t + 1)
                            if t >= 2:
                                s_made.wait(eng, b, (t - 1) * A.tile_units)
                            apart(eng, m)
                            for j in range(A.per_tile):
                                last = eng.tensor_scalar(kz[:, (t % 2) * A.per_tile + j, :], kT, headmask[:, j:j + 1],
                                                         None, ALU.mult)
                            last.then_inc(kz_ready.sem, 1)

            @block.tensor
            def _(eng):
                eng.wait_ge(s["wb_loaded"], 48)
                eng.wait_ge(val_loaded, 64)

                def project(b, t):
                    for kc in range(KC):
                        last = eng.matmul(MB[0][:, :], wq[:, kc, t * P:(t + 1) * P], xnT[:, kc, :],
                                          start=(kc == 0), stop=(kc == KC - 1))
                    last.then_inc(qk_made.sem, 1)
                    for kc in range(KC):
                        last = eng.matmul(MB[1][:, :], wk[:, kc, t * P:(t + 1) * P], xnT[:, kc, :],
                                          start=(kc == 0), stop=(kc == KC - 1))
                    last.then_inc(qk_made.sem, 1)

                with eng.Fori(0, B) as b:
                    staged.wait(eng, b, 1)
                    for c in range(KC):
                        for t in range(QT):
                            last = eng.transpose(MB[c][:, t * P:(t + 1) * P], xstage[:, t, c * P:(c + 1) * P], ident[:, :])
                        last.then_inc(xt_made.sem, 1)
                    xt_ready.wait(eng, b, KC)
                    for t in range(QT):
                        for kc in range(KC):
                            last = eng.matmul(OB[0][:, t * 64:(t + 1) * 64], xnT[:, kc, t * P:(t + 1) * P],
                                              wgate[:, kc, :], start=(kc == 0), stop=(kc == KC - 1))
                    last.then_inc(gate_made.sem, 1)
                    project(b, 0)
                    for n in range(VU):
                        t, h = divmod(n, HB)
                        if n >= 2:
                            val_scaled.wait(eng, b, n - 1)
                        for kc in range(KC):
                            last = eng.matmul(SB[n % 2][:, :], xnT[:, kc, t * P:(t + 1) * P],
                                              w_val[:, kc, h * EB * DK:(h + 1) * EB * DK],
                                              start=(kc == 0), stop=(kc == KC - 1))
                        last.then_inc(val_made.sem, 1)
                    for step in range(STEPS):
                        t = tile_at(step)
                        if t is not None:
                            k_ready.wait(eng, b, t)
                            if groups_before(step):
                                otok_ready.wait(eng, b, groups_before(step))
                            project(b, t)
                        if step < U:
                            g, qt, j, h = A.unit(step)
                            tl, hj = divmod(h, A.per_tile)
                            L = P * A.keys(qt)
                            if A.first_of_tile(step):
                                kz_ready.wait(eng, b, tl + 1)
                                q_ready.wait(eng, b, tl + 1)
                            if step >= 2:
                                low_ready.wait(eng, b, step - 1)
                            else:
                                val_scaled.wait(eng, b, VU)
                            eng.matmul(SB[step % 2][:, 0:L], qT[:, tl % 2, qt * P:(qt + 1) * P],
                                       kz[:, (tl % 2) * A.per_tile + hj, 0:L], start=True, stop=True
                                       ).then_inc(s_made.sem, 1)
                        u = step - 2
                        if 0 <= u < U:
                            qt = A.unit(u)[1]
                            p_ready.wait(eng, b, u + 1)
                            if u >= 2:
                                (pt_even if u % 2 == 0 else pt_odd).wait(eng, b, u // 2)
                            for kt in range(A.keys(qt)):
                                last = eng.transpose(TB[u % 2][:, kt * P:(kt + 1) * P],
                                                     prob[:, u % NS, kt * P:(kt + 1) * P], ident[:, :])
                            last.then_inc(t_made.sem, 1)
                        u = step - 4
                        if closes_pass(u):
                            g, qt, _, _ = A.unit(u)
                            pt_even.wait(eng, b, (u + 1) // 2)
                            pt_odd.wait(eng, b, (u + 1) // 2)
                            if u < A.group:
                                v_ready.wait(eng, b, VU)
                            if qt == 0 and g >= 2:
                                ot_ready.wait(eng, b, g - 1)
                            for kt in range(A.keys(qt)):
                                for j in range(A.group):
                                    h = g * A.group + j
                                    r = A.strip * j
                                    last = eng.matmul(OB[g % 2][r:r + DK, qt * P:(qt + 1) * P],
                                                      vtok[:, kt, h * DK:(h + 1) * DK],
                                                      pT[:, (u - A.group + 1 + j) % PTR, kt * P:(kt + 1) * P],
                                                      start=(kt == 0), stop=(kt == A.keys(qt) - 1))
                            last.then_inc(av_done.sem, 1)
                        u = step - 7
                        if closes_group(u):
                            g = u // GS
                            ot_ready.wait(eng, b, g + 1)
                            k_ready.wait(eng, b, tiles_until(step))
                            if g >= 1:
                                otok_ready.wait(eng, b, g)
                            for qt in range(QT):
                                last = eng.transpose(MB[1][:, qt * P:(qt + 1) * P], oT[:, qt * P:(qt + 1) * P], ident[:, :])
                            last.then_inc(heads_made.sem, 1)
                    otok_ready.wait(eng, b, A.groups)
                    eng.wait_ge(out_loaded, 16)
                    for n in range(VU + 2):
                        if n < VU:
                            sp_ready.wait(eng, b, n + 1)
                            if n >= 2:
                                spt_ready.wait(eng, b, n - 1)
                            for c in range(4):
                                last = eng.transpose(TB[n % 2][:, c * P:(c + 1) * P],
                                                     spread[:, n % NG, c * P:(c + 1) * P], ident[:, :])
                            last.then_inc(spt_made.sem, 1)
                        w = n - 2
                        if w >= 0:
                            qt, h = divmod(w, HB)
                            spt_ready.wait(eng, b, w + 1)
                            if qt >= 2 and h == 0:
                                turn_done.wait(eng, b, qt - 1)
                            for c in range(4):
                                last = eng.matmul(OB[qt % 2][:, 0:D], spreadT[:, w % NG, c * P:(c + 1) * P],
                                                  w_out[:, h * 4 + c, :], start=(h == 0 and c == 0),
                                                  stop=(h == HB - 1 and c == 3))
                            last.then_inc(sp_used.sem, 1)

            @block.scalar
            def _(eng):
                ln_act(eng)
                eng.wait_ge(xn_done, xn_count)
                with eng.Fori(0, B) as b:
                    turn_done.wait(eng, b, 0)
                    eng.activation(xstage, xn[:, bass.ts(b, QT), :], ACT.Copy).then_inc(staged.sem, 1)
                    gate_made.wait(eng, b, 1)
                    eng.activation(gates, OB[0][:, 0:QT * 64].rearrange("p (a e) -> p a e", e=EB), ACT.Sigmoid
                                   ).then_inc(gate_ready.sem, 1)
                    for step in range(STEPS):
                        if step < U:
                            L = P * A.keys(A.unit(step)[1])
                            low_ready.wait(eng, b, step + 1)
                            if step >= NS:
                                t_made.wait(eng, b, step - NS + 1)
                            eng.activation(prob[:, step % NS, 0:L], sneg[:, step % NS, 0:L], ACT.Exp,
                                           bias=low[:, step:step + 1], scale=-1.0,
                                           accum_out=rowsum[:, step:step + 1]).then_inc(p_ready.sem, 1)
                        u = step - 2
                        if 0 <= u < U and u % 2 == 1:
                            L = P * A.keys(A.unit(u)[1])
                            t_made.wait(eng, b, u + 1)
                            if u >= PTR:
                                av_done.wait(eng, b, u // A.group - 1)
                            eng.activation(pT[:, u % PTR, 0:L], TB[u % 2][:, 0:L], ACT.Copy).then_inc(pt_odd.sem, 1)
                        u = step - 5
                        if closes_group(u):
                            g = u // GS
                            av_done.wait(eng, b, (g + 1) * QT)
                            if g >= 1:
                                heads_made.wait(eng, b, g)
                            eng.activation(oT, OB[g % 2][:, :], ACT.Copy).then_inc(ot_ready.sem, 1)
                    for n in range(VU):
                        spt_made.wait(eng, b, n + 1)
                        if n >= NG:
                            sp_used.wait(eng, b, n - NG + 1)
                        eng.activation(spreadT[:, n % NG, :], TB[n % 2][:, :], ACT.Copy).then_inc(spt_ready.sem, 1)

            @block.vector
            def _(eng):
                eng.wait_ge(consts, 3)
                ln_dve(eng)

                def take_qk(b, t):
                    qk_made.wait(eng, b, 2 * t + 1)
                    if t >= 2:
                        s_made.wait(eng, b, (t - 1) * A.tile_units)
                    eng.tensor_scalar(qT[:, t % 2, :], MB[0][:, :], -(DK ** -0.5), None, ALU.mult).then_inc(q_ready.sem, 1)
                    qk_made.wait(eng, b, 2 * t + 2)
                    if t >= 1:
                        kz_ready.wait(eng, b, t)
                    eng.tensor_copy(kT, MB[1][:, :]).then_inc(k_ready.sem, 1)

                with eng.Fori(0, B) as b:
                    for c in range(KC):
                        xt_made.wait(eng, b, c + 1)
                        eng.tensor_copy(xnT[:, c, :], MB[c][:, :]).then_inc(xt_ready.sem, 1)
                    take_qk(b, 0)
                    wide_best = best.unsqueeze(2).to_broadcast([P, VU, EB])
                    wide_rev = rev.unsqueeze(1).to_broadcast([P, VU, EB])
                    gate_ready.wait(eng, b, 1)
                    eng.tensor_reduce(best, gates, AX.X, ALU.max).then_inc(pick.sem, 1)
                    pick.wait(eng, b, 1)
                    eng.tensor_tensor(hit, gates, wide_best, ALU.is_equal).then_inc(pick.sem, 1)
                    pick.wait(eng, b, 2)
                    eng.tensor_tensor(gm, hit, wide_rev, ALU.mult).then_inc(pick.sem, 1)
                    pick.wait(eng, b, 3)
                    eng.tensor_reduce(best, gm, AX.X, ALU.max).then_inc(pick.sem, 1)
                    pick.wait(eng, b, 4)
                    eng.tensor_tensor(hit, gm, wide_best, ALU.is_equal).then_inc(pick.sem, 1)
                    pick.wait(eng, b, 5)
                    eng.tensor_tensor(gm, hit, gates, ALU.mult).then_inc(pick.sem, 1)
                    pick.wait(eng, b, 6)
                    for n in range(VU + 1):
                        if n < VU:
                            val_made.wait(eng, b, n + 1)
                            if n >= NG:
                                v_ready.wait(eng, b, n - NG + 1)
                            eng.tensor_tensor(scaled[:, n % NG, :].rearrange("p (e k) -> p e k", e=EB),
                                              SB[n % 2][:, :].rearrange("p (e k) -> p e k", e=EB),
                                              gm[:, n, :].unsqueeze(2).to_broadcast([P, EB, DK]), ALU.mult
                                              ).then_inc(val_scaled.sem, 1)
                        w = n - 1
                        if w >= 0:
                            t, h = divmod(w, HB)
                            val_scaled.wait(eng, b, w + 1)
                            eng.tensor_reduce(vtok[:, t, h * DK:(h + 1) * DK],
                                              scaled[:, w % NG, :].rearrange("p (e k) -> p k e", e=EB), AX.X, ALU.add
                                              ).then_inc(v_ready.sem, 1)
                    for step in range(STEPS):
                        t = tile_at(step)
                        if t is not None:
                            take_qk(b, t)
                        if step < U:
                            g, qt, j, h = A.unit(step)
                            L = P * A.keys(qt)
                            s_made.wait(eng, b, step + 1)
                            if step >= NS:
                                p_ready.wait(eng, b, step - NS + 1)
                            apart(eng, m)
                            eng.tensor_tensor_reduce(sneg[:, step % NS, 0:L], SB[step % 2][:, 0:L], cneg[:, S - L:S],
                                                     1.0, 3.0e38, ALU.add, ALU.min, low[:, step:step + 1]
                                                     ).then_inc(low_ready.sem, 1)
                        u = step - 2
                        if 0 <= u < U and u % 2 == 0:
                            L = P * A.keys(A.unit(u)[1])
                            t_made.wait(eng, b, u + 1)
                            if u >= PTR:
                                av_done.wait(eng, b, u // A.group - 1)
                            eng.tensor_copy(pT[:, u % PTR, 0:L], TB[u % 2][:, 0:L]).then_inc(pt_even.sem, 1)
                        u = step - 4
                        if closes_group(u):
                            g = u // GS
                            p_ready.wait(eng, b, (g + 1) * GS)
                            eng.reciprocal(rinv[:, g * GS:(g + 1) * GS], rowsum[:, g * GS:(g + 1) * GS]
                                           ).then_inc(rinv_ready.sem, 1)
                            rinv_ready.wait(eng, b, g + 1)

                            def of_group(z):
                                return z.rearrange("p (t h) e -> p t h e", h=HB)[:, :, 2 * g:2 * g + 2, :]

                            eng.tensor_tensor(of_group(gmr), of_group(gm),
                                              rinv[:, g * GS:(g + 1) * GS].rearrange("p (t j) -> p t j", j=2)
                                              .unsqueeze(3).to_broadcast([P, QT, 2, EB]), ALU.mult
                                              ).then_inc(gmr_ready.sem, 1)
                        u = step - 7
                        if closes_group(u):
                            g = u // GS
                            heads_made.wait(eng, b, g + 1)
                            eng.tensor_copy(otok[:, :, g * P:(g + 1) * P],
                                            MB[1][:, :].rearrange("p (t c) -> p t c", t=QT)).then_inc(otok_ready.sem, 1)
                    gmr_ready.wait(eng, b, A.groups)
                    otok_ready.wait(eng, b, A.groups)
                    for n in range(VU + 3):
                        if n < VU:
                            qt, h = divmod(n, HB)
                            if n >= NG:
                                spt_made.wait(eng, b, n - NG + 1)
                            eng.tensor_tensor(spread[:, n % NG, :].rearrange("p (e k) -> p e k", e=EB),
                                              otok[:, qt, h * DK:(h + 1) * DK].unsqueeze(1).to_broadcast([P, EB, DK]),
                                              gmr[:, n, :].unsqueeze(2).to_broadcast([P, EB, DK]), ALU.mult
                                              ).then_inc(sp_ready.sem, 1)
                        w = n - 3
                        if w >= 0 and w % HB == HB - 1:
                            qt = w // HB
                            sp_used.wait(eng, b, w + 1)
                            xt = x[:, b * QT + qt, :]
                            eng.scalar_tensor_tensor(out=xt, in0=OB[qt % 2][:, 0:D], scalar=gate, in1=xt,
                                                     op0=ALU.mult, op1=ALU.add).then_inc(turn_done.sem, 1)


def product_key_experts(nc, a, m):
    s = m["s"]
    bank, ident, x = m["bank"], m["ident"], m["x"]
    HP, WP, UPP, XP, SP = bank[0:2], bank[2:5], bank[5], bank[6], bank[7]
    take, wide, wab = carve(m), carve(m, "wc"), carve(m, "wab")
    down = carve(m, "big1")(KC * ELO, EHI)
    up = carve(m, "big2")(ELO, D)
    hot = wide(8192).bitcast(BF16).rearrange("p (m t) -> p m t", t=P)
    wq, keysT = wab(2 * HD, D), wab(2 * HD, NK)
    simw = take(KC, 2 * HD * NK)
    xstage, xnT = take(D), take(KC, P)
    sims = take(2 * HD, NK)
    Hg = take(ELO, P)
    xn = Hg.rearrange("p (t a) b -> p t (a b)", a=D // P)
    G = carve(m, "wab")(ELO, P)
    scale, shift = take(B * QT), take(B * QT)
    elo = take(ELO * P // 2).bitcast(BF16).rearrange("p (j t) -> p j t", t=P)
    b12 = take(ELO * P // 2).bitcast(BF16).rearrange("p (j t) -> p j t", t=P)
    b3 = take(ELO * P // 2).bitcast(BF16).rearrange("p (j t) -> p j t", t=P)
    sel = take(4, P)
    selT = take(4 * P // 2).bitcast(BF16).rearrange("p (f t) -> p f t", t=P)
    top, topi = take(2 * HD, TOP), take(2 * HD, TOP).bitcast(U32)
    topf = take(2 * HD, TOP)
    pairs, eq = take(HD, TOP * TOP), take(HD * TOP, TOP)
    score, pk, pa, pb = take(HD, TOP), take(NSEL).bitcast(U32), take(NSEL).bitcast(U32), take(NSEL).bitcast(U32)
    paf, pbf, i1, i2, over = take(NSEL), take(NSEL), take(NSEL), take(NSEL), take(NSEL)
    part, rest = take(NSEL // 2).bitcast(BF16), take(NSEL)
    iota = take(TOP)
    NT, NJ = B * QT, 4
    gate = m["gates"][:, 3:4]
    TW = 16

    with ExitStack() as ctx:
        def sig(what, per):
            return Signal(nc, ctx, f"D_{what}", per)

        def sem(what):
            return ctx.enter_context(nc.semaphore("D_" + what))

        w_loaded, down_loaded, up_loaded = sem("w_loaded"), sem("down_loaded"), sem("up_loaded")
        fold_made, fold_ready, consts = sem("fold_made"), sem("fold_ready"), sem("consts")
        staged, xt_made, xt_ready = sig("staged", 1), sig("xn_transposed", 1), sig("xnT_ready", 1)
        sim_made, sim_ready = sig("sims_made", 2), sig("sims_ready", 2)
        STEPS = 52
        step = sig("pick_step", STEPS)
        selt_made, selt_ready = sig("sel_transposed", 1), sig("selT_ready", 1)
        h_made, h_ready = sig("hidden_made", ELO // NJ), sig("hidden_ready", ELO // NJ)
        hot_ready, b_ready = sig("hot_ready", 1), sig("elo_ready", 3)
        w_made, g_ready = sig("weights_made", P // TW), sig("weighted", P // TW)
        up_made, turn_done = sig("up_made", 1), sig("x_updated", 1)
        ln_act, ln_dve, xn_done, xn_count = layer_norm(nc, ctx, m, "D", 2, x, xn, take, (scale, shift))

        def turns(eng, turn):
            with eng.Fori(0, NT - 1) as i:
                turn(i, True)
            turn(NT - 1, False)

        with nc.Block() as block:
            @block.sync
            def _(eng):
                eng.wait_ge(s["wa_loaded"], 16 * 9)
                eng.wait_ge(s["wb_loaded"], 48)
                eng.dma_start(wq, a["L1_ffn_w_q"].rearrange("(n p) d -> p n d", p=P)).then_inc(w_loaded, 16)
                eng.dma_start(keysT, a["D.keysT"]).then_inc(w_loaded, 16)
                eng.dma_start(down, a["D.downT"]).then_inc(down_loaded, 16)
                eng.dma_start(up, a["D.up"]).then_inc(up_loaded, 16)

            @block.gpsimd
            def _(eng):
                eng.iota(iota, pattern=[[1, TOP]], base=0, channel_multiplier=0,
                         allow_small_or_imprecise_dtypes=True).then_inc(consts, 1)
                eng.memset(sel, 0.0).then_inc(consts, 1)

            @block.tensor
            def _(eng):
                eng.wait_ge(w_loaded, 32)
                for n in range(4):
                    kc, c = divmod(n, 2)
                    for q in range(HD):
                        hc = c * HD + q
                        last = eng.matmul(bank[n][:, q * NK:(q + 1) * NK], wq[:, hc, kc * P:(kc + 1) * P],
                                          keysT[:, hc, :], start=True, stop=True)
                    last.then_inc(fold_made, 1)

                def select(i):
                    staged.wait(eng, i, 1)
                    for c in range(KC):
                        last = eng.transpose(XP[:, c * P:(c + 1) * P], xstage[:, c * P:(c + 1) * P], ident[:, :])
                    last.then_inc(xt_made.sem, 1)
                    xt_ready.wait(eng, i, 1)
                    for n in range(2):
                        for kc in range(KC):
                            last = eng.matmul(HP[n][:, :], xnT[:, kc, :], simw[:, kc, n * 512:(n + 1) * 512],
                                              start=(kc == 0), stop=(kc == KC - 1))
                        last.then_inc(sim_made.sem, 1)

                def turn_picks(i):
                    step.wait(eng, i, STEPS)
                    for f in range(4):
                        last = eng.transpose(SP[:, f * P:(f + 1) * P], sel[:, f, :], ident[:, :])
                    last.then_inc(selt_made.sem, 1)

                eng.wait_ge(fold_ready, 4)
                select(0)
                turn_picks(0)
                eng.wait_ge(down_loaded, 16)
                eng.wait_ge(up_loaded, 16)

                def turn(i, more):
                    for n in range(ELO // NJ):
                        if n >= 2:
                            h_ready.wait(eng, i, n - 1)
                        else:
                            sim_ready.wait(eng, i, 2)
                        for q in range(NJ):
                            for kc in range(KC):
                                last = eng.matmul(HP[n % 2][:, q * P:(q + 1) * P], down[:, kc * ELO + n * NJ + q, :],
                                                  xnT[:, kc, :], start=(kc == 0), stop=(kc == KC - 1))
                        last.then_inc(h_made.sem, 1)
                    if more:
                        h_ready.wait(eng, i, ELO // NJ)
                        select(i + 1)
                    hot_ready.wait(eng, i, 1)
                    b_ready.wait(eng, i, 3)
                    for n in range(P // TW):
                        if n >= 3:
                            g_ready.wait(eng, i, n - 2)
                        for q in range(TW):
                            t = n * TW + q
                            dst = WP[n % 3][:, q * ELO:(q + 1) * ELO]
                            eng.matmul(dst, hot[:, :, t], b12[:, :, t], start=True, stop=False)
                            last = eng.matmul(dst, hot[:, :, t], b3[:, :, t], start=False, stop=True)
                        last.then_inc(w_made.sem, 1)
                    g_ready.wait(eng, i, P // TW)
                    turn_done.wait(eng, i, 0)
                    for j in range(ELO):
                        last = eng.matmul(UPP[:, 0:D], G[:, j, :], up[:, j, :], start=(j == 0), stop=(j == ELO - 1))
                    last.then_inc(up_made.sem, 1)
                    if more:
                        turn_picks(i + 1)

                turns(eng, turn)

            @block.scalar
            def _(eng):
                ln_act(eng)
                for n in range(4):
                    kc, c = divmod(n, 2)
                    eng.wait_ge(fold_made, n + 1)
                    eng.activation(simw[:, kc, c * 512:(c + 1) * 512], bank[n][:, :], ACT.Copy).then_inc(fold_ready, 1)
                eng.wait_ge(xn_done, xn_count)

                def stage(i):
                    xt_made.wait(eng, i, 0)
                    eng.activation(xstage, x[:, i, :], ACT.Identity, scale=scale[:, bass.ds(i, 1)],
                                   bias=shift[:, bass.ds(i, 1)]).then_inc(staged.sem, 1)

                def select(i):
                    xt_made.wait(eng, i, 1)
                    for c in range(KC):
                        last = eng.activation(xnT[:, c, :], XP[:, c * P:(c + 1) * P], ACT.Copy,
                                              scale=m["cols"][:, 8 + c:9 + c])
                    last.then_inc(xt_ready.sem, 1)
                    for n in range(2):
                        sim_made.wait(eng, i, n + 1)
                        if n == 0:
                            step.wait(eng, i, 0)
                        eng.activation(sims[:, n * HD:(n + 1) * HD, :],
                                       HP[n][:, :].rearrange("p (a b) -> p a b", b=NK), ACT.Copy).then_inc(sim_ready.sem, 1)

                def picks(i):
                    selt_made.wait(eng, i, 1)
                    b_ready.wait(eng, i, 0)
                    eng.activation(selT, SP[:, :].rearrange("p (f t) -> p f t", t=P), ACT.Copy).then_inc(selt_ready.sem, 1)

                stage(0)
                select(0)
                picks(0)

                def turn(i, more):
                    if more:
                        stage(i + 1)
                    g_ready.wait(eng, i, 0)
                    for n in range(ELO // NJ):
                        h_made.wait(eng, i, n + 1)
                        eng.activation(Hg[:, n * NJ:(n + 1) * NJ, :], HP[n % 2][:, :].rearrange("p (j t) -> p j t", t=P),
                                       ACT.Gelu).then_inc(h_ready.sem, 1)
                    if more:
                        select(i + 1)
                        picks(i + 1)

                turns(eng, turn)

            @block.vector
            def _(eng):
                eng.wait_ge(consts, 2)
                ln_dve(eng)

                def topk(i):
                    n = [0]

                    def mark(ins):
                        ins.then_inc(step.sem, 1)
                        n[0] += 1

                    def reach():
                        step.wait(eng, i, n[0])

                    sim_ready.wait(eng, i, 2)
                    apart(eng, m)
                    for hc in range(2 * HD):
                        mark(eng.max(top[:, hc, :], sims[:, hc, :]))
                    reach()
                    apart(eng, m)
                    for hc in range(2 * HD):
                        last = eng.max_index(topi[:, hc, :], top[:, hc, :], sims[:, hc, :])
                    mark(last)
                    halves = top.rearrange("p (h c) k -> p h c k", c=2)
                    mark(eng.tensor_tensor(pairs.rearrange("p h (a b) -> p h a b", b=TOP),
                                           halves[:, :, 0, :].unsqueeze(3).to_broadcast([P, HD, TOP, TOP]),
                                           halves[:, :, 1, :].unsqueeze(2).to_broadcast([P, HD, TOP, TOP]), ALU.add))
                    reach()
                    apart(eng, m)
                    for h in range(HD):
                        mark(eng.max(score[:, h, :], pairs[:, h, :]))
                    mark(eng.tensor_copy(topf, topi))
                    reach()
                    apart(eng, m)
                    for h in range(HD):
                        last = eng.max_index(pk[:, h * TOP:(h + 1) * TOP], score[:, h, :], pairs[:, h, :])
                    mark(last)
                    reach()
                    mark(eng.tensor_scalar(pa, pk, 3, None, ALU.logical_shift_right))
                    mark(eng.tensor_scalar(pb, pk, TOP - 1, None, ALU.bitwise_and))
                    reach()
                    mark(eng.tensor_copy(paf, pa))
                    mark(eng.tensor_copy(pbf, pb))
                    reach()
                    numbers = topf.rearrange("p (h c) k -> p h c k", c=2)
                    for c, place, key in ((0, paf, i1), (1, pbf, i2)):
                        mark(eng.tensor_tensor(eq, place.unsqueeze(2).to_broadcast([P, NSEL, TOP]),
                                               iota.unsqueeze(1).to_broadcast([P, NSEL, TOP]), ALU.is_equal))
                        reach()
                        e4 = eq.rearrange("p (h k) a -> p h k a", k=TOP)
                        mark(eng.tensor_tensor(e4, e4, numbers[:, :, c, :].unsqueeze(2).to_broadcast([P, HD, TOP, TOP]),
                                               ALU.mult))
                        reach()
                        mark(eng.tensor_reduce(key, eq, AX.X, ALU.add))
                        reach()
                    mark(eng.tensor_scalar(over, i2, float(ELO), None, ALU.is_ge))
                    reach()
                    selt_made.wait(eng, i, 0)
                    for d in range(2):
                        mark(eng.scalar_tensor_tensor(out=sel[:, 0, d * NSEL:(d + 1) * NSEL], in0=i1, scalar=2.0, in1=over,
                                                      op0=ALU.mult, op1=ALU.add))
                        mark(eng.scalar_tensor_tensor(out=sel[:, 1, d * NSEL:(d + 1) * NSEL], in0=over,
                                                      scalar=-float(ELO), in1=i2, op0=ALU.mult, op1=ALU.add))
                    flat = score.rearrange("p h k -> p (h k)")
                    mark(eng.tensor_scalar(rest, flat, 0.0, None, ALU.max))
                    reach()
                    for q in range(3):
                        dst = sel[:, 2, q * NSEL:(q + 1) * NSEL] if q < 2 else sel[:, 3, 0:NSEL]
                        mark(eng.tensor_copy(part, rest))
                        reach()
                        mark(eng.tensor_copy(dst, part))
                        if q < 2:
                            mark(eng.tensor_tensor(rest, rest, part, ALU.subtract))
                            reach()
                    assert n[0] == STEPS, n[0]

                topk(0)

                def turn(i, more):
                    selt_ready.wait(eng, i, 1)
                    for mm in range(EHI):
                        last = eng.tensor_scalar(hot[:, mm, :], selT[:, 0, :], float(mm), None, ALU.is_equal)
                    last.then_inc(hot_ready.sem, 1)
                    for j in range(ELO):
                        last = eng.tensor_scalar(elo[:, j, :], selT[:, 1, :], float(j), None, ALU.is_equal)
                    last.then_inc(b_ready.sem, 1)
                    b_ready.wait(eng, i, 1)
                    for f, dst in ((2, b12), (3, b3)):
                        eng.tensor_tensor(dst, elo, selT[:, f, :].unsqueeze(1).to_broadcast([P, ELO, P]), ALU.mult
                                          ).then_inc(b_ready.sem, 1)
                    h_ready.wait(eng, i, ELO // NJ)
                    for n in range(P // TW):
                        w_made.wait(eng, i, n + 1)
                        if n == 0:
                            up_made.wait(eng, i, 0)
                        eng.tensor_tensor(G[:, :, n * TW:(n + 1) * TW],
                                          WP[n % 3][:, :].rearrange("p (t j) -> p j t", j=ELO),
                                          Hg[:, :, n * TW:(n + 1) * TW], ALU.mult).then_inc(g_ready.sem, 1)
                    if more:
                        topk(i + 1)
                    up_made.wait(eng, i, 1)
                    xt = x[:, i, :]
                    eng.scalar_tensor_tensor(out=xt, in0=UPP[:, 0:D], scalar=gate, in1=xt, op0=ALU.mult, op1=ALU.add
                                             ).then_inc(turn_done.sem, 1)

                turns(eng, turn)


def layouts(i):
    c = np.ascontiguousarray
    r = {"x": c(i["x"]), "bias": c(i["fside_BxSxS2_0"]), "mask": c(i["mask_BxS2_ik0"])}
    r["ctxT"] = c(np.transpose(i["ctx_1024"], (2, 0, 1)).reshape(D, B * S))
    for n, k in (("A.wqT", "WQ"), ("A.wkT", "WK"), ("A.wvT", "WV"), ("A.woT", "WO")):
        r[n] = c(i[f"L0_xattn_{k}_w"].T)
    r["B.val"] = c(i["L0_ffn_value_experts"].transpose(2, 1, 0, 3).reshape(D, -1))
    r["B.out"] = c(i["L0_ffn_output_experts"].reshape(4, 2, HB, 64, D).transpose(1, 3, 2, 0, 4).reshape(P, 32, D))
    r["D.keysT"] = c(i["L1_ffn_keys"].transpose(3, 0, 2, 1).reshape(P, 2 * HD, NK))
    r["D.downT"] = c(i["L1_ffn_expert_down"].reshape(EHI, ELO, KC, P).transpose(3, 2, 1, 0).reshape(P, KC * ELO, EHI))
    r["D.up"] = c(i["L1_ffn_expert_up"].reshape(EHI, ELO, D))
    r["C.wk"] = c(i["L1_xattn_w_kv"][:, :1024])
    r["C.wv"] = c(i["L1_xattn_w_kv"][:, 1024:])
    r["mask.cols"] = c(i["mask_BxS2_ik0"].reshape(B, QT, P).transpose(0, 2, 1))
    for k in ("L0_xattn_WQ_b", "L0_xattn_WK_b", "L1_xattn_ln_gamma", "L1_xattn_ln_beta", "L1_ffn_norm_w"):
        r[k + ".cols"] = c(i[k].reshape(KC, P).T)
    for k in ("L0_ffn_w_gate", "L0_ffn_w_q", "L0_ffn_w_k", "L1_ffn_w_q", "g_xattn", "g_ffn", "L1_xattn_gate", "L0_xattn_WV_b", "L0_xattn_WO_b", "L1_xattn_b_out", "L1_xattn_w_q",
              "L1_xattn_w_out"):
        r[k] = c(i[k])
    return r


def kernel(**inputs):
    import concourse.bacc as bacc
    from concourse.bass_utils import run_bass_kernel_spmd

    arrays = layouts({name: np.asarray(value) for name, value in inputs.items()})
    nc = bacc.Bacc("TRN2", target_bir_lowering=False, num_devices=1)
    names = {key: "in_" + key.replace(".", "_") for key in arrays}
    views = {key: nc.dram_tensor(names[key], value.shape, mybir.dt.from_np(value.dtype), kind="ExternalInput").ap()
             for key, value in arrays.items()}
    out = nc.dram_tensor("out_0", (B, S, D), F32, kind="ExternalOutput").ap()
    build(nc, views, out)
    result = run_bass_kernel_spmd(nc, [{names[key]: value for key, value in arrays.items()}], core_ids=[0])
    return result.results[0]["out_0"]
```

```python
from contextlib import ExitStack

import numpy as np

import concourse.bass as bass
from concourse import mybir

F32 = mybir.dt.float32
BF16 = mybir.dt.bfloat16
I32 = mybir.dt.int32
U32 = mybir.dt.uint32
ALU = mybir.AluOpType
ACT = mybir.ActivationFunctionType
AX = mybir.AxisListType

P = 128
B, S, D = 4, 512, 256
QT = S // P
KC = D // P
EPS = 1e-5
MASKED = 1e9
CAUSAL = 3.0e38


class Signal:

    def __init__(self, nc, ctx, name, per):
        self.sem = ctx.enter_context(nc.semaphore(name))
        self.per = per

    def wait(self, eng, turn, n):
        if isinstance(turn, int) and turn * self.per + n <= 0:
            return
        eng.wait_ge(self.sem, turn * self.per + n)


TICKS = 16


def apart(eng, m):
    m["ticks"] += 1
    n = m["ticks"] % TICKS
    if eng is m["pool"]:
        eng.tensor_tensor(m["tick"][:, n:n + 1], m["cst"][:, 0:1], m["cst"][:, 1:2], ALU.mult)
    else:
        eng.memset(m["tick"][:, TICKS + n:TICKS + n + 1], 0.0)


class Attention:

    def __init__(self, heads, dk, group, causal=False):
        self.heads, self.dk, self.group, self.causal = heads, dk, group, causal
        self.width = heads * dk
        self.per_tile = P // dk
        self.tiles = heads // self.per_tile
        self.groups = heads // group
        self.strip = P // group
        self.units = heads * QT
        self.tile_units = self.per_tile * QT
        self.group_units = group * QT

    def unit(self, u):
        g, r = divmod(u, self.group_units)
        qt, j = divmod(r, self.group)
        return g, qt, j, g * self.group + j

    def keys(self, qt):
        return qt + 1 if self.causal else QT

    def first_of_tile(self, s):
        return s % self.tile_units == 0 and 0 <= s < self.units


A_ = Attention(16, 16, 4)
B_ = Attention(8, 64, 2, causal=True)
C_ = Attention(16, 64, 2)

EB, HB = 8, 8
HD, NK, TOP = 8, 64, 8
NSEL = HD * TOP
EHI, ELO = 128, 32


def build(nc, a, out, phases="ABCD"):
    with ExitStack() as ctx:
        def sb(name, shape, dt=F32):
            return ctx.enter_context(nc.sbuf_tensor(name, shape, dt))

        def sem(name):
            return ctx.enter_context(nc.semaphore(name))

        bank = [ctx.enter_context(nc.psum_tensor(f"bank{i}", [P, 512], F32)) for i in range(8)]
        m = {}
        m["bank"] = bank
        m["x"] = sb("x", [P, B * QT, D])
        m["ident"] = sb("ident", [P, P])
        m["cst"] = sb("cst", [P, 64])
        m["gates"] = sb("gates", [P, 8])
        m["cols"] = sb("cols", [P, 32])
        m["tick"], m["ticks"] = sb("tick", [P, 2 * TICKS]), 0
        m["pool"] = nc.gpsimd
        m["big1"] = sb("big1", [P, 8192])
        m["big2"] = sb("big2", [P, 8192])
        m["wab"] = sb("wab", [P, 5248])
        m["wc"] = sb("wc", [P, 8192])
        m["work"] = sb("work", [P, 18800])
        s = {n: sem(n) for n in ("x_loaded", "identity_made", "wa_loaded", "wb_loaded",
                                 "wc_loaded", "x_first_loaded", "scalars_loaded", "scalars_ready")}
        m["s"] = s
        prologue(nc, a, m)
        if "A" in phases:
            cross_attention(nc, a, m, A_, "A")
        if "B" in phases:
            moe_attention(nc, a, m)
        if "C" in phases:
            cross_attention(nc, a, m, C_, "C")
        if "D" in phases:
            product_key_experts(nc, a, m)
        epilogue(nc, out, m)


def carve(m, key="work"):
    at = [0]
    region = m[key]

    def take(*shape):
        n = int(np.prod(shape))
        v = region[:, at[0]:at[0] + n]
        at[0] += n
        if len(shape) == 2:
            v = v.rearrange("p (a b) -> p a b", b=shape[1])
        elif len(shape) == 3:
            v = v.rearrange("p (a b c) -> p a b c", b=shape[1], c=shape[2])
        return v
    return take


def weight_views(m):
    ta = carve(m, "wab")
    v = {}
    v["A.wq"], v["A.wk"], v["A.wv"] = ta(KC, 256), ta(KC, 256), ta(KC, 256)
    v["A.wo"] = ta(4, 256)
    v["A.bv"], v["A.bo"] = ta(256), ta(256)
    v["B.gate"], v["B.wq"], v["B.wk"] = ta(KC, HB * EB), ta(KC, 512), ta(KC, 512)
    tc = carve(m, "wc")
    v["C.wq"], v["C.wk"], v["C.wv"] = tc(KC, 1024), tc(KC, 1024), tc(KC, 1024)
    v["C.wo"] = tc(8, 256)
    return v


def prologue(nc, a, m):
    s, v = m["s"], weight_views(m)
    with nc.Block() as block:
        @block.sync
        def _(eng):
            tokens = a["x"].rearrange("b (t p) d -> p (b t) d", p=P)
            eng.dma_start(m["x"][:, 0:QT, :], tokens[:, 0:QT, :]).then_inc(s["x_first_loaded"], 16)
            for n, name in enumerate(("g_xattn", "g_ffn")):
                eng.dma_start(m["gates"][:, 2 * n:2 * n + 2],
                              a[name].rearrange("(a n) -> a n", a=1).to_broadcast([P, 2])
                              ).then_inc(s["scalars_loaded"], 16)
            eng.dma_start(m["gates"][:, 4:5], a["L1_xattn_gate"].rearrange("(a n) -> a n", a=1).to_broadcast([P, 1])
                          ).then_inc(s["scalars_loaded"], 16)
            for n, name in enumerate(("L0_xattn_WQ_b", "L0_xattn_WK_b", "L1_xattn_ln_gamma", "L1_xattn_ln_beta",
                                      "L1_ffn_norm_w")):
                eng.dma_start(m["cols"][:, 2 * n:2 * n + 2], a[name + ".cols"]).then_inc(s["scalars_loaded"], 16)
            for name, key in (("A.wq", "A.wqT"), ("A.wk", "A.wkT"), ("A.wv", "A.wvT")):
                eng.dma_start(v[name], a[key].rearrange("(c p) n -> p c n", p=P)).then_inc(s["wa_loaded"], 16)
            for name, key in (("A.bv", "L0_xattn_WV_b"), ("A.bo", "L0_xattn_WO_b")):
                eng.dma_start(v[name], a[key].rearrange("(a n) -> a n", a=1).to_broadcast([P, 256])
                              ).then_inc(s["wa_loaded"], 16)
            for name, key in (("B.gate", "L0_ffn_w_gate"), ("B.wq", "L0_ffn_w_q"), ("B.wk", "L0_ffn_w_k")):
                eng.dma_start(v[name], a[key].rearrange("(c p) n -> p c n", p=P)).then_inc(s["wb_loaded"], 16)
            eng.dma_start(m["x"][:, QT:, :], tokens[:, QT:, :]).then_inc(s["x_loaded"], 16)
            eng.wait_ge(s["identity_made"], 4)
            for j in range(4):
                eng.dma_start(v["A.wo"][32 * j:32 * j + 16, :, :],
                              a["A.woT"].rearrange("(g j r) n -> j r g n", j=4, r=16)[j]).then_inc(s["wa_loaded"], 16)

        @block.gpsimd
        def _(eng):
            eng.memset(m["ident"][:, :], 0.0).then_inc(s["identity_made"], 1)
            eng.wait_ge(s["identity_made"], 1)
            eng.affine_select(out=m["ident"][:, :], in_=m["ident"][:, :], compare_op=ALU.not_equal, fill=1.0,
                              base=0, pattern=[[-1, P]], channel_multiplier=1).then_inc(s["identity_made"], 1)
            eng.memset(m["cst"][:, :], 1.0).then_inc(s["identity_made"], 1)
            eng.memset(v["A.wo"], 0.0).then_inc(s["identity_made"], 1)
            eng.wait_ge(s["identity_made"], 4)
            n = 4
            for at, count, rows in ((0, 8, 16), (8, 2, 64)):
                part = m["cst"][:, at:at + count]
                eng.affine_select(out=part, in_=part, compare_op=ALU.is_ge, fill=0.0, base=0,
                                  pattern=[[-rows, count]], channel_multiplier=1).then_inc(s["identity_made"], 1)
                n += 1
                eng.wait_ge(s["identity_made"], n)
                eng.affine_select(out=part, in_=part, compare_op=ALU.is_ge, fill=0.0, base=rows - 1,
                                  pattern=[[rows, count]], channel_multiplier=-1).then_inc(s["identity_made"], 1)
                n += 1

        @block.scalar
        def _(eng):
            eng.wait_ge(s["scalars_loaded"], 8 * 16)
            eng.activation(m["gates"][:, 0:5], m["gates"][:, 0:5], ACT.Tanh).then_inc(s["scalars_ready"], 1)

        @block.vector
        def _(eng):
            eng.wait_ge(s["scalars_ready"], 1)
            eng.tensor_tensor(m["gates"][:, 5:6], m["gates"][:, 1:2], m["gates"][:, 4:5], ALU.mult
                              ).then_inc(s["scalars_ready"], 1)


def epilogue(nc, out, m):
    with ExitStack() as ctx:
        stored = ctx.enter_context(nc.semaphore("stored"))
        with nc.Block() as block:
            @block.sync
            def _(eng):
                eng.dma_start(out.rearrange("b (t p) d -> p (b t) d", p=P), m["x"][:, :, :]).then_inc(stored, 16)
                eng.wait_ge(stored, 16)


def layer_norm(nc, ctx, m, name, rounds, source, xn, scratch, affine=None):
    NT = B * QT
    stats, mv = scratch(NT, 6), scratch(NT, 2)
    std, rstd, t1, t2 = scratch(NT), scratch(NT), scratch(NT), scratch(NT)
    var_ready = ctx.enter_context(nc.semaphore(name + "_var_ready"))
    std_ready = ctx.enter_context(nc.semaphore(name + "_std_ready"))
    step = ctx.enter_context(nc.semaphore(name + "_stat_step"))
    done = ctx.enter_context(nc.semaphore(name + "_xn_ready"))

    def on_scalar(eng):
        for r in range(rounds):
            eng.wait_ge(var_ready, r + 1)
            eng.activation(std, mv[:, :, 1], ACT.Sqrt).then_inc(std_ready, 1)

    def on_vector(eng):
        n = 0
        for r in range(rounds):
            kind = "rms" if name[0] == "D" and r == rounds - 1 else "ln"
            src = source if r == 0 else xn
            if r:
                eng.wait_ge(done, NT * r)
            for t in range(NT):
                eng.bn_stats(stats[:, t, :], src[:, t, :]).then_inc(step, 1)
            n += NT
            for t in range(NT):
                eng.wait_ge(step, n - NT + t + 1)
                eng.bn_aggr(mv[:, t, :], stats[:, t, :]).then_inc(step, 1)
            n += NT
            eng.wait_ge(step, n)
            if kind == "rms":
                eng.tensor_tensor(t1, mv[:, :, 0], mv[:, :, 0], ALU.mult).then_inc(step, 1)
                eng.wait_ge(step, n + 1)
                eng.tensor_tensor(mv[:, :, 1], mv[:, :, 1], t1, ALU.add).then_inc(step, 1)
                n += 2
                eng.wait_ge(step, n)
            eng.tensor_scalar(mv[:, :, 1], mv[:, :, 1], 1e-6 if kind == "rms" else EPS, None, ALU.add
                              ).then_inc(var_ready, 1)
            eng.wait_ge(std_ready, r + 1)
            eng.reciprocal(rstd, std).then_inc(step, 1)
            eng.wait_ge(step, n + 1)
            eng.tensor_tensor(t1, rstd, rstd, ALU.mult).then_inc(step, 1)
            eng.wait_ge(step, n + 2)
            eng.tensor_tensor(t2, t1, mv[:, :, 1], ALU.mult).then_inc(step, 1)
            eng.wait_ge(step, n + 3)
            eng.tensor_scalar(t1, t2, -0.5, 1.5, ALU.mult, ALU.add).then_inc(step, 1)
            eng.wait_ge(step, n + 4)
            eng.tensor_tensor(rstd, rstd, t1, ALU.mult).then_inc(step, 1)
            n += 5
            eng.wait_ge(step, n)
            if affine:
                scale, shift = affine
                if r == 0:
                    eng.tensor_copy(scale, rstd).then_inc(step, 1)
                    eng.tensor_scalar(shift, mv[:, :, 0], -1.0, None, ALU.mult).then_inc(step, 1)
                    n += 2
                    eng.wait_ge(step, n)
                else:
                    eng.tensor_tensor(scale, scale, rstd, ALU.mult).then_inc(step, 1)
                    eng.wait_ge(step, n + 1)
                    eng.tensor_tensor(shift, shift, scale, ALU.mult).then_inc(done, 1)
                    n += 1
                    continue
            for t in range(NT):
                eng.tensor_scalar(xn[:, t, :], src[:, t, :], mv[:, t, 0:1], rstd[:, t:t + 1],
                                  ALU.subtract, ALU.mult).then_inc(done, 1)
    return on_scalar, on_vector, done, NT * rounds if affine is None else NT * (rounds - 1) + 1


class Norm:
    PARTS = 6

    def __init__(self, nc, ctx, m, name, rounds, take, xstage, staged_used):
        self.m, self.rounds, self.x, self.xn = m, rounds, m["x"], xstage
        self.staged_used = staged_used
        self.parts = self.PARTS * len(rounds)
        self.stats, self.mv = take(QT, 6), take(QT, 2)
        self.std, self.rstd, self.t1, self.t2 = take(QT), take(QT), take(QT), take(QT)
        self.before = [2 * QT + (2 if kind == "rms" else 0) for kind in rounds]
        self.base = [sum(self.before[:r]) + 5 * r for r in range(len(rounds) + 1)]
        self.eps_added = Signal(nc, ctx, name + "_eps_added", len(rounds))
        self.root_ready = Signal(nc, ctx, name + "_root_ready", len(rounds))
        self.step = Signal(nc, ctx, name + "_stat_step", self.base[-1])
        self.done = Signal(nc, ctx, name + "_xn_ready", len(rounds) * QT)

    def wait(self, eng, b):
        self.done.wait(eng, b, self.done.per)

    def on_scalar(self, eng, b, part):
        r, k = divmod(part, self.PARTS)
        if k == 2:
            self.eps_added.wait(eng, b, r + 1)
            eng.activation(self.std, self.mv[:, :, 1], ACT.Sqrt).then_inc(self.root_ready.sem, 1)

    def on_vector(self, eng, b, part):
        r, k = divmod(part, self.PARTS)
        kind, base = self.rounds[r], self.base[r]
        mean, var = self.mv[:, :, 0], self.mv[:, :, 1]

        def source(t):
            return self.x[:, b * QT + t, :] if r == 0 else self.xn[:, t, :]

        if k < 2:
            for t in range(2 * k, 2 * k + 2):
                if r:
                    self.done.wait(eng, b, (r - 1) * QT + t + 1)
                eng.bn_stats(self.stats[:, t, :], source(t)).then_inc(self.step.sem, 1)
            self.step.wait(eng, b, base + 4 * k + 2)
            apart(eng, self.m)
            for t in range(2 * k, 2 * k + 2):
                eng.bn_aggr(self.mv[:, t, :], self.stats[:, t, :]).then_inc(self.step.sem, 1)
        if k == 2:
            self.step.wait(eng, b, base + 2 * QT)
            if kind == "rms":
                eng.tensor_tensor(self.t1, mean, mean, ALU.mult).then_inc(self.step.sem, 1)
                self.step.wait(eng, b, base + 2 * QT + 1)
                eng.tensor_tensor(var, var, self.t1, ALU.add).then_inc(self.step.sem, 1)
                self.step.wait(eng, b, base + 2 * QT + 2)
            eng.tensor_scalar(var, var, 1e-6 if kind == "rms" else EPS, None, ALU.add).then_inc(self.eps_added.sem, 1)
        if k == 3:
            n = base + self.before[r]
            self.root_ready.wait(eng, b, r + 1)
            eng.reciprocal(self.rstd, self.std).then_inc(self.step.sem, 1)
            self.step.wait(eng, b, n + 1)
            eng.tensor_tensor(self.t1, self.rstd, self.rstd, ALU.mult).then_inc(self.step.sem, 1)
            self.step.wait(eng, b, n + 2)
            eng.tensor_tensor(self.t2, self.t1, var, ALU.mult).then_inc(self.step.sem, 1)
            self.step.wait(eng, b, n + 3)
            eng.tensor_scalar(self.t1, self.t2, -0.5, 1.5, ALU.mult, ALU.add).then_inc(self.step.sem, 1)
            self.step.wait(eng, b, n + 4)
            eng.tensor_tensor(self.rstd, self.rstd, self.t1, ALU.mult).then_inc(self.step.sem, 1)
            self.step.wait(eng, b, n + 5)
            if r == 0:
                self.staged_used(eng, b)
        if k >= 4:
            for t in range(2 * k - 8, 2 * k - 6):
                if kind == "rms":
                    eng.tensor_scalar(self.xn[:, t, :], source(t), self.rstd[:, t:t + 1], None, ALU.mult
                                      ).then_inc(self.done.sem, 1)
                else:
                    eng.tensor_scalar(self.xn[:, t, :], source(t), mean[:, t:t + 1], self.rstd[:, t:t + 1],
                                      ALU.subtract, ALU.mult).then_inc(self.done.sem, 1)

    def all_parts(self, eng, b, on):
        for part in range(self.parts):
            on(eng, b, part)


def turns(eng, turn):
    turn(0, True)
    with eng.Fori(1, B - 1) as b:
        turn(b, True)
    turn(B - 1, False)


def cross_attention(nc, a, m, A, name):
    masked = name == "A"
    s, v = m["s"], weight_views(m)
    bank, ident, x = m["bank"], m["ident"], m["x"]
    SB, TB, OB, MB = bank[0:2], bank[2:4], bank[4:6], bank[6:8]
    wq, wk, wv, wo = (v[f"{name}.{w}"] for w in ("wq", "wk", "wv", "wo"))
    GS, U, T = A.group_units, A.units, A.tiles
    headmask = m["cst"][:, 0:8] if name == "A" else m["cst"][:, 8:10]
    gate = m["gates"][:, 0:1] if name == "A" else m["gates"][:, 5:6]
    take, big1, big2 = carve(m), carve(m, "big1"), carve(m, "big2")
    NS, PTR = 3, 2 * A.group
    ctxT = big2(KC, B * S)
    vtok = big1(QT, A.width)
    xstage = take(QT, D)
    xnT, ctxb = take(KC, S), take(KC, S)
    qT, kT = take(2, S), take(S)
    prob = take(NS, S)
    pT = take(PTR, QT * P)
    rbs = take(S)
    rmat = take(2 * GS, A.dk)
    low, rowsum, rinv = take(U), take(U), take(U)
    y = take(2, D)
    if masked:
        blocks = carve(m, "wc")(2, A.per_tile * S).bitcast(BF16)
        blocks = [[blocks[:, slot, w * A.per_tile * S:(w + 1) * A.per_tile * S].rearrange("p (h n) -> p h n", n=S)
                   for w in range(2)] for slot in range(2)]
        parts = big1(2, 3 * S // 2).bitcast(BF16).rearrange("p w (i n) -> p w i n", n=S)
        rest = take(2, S)
        scratch = nc.dram_tensor("parts", [2, 2, 3, P, S], BF16).ap()
        onorm, braw = big2(A.groups, S), big2(QT, S)
        sneg = take(NS, S)
        bneg, bnext = big1(QT, S), big1(QT, S)
        rows, rnext = take(2, S), big1(2, S)
        mm, bt = take(S), take(S)
        mraw, mcraw, mcol = take(S).bitcast(I32), take(QT).bitcast(I32), take(QT)
    else:
        kz, onorm, bo = take(2 * A.per_tile, S), take(A.groups, S), take(D)

    PAIRS = [(i, j) for i in range(3) for j in range(3)][:8]
    NBLOCKS = 2 * len(PAIRS)

    with ExitStack() as ctx:
        def sig(what, per):
            return Signal(nc, ctx, f"{name}_{what}", per)

        turn_done = sig("x_updated", QT)
        ctx_loaded = ctx.enter_context(nc.semaphore(f"{name}_ctx_loaded"))
        ctx_staged = sig("ctx_staged", 1)
        xt_made = sig("xn_transposed", KC)
        xt_ready = sig("xnT_ready", KC)
        v_made, v_ready = sig("v_made", QT * max(1, A.width // 512)), sig("v_ready", QT * max(1, A.width // 512))
        qk_made, q_ready, k_ready = sig("qk_made", 2 * T), sig("q_ready", T), sig("k_ready", T)
        if masked:
            bias_loaded, bias_step, bias_ready = sig("bias_loaded", 48), sig("bias_step", 5 + 4 * QT), sig("bias_ready", 2)
            cleared = ctx.enter_context(nc.semaphore(f"{name}_cleared"))
            split_step, parts_stored = sig("split_step", 10 * T), sig("parts_stored", 32 * T)
            blocks_loaded = [sig(f"blocks_loaded_{slot}", 16 * NBLOCKS) for slot in range(2)]
        else:
            kz_ready = sig("kz_ready", T)
            bo_loaded = ctx.enter_context(nc.semaphore(f"{name}_bo_loaded"))
        ctx_first = ctx.enter_context(nc.semaphore(f"{name}_ctx_first_loaded"))
        s_made, low_ready = sig("scores_made", U), sig("low_ready", U)
        p_ready = sig("probs_ready", U)
        t_made = sig("probs_transposed", U)
        pt_even, pt_odd = sig("pT_even_ready", U // 2), sig("pT_odd_ready", U // 2)
        av_done = sig("av_done", A.groups * QT)
        rinv_ready = sig("rinv_ready", A.groups)
        rmat_ready = sig("rmat_ready", A.groups)
        rb_made, rb_copied = sig("rb_made", A.groups), sig("rb_copied", A.groups)
        on_ready = sig("onorm_ready", A.groups)
        out_made, y_ready = sig("out_made", QT), sig("y_ready", QT)
        norm = Norm(nc, ctx, m, name, ("ln",) if masked else ("ln", "ln"), take, xstage,
                    lambda eng, b: xt_made.wait(eng, b - 1, KC))

        STEPS = U + 9
        STAGE, TURN = (8, 20) if masked else (U - 11, U - 8)
        VW = min(512, A.width)
        VCHUNKS = [(kt, c) for kt in range(QT) for c in range(A.width // VW)]

        def closes_pass(u):
            return 0 <= u < U and u % A.group == A.group - 1

        def closes_group(u):
            return 0 <= u < U and u % GS == GS - 1

        def tile_at(step):
            if masked:
                return {2: 1, A.tile_units + 2: T}.get(step)
            u = step + 5
            return u // A.tile_units if 5 < u <= U and u % A.tile_units == 0 else None

        def groups_before(step):
            return sum(closes_group(z - 7) for z in range(step))

        def tiles_until(step, more):
            return 1 + sum(tile_at(z) is not None and (more or tile_at(z) < T) for z in range(step + 1))

        def norm_parts(step):
            first = TURN - 5 - norm.parts
            return [step - first] if 0 <= step - first < norm.parts else []

        def each_tile(step, b, more, do):
            t = tile_at(step)
            if t is not None and t < T:
                do(b, t)
            elif t is not None and more:
                do(b + 1, 0)

        def spread_sums(eng, b, g):
            rinv_ready.wait(eng, b, g + 1)
            rb_made.wait(eng, b if g >= 2 else b - 1, g - 1 if g >= 2 else A.groups - 1 + g)
            if eng is m["pool"]:
                apart(eng, m)
            eng.tensor_copy(rmat[:, (g % 2) * GS:(g % 2 + 1) * GS, :],
                            rinv[:, g * GS:(g + 1) * GS].unsqueeze(2).to_broadcast([P, GS, A.dk])
                            ).then_inc(rmat_ready.sem, 1)

        def fold_bias(eng, b, t):
            n = 5 + 4 * t
            bias_step.wait(eng, b, n)
            if eng is m["pool"]:
                apart(eng, m)
            eng.tensor_scalar(mm, rnext[:, 0, :], mcol[:, t:t + 1], None, ALU.mult).then_inc(bias_step.sem, 1)
            bias_step.wait(eng, b, n + 1)
            eng.tensor_tensor(bt, braw[:, t, :], mm, ALU.mult).then_inc(bias_step.sem, 1)
            bias_step.wait(eng, b, n + 2)
            if eng is m["pool"]:
                apart(eng, m)
            eng.tensor_scalar(mm, mm, -MASKED, MASKED, ALU.mult, ALU.add).then_inc(bias_step.sem, 1)
            bias_step.wait(eng, b, n + 3)
            eng.tensor_tensor(bnext[:, t, :], mm, bt, ALU.subtract).then_inc(bias_step.sem, 1)

        with nc.Block() as block:
            @block.sync
            def _(eng):
                context = a["ctxT"].rearrange("(c p) n -> p c n", p=P)
                eng.dma_start(ctxT[:, :, 0:S], context[:, :, 0:S]).then_inc(ctx_first, 16)
                if name == "C":
                    for w, key in (("C.wq", "L1_xattn_w_q"), ("C.wk", "C.wk"), ("C.wv", "C.wv"), ("C.wo", "L1_xattn_w_out")):
                        eng.dma_start(v[w], a[key].rearrange("(c p) n -> p c n", p=P)).then_inc(s["wc_loaded"], 16)
                    eng.dma_start(bo, a["L1_xattn_b_out"].rearrange("(a n) -> a n", a=1).to_broadcast([P, D])
                                  ).then_inc(bo_loaded, 16)
                def load_bias(b):
                    bias_step.wait(eng, b - 1, 5 + 4 * QT)
                    eng.dma_start(mraw, a["mask"][b].rearrange("(a k) -> a k", a=1).to_broadcast([P, S])).then_inc(bias_loaded.sem, 16)
                    eng.dma_start(mcraw, a["mask.cols"][b]).then_inc(bias_loaded.sem, 16)
                    eng.dma_start(braw, a["bias"][b].rearrange("(t p) k -> p t k", p=P)).then_inc(bias_loaded.sem, 16)

                def move_parts(b, t):
                    s_made.wait(eng, b - 1, (t + 1) * A.tile_units)
                    for w in range(2):
                        split_step.wait(eng, b, 10 * t + 5 * (w + 1))
                        eng.dma_start(scratch[t % 2, w].rearrange("i p n -> p i n"), parts[:, w]).then_inc(parts_stored.sem, 16)
                    parts_stored.wait(eng, b, 32 * (t + 1))
                    for w in range(2):
                        for n, pair in enumerate(PAIRS):
                            eng.dma_start(blocks[t % 2][w][n * A.dk:(n + 1) * A.dk],
                                          scratch[t % 2, w, pair[w]].rearrange("(h r) n -> r h n", r=A.dk)
                                          ).then_inc(blocks_loaded[t % 2].sem, 16)

                if masked:
                    load_bias(0)
                eng.dma_start(ctxT[:, :, S:], context[:, :, S:]).then_inc(ctx_loaded, 16)
                if masked:
                    move_parts(0, 0)

                    def later(b):
                        load_bias(b)
                        move_parts(b - 1, 1)
                        move_parts(b, 0)

                    later(1)
                    with eng.Fori(2, B) as b:
                        later(b)
                    move_parts(B - 1, 1)

            @block.gpsimd
            def _(eng):
                def fold_rows(b):
                    bias_loaded.wait(eng, b, 48)
                    bias_ready.wait(eng, b - 1, 2)
                    apart(eng, m)
                    eng.tensor_scalar(mm, mraw, 0.0, None, ALU.is_equal).then_inc(bias_step.sem, 1)
                    eng.tensor_scalar(mcol, mcraw, 0.0, None, ALU.is_equal).then_inc(bias_step.sem, 1)
                    bias_step.wait(eng, b, 2)
                    apart(eng, m)
                    eng.tensor_scalar(rnext[:, 1, :], mm, A.dk ** -0.5, -(A.dk ** -0.5), ALU.mult, ALU.add
                                      ).then_inc(bias_step.sem, 1)
                    eng.tensor_scalar(mcol, mcol, -1.0, 1.0, ALU.mult, ALU.add).then_inc(bias_step.sem, 1)
                    eng.tensor_scalar(rnext[:, 0, :], mm, -1.0, 1.0, ALU.mult, ALU.add).then_inc(bias_step.sem, 1)

                def split(b, t):
                    for w, (full, ready) in enumerate(((qT[:, 0, :], q_ready), (kT, k_ready))):
                        n = 10 * t + 5 * w
                        ready.wait(eng, b, t + 1)
                        if w == 0:
                            parts_stored.wait(eng, b if t else b - 1, 32 * (t if t else T))
                        apart(eng, m)
                        eng.tensor_copy(parts[:, w, 0], full).then_inc(split_step.sem, 1)
                        for i in range(1, 3):
                            split_step.wait(eng, b, n + 2 * i - 1)
                            eng.tensor_tensor(rest[:, w], full if i == 1 else rest[:, w], parts[:, w, i - 1], ALU.subtract
                                              ).then_inc(split_step.sem, 1)
                            split_step.wait(eng, b, n + 2 * i)
                            apart(eng, m)
                            eng.tensor_copy(parts[:, w, i], rest[:, w]).then_inc(split_step.sem, 1)

                def spread_heads(b, t):
                    k_ready.wait(eng, b, t + 1)
                    s_made.wait(eng, b if t >= 2 else b - 1, (t - 1) * A.tile_units + (0 if t >= 2 else U))
                    apart(eng, m)
                    for j in range(A.per_tile):
                        last = eng.tensor_scalar(kz[:, (t % 2) * A.per_tile + j, :], kT, headmask[:, j:j + 1],
                                                 None, ALU.mult)
                    last.then_inc(kz_ready.sem, 1)

                prepare = split if masked else spread_heads
                if masked:
                    fold_rows(0)
                prepare(0, 0)
                fold_at = {8: -1, 10: 0, 14: 1, 22: 2, 28: 3}

                def turn(b, more):
                    for step in range(STEPS):
                        if masked and more and step in fold_at:
                            if fold_at[step] < 0:
                                fold_rows(b + 1)
                            else:
                                fold_bias(eng, b + 1, fold_at[step])
                        each_tile(step, b, more, prepare)
                        if closes_group(step - 5) and not masked:
                            spread_sums(eng, b, (step - 5) // GS)

                turns(eng, turn)

            @block.tensor
            def _(eng):
                def turn_x(b):
                    norm.wait(eng, b)
                    k_ready.wait(eng, b - 1, T)
                    if groups_before(TURN):
                        rb_copied.wait(eng, b - 1, groups_before(TURN))
                    for c in range(KC):
                        for t in range(QT):
                            last = eng.transpose(MB[c][:, t * P:(t + 1) * P], xstage[:, t, c * P:(c + 1) * P], ident[:, :])
                        last.then_inc(xt_made.sem, 1)

                def project(b, t, step):
                    if t == 0:
                        xt_ready.wait(eng, b, KC)
                        ctx_staged.wait(eng, b, 1)
                    else:
                        k_ready.wait(eng, b, t)
                        if groups_before(step):
                            rb_copied.wait(eng, b, groups_before(step))
                        else:
                            y_ready.wait(eng, b - 1, QT)
                    for kc in range(KC):
                        last = eng.matmul(MB[0][:, :], wq[:, kc, t * P:(t + 1) * P], xnT[:, kc, :],
                                          start=(kc == 0), stop=(kc == KC - 1))
                    last.then_inc(qk_made.sem, 1)
                    for kc in range(KC):
                        last = eng.matmul(MB[1][:, :], wk[:, kc, t * P:(t + 1) * P], ctxb[:, kc, :],
                                          start=(kc == 0), stop=(kc == KC - 1))
                    last.then_inc(qk_made.sem, 1)

                def values(b):
                    for n, (kt, c) in enumerate(VCHUNKS):
                        if n >= 2:
                            v_ready.wait(eng, b, n - 1)
                        else:
                            (low_ready if masked else p_ready).wait(eng, b - 1, U)
                        for kc in range(KC):
                            last = eng.matmul(SB[n % 2][:, 0:VW], ctxb[:, kc, kt * P:(kt + 1) * P],
                                              wv[:, kc, c * VW:(c + 1) * VW], start=(kc == 0), stop=(kc == KC - 1))
                        last.then_inc(v_made.sem, 1)

                eng.wait_ge(s["identity_made"], 8)
                if masked:
                    eng.wait_ge(cleared, 2)
                eng.wait_ge(s["wa_loaded" if masked else "wc_loaded"], 16 * (9 if masked else 4))
                turn_x(0)
                project(0, 0, 0)
                values(0)

                def turn(b, more):
                    for step in range(STEPS):
                        if step == TURN and more:
                            turn_x(b + 1)
                        each_tile(step, b, more, lambda b, t: project(b, t, step))
                        if step < U:
                            g, qt, j, h = A.unit(step)
                            tl, hj = divmod(h, A.per_tile)
                            if A.first_of_tile(step):
                                if masked:
                                    blocks_loaded[tl % 2].wait(eng, b, 16 * NBLOCKS)
                                else:
                                    kz_ready.wait(eng, b, tl + 1)
                                    q_ready.wait(eng, b, tl + 1)
                            if step >= 2:
                                (low_ready if masked else p_ready).wait(eng, b, step - 1)
                            else:
                                v_ready.wait(eng, b, len(VCHUNKS))
                            if masked:
                                left = blocks[tl % 2][0][:, hj, qt * P:(qt + 1) * P]
                                right = blocks[tl % 2][1][:, hj, :]
                            else:
                                left, right = qT[:, tl % 2, qt * P:(qt + 1) * P], kz[:, (tl % 2) * A.per_tile + hj, :]
                            eng.matmul(SB[step % 2][:, :], left, right, start=True, stop=True).then_inc(s_made.sem, 1)
                        u = step - 2
                        if 0 <= u < U:
                            p_ready.wait(eng, b, u + 1)
                            if u >= 2:
                                (pt_even if u % 2 == 0 else pt_odd).wait(eng, b, u // 2)
                            else:
                                (pt_even if u % 2 == 0 else pt_odd).wait(eng, b - 1, U // 2)
                            for kt in range(QT):
                                last = eng.transpose(TB[u % 2][:, kt * P:(kt + 1) * P],
                                                     prob[:, u % NS, kt * P:(kt + 1) * P], ident[:, :])
                            last.then_inc(t_made.sem, 1)
                        u = step - 4
                        if closes_pass(u):
                            g, qt, _, _ = A.unit(u)
                            pt_even.wait(eng, b, (u + 1) // 2)
                            pt_odd.wait(eng, b, (u + 1) // 2)
                            if qt == 0:
                                on_ready.wait(eng, b if g >= 2 else b - 1, g - 1 if g >= 2 else A.groups - 1 + g)
                            for kt in range(QT):
                                for j in range(A.group):
                                    h = g * A.group + j
                                    un = u - A.group + 1 + j
                                    r = A.strip * j
                                    last = eng.matmul(OB[g % 2][r:r + A.dk, qt * P:(qt + 1) * P],
                                                      vtok[:, kt, h * A.dk:(h + 1) * A.dk],
                                                      pT[:, un % PTR, kt * P:(kt + 1) * P],
                                                      start=(kt == 0), stop=(kt == QT - 1))
                            last.then_inc(av_done.sem, 1)
                        if step == U + 4 and more:
                            values(b + 1)
                        u = step - 7
                        if closes_group(u):
                            g = u // GS
                            rmat_ready.wait(eng, b, g + 1)
                            k_ready.wait(eng, b, tiles_until(step, more))
                            if g >= 1:
                                rb_copied.wait(eng, b, g)
                            else:
                                y_ready.wait(eng, b - 1, QT)
                            for qt in range(QT):
                                for j in range(A.group):
                                    r = A.strip * j
                                    last = eng.matmul(MB[1][r:r + A.dk, qt * P:(qt + 1) * P],
                                                      rmat[:, (g % 2) * GS + qt * A.group + j, 0:A.dk], ident[:, :],
                                                      start=True, stop=True)
                            last.then_inc(rb_made.sem, 1)
                    on_ready.wait(eng, b, A.groups)
                    rb_copied.wait(eng, b, A.groups)
                    for t in range(QT):
                        if t >= 2:
                            y_ready.wait(eng, b, t - 1)
                        NG = A.groups
                        for g in range(NG):
                            last = eng.matmul(MB[t % 2][:, 0:D], onorm[:, g, t * P:(t + 1) * P], wo[:, g, :],
                                              start=(g == 0), stop=(g == NG - 1))
                        last.then_inc(out_made.sem, 1)

                turns(eng, turn)

            @block.scalar
            def _(eng):
                def stage_ctx(b):
                    qk_made.wait(eng, b - 1, 2 * T)
                    eng.activation(ctxb, ctxT[:, :, bass.ts(b, S)], ACT.Copy).then_inc(ctx_staged.sem, 1)

                def values(b):
                    if not masked:
                        for n, (kt, c) in enumerate(VCHUNKS):
                            v_made.wait(eng, b, n + 1)
                            eng.activation(vtok[:, kt, c * VW:(c + 1) * VW], SB[n % 2][:, 0:VW], ACT.Copy
                                           ).then_inc(v_ready.sem, 1)

                eng.wait_ge(ctx_first, 16)
                stage_ctx(0)
                norm.all_parts(eng, 0, norm.on_scalar)
                values(0)
                eng.wait_ge(ctx_loaded, 16)

                def turn(b, more):
                    for step in range(STEPS):
                        if more:
                            for part in norm_parts(step):
                                norm.on_scalar(eng, b + 1, part)
                            if step == STAGE:
                                stage_ctx(b + 1)
                        if step < U:
                            if step == 0:
                                rinv_ready.wait(eng, b - 1, A.groups)
                            low_ready.wait(eng, b, step + 1)
                            if step >= NS:
                                t_made.wait(eng, b, step - NS + 1)
                            else:
                                t_made.wait(eng, b - 1, U)
                            src = sneg[:, step % NS, :] if masked else SB[step % 2][:, :]
                            done = eng.activation(prob[:, step % NS, :], src, ACT.Exp, bias=low[:, step:step + 1],
                                                  scale=-1.0 if masked else 1.0, accum_out=rowsum[:, step:step + 1])
                            done.then_inc(p_ready.sem, 1)
                        u = step - 2
                        if 0 <= u < U and u % 2 == 1:
                            t_made.wait(eng, b, u + 1)
                            if u >= PTR:
                                av_done.wait(eng, b, u // A.group - 1)
                            else:
                                av_done.wait(eng, b - 1, A.groups * QT)
                            eng.activation(pT[:, u % PTR, :], TB[u % 2][:, :], ACT.Copy).then_inc(pt_odd.sem, 1)
                        u = step - 7
                        if closes_group(u):
                            if u == U - 1 and more:
                                values(b + 1)
                            g = u // GS
                            rb_made.wait(eng, b, g + 1)
                            on_ready.wait(eng, b if g >= 1 else b - 1, g if g >= 1 else A.groups)
                            eng.activation(rbs, MB[1][:, :], ACT.Copy).then_inc(rb_copied.sem, 1)

                turns(eng, turn)

            @block.vector
            def _(eng):
                def turn_x(b):
                    for c in range(KC):
                        xt_made.wait(eng, b, c + 1)
                        if masked:
                            eng.tensor_copy(xnT[:, c, :], MB[c][:, :]).then_inc(xt_ready.sem, 1)
                        else:
                            eng.tensor_scalar(xnT[:, c, :], MB[c][:, :], m["cols"][:, 4 + c:5 + c],
                                              m["cols"][:, 6 + c:7 + c], ALU.mult, ALU.add).then_inc(xt_ready.sem, 1)

                def take_bias(b):
                    bias_step.wait(eng, b, 5)
                    eng.tensor_copy(rows, rnext).then_inc(bias_ready.sem, 1)

                def take_bias_tiles(b):
                    bias_step.wait(eng, b, 5 + 4 * QT)
                    eng.tensor_copy(bneg, bnext).then_inc(bias_ready.sem, 1)

                def take_qk(b, t):
                    if t == 0 and masked:
                        take_bias(b)
                        bias_ready.wait(eng, b, 1)
                    qk_made.wait(eng, b, 2 * t + 1)
                    if masked:
                        split_step.wait(eng, b if t else b - 1, 10 * (t if t else T))
                    else:
                        s_made.wait(eng, b if t >= 2 else b - 1, (t - 1) * A.tile_units + (0 if t >= 2 else U))
                    if masked:
                        eng.scalar_tensor_tensor(out=qT[:, 0, :], in0=MB[0][:, :],
                                                 scalar=m["cols"][:, t:t + 1], in1=rows[:, 1, :],
                                                 op0=ALU.add, op1=ALU.mult).then_inc(q_ready.sem, 1)
                    else:
                        eng.tensor_scalar(qT[:, t % 2, :], MB[0][:, :], A.dk ** -0.5, None, ALU.mult
                                          ).then_inc(q_ready.sem, 1)
                    qk_made.wait(eng, b, 2 * t + 2)
                    if not masked:
                        kz_ready.wait(eng, b if t >= 1 else b - 1, t if t >= 1 else T)
                    if masked:
                        eng.scalar_tensor_tensor(out=kT, in0=MB[1][:, :], scalar=m["cols"][:, 2 + t:3 + t],
                                                 in1=rows[:, 0, :], op0=ALU.add, op1=ALU.mult).then_inc(k_ready.sem, 1)
                    else:
                        eng.tensor_copy(kT, MB[1][:, :]).then_inc(k_ready.sem, 1)

                def values(b):
                    if masked:
                        for n, (kt, c) in enumerate(VCHUNKS):
                            v_made.wait(eng, b, n + 1)
                            eng.tensor_tensor(vtok[:, kt, :], SB[n % 2][:, 0:VW], v["A.bv"], ALU.add
                                              ).then_inc(v_ready.sem, 1)

                eng.wait_ge(s["x_first_loaded"], 16)
                eng.wait_ge(s["scalars_ready"], 2)
                eng.wait_ge(s["identity_made"], 8)
                if masked:
                    for k in OB:
                        eng.memset(k[:, :], 0.0).then_inc(cleared, 1)
                norm.all_parts(eng, 0, norm.on_vector)
                if masked:
                    eng.wait_ge(s["wa_loaded"], 16 * 9)
                else:
                    eng.wait_ge(bo_loaded, 16)
                turn_x(0)
                take_qk(0, 0)
                values(0)
                if masked:
                    for t in range(QT):
                        fold_bias(eng, 0, t)
                eng.wait_ge(s["x_loaded"], 16)

                def turn(b, more):
                    if masked:
                        take_bias_tiles(b)
                    for step in range(STEPS):
                        if more:
                            for part in norm_parts(step):
                                norm.on_vector(eng, b + 1, part)
                            if step == TURN:
                                turn_x(b + 1)
                        each_tile(step, b, more, take_qk)
                        if step < U:
                            g, qt, j, h = A.unit(step)
                            s_made.wait(eng, b, step + 1)
                            if masked:
                                if step == 0:
                                    bias_ready.wait(eng, b, 2)
                                if step >= NS:
                                    p_ready.wait(eng, b, step - NS + 1)
                                else:
                                    p_ready.wait(eng, b - 1, U)
                                apart(eng, m)
                                eng.tensor_tensor_reduce(sneg[:, step % NS, :], SB[step % 2][:, :], bneg[:, qt, :],
                                                         1.0, 3.0e38, ALU.add, ALU.min, low[:, step:step + 1]
                                                         ).then_inc(low_ready.sem, 1)
                            else:
                                if step == 0:
                                    p_ready.wait(eng, b - 1, U)
                                eng.tensor_reduce(low[:, step:step + 1], SB[step % 2][:, :], AX.X, ALU.max,
                                                  negate=True).then_inc(low_ready.sem, 1)
                        u = step - 2
                        if 0 <= u < U and u % 2 == 0:
                            t_made.wait(eng, b, u + 1)
                            if u >= PTR:
                                av_done.wait(eng, b, u // A.group - 1)
                            else:
                                av_done.wait(eng, b - 1, A.groups * QT)
                            eng.tensor_copy(pT[:, u % PTR, :], TB[u % 2][:, :]).then_inc(pt_even.sem, 1)
                        u = step - 4
                        if closes_group(u):
                            g = u // GS
                            p_ready.wait(eng, b, (g + 1) * GS)
                            rmat_ready.wait(eng, b - 1, A.groups)
                            eng.reciprocal(rinv[:, g * GS:(g + 1) * GS], rowsum[:, g * GS:(g + 1) * GS]
                                           ).then_inc(rinv_ready.sem, 1)
                            if masked:
                                spread_sums(eng, b, g)
                        if step == U + 4 and more:
                            values(b + 1)
                        u = step - 8
                        if closes_group(u):
                            g = u // GS
                            rb_copied.wait(eng, b, g + 1)
                            av_done.wait(eng, b, (g + 1) * QT)
                            eng.tensor_tensor(onorm[:, g, :], OB[g % 2][:, :], rbs, ALU.mult).then_inc(on_ready.sem, 1)
                    for t in range(QT):
                        out_made.wait(eng, b, t + 1)
                        eng.tensor_tensor(y[:, t % 2, :], MB[t % 2][:, 0:D], v["A.bo"] if masked else bo, ALU.add
                                          ).then_inc(y_ready.sem, 1)
                        y_ready.wait(eng, b, t + 1)
                        xt = x[:, b * QT + t, :]
                        eng.scalar_tensor_tensor(out=xt, in0=y[:, t % 2, :], scalar=gate, in1=xt,
                                                 op0=ALU.mult, op1=ALU.add).then_inc(turn_done.sem, 1)

                turns(eng, turn)


def moe_attention(nc, a, m):
    A = B_
    s, v = m["s"], weight_views(m)
    bank, ident, x = m["bank"], m["ident"], m["x"]
    SB, TB, OB, MB = bank[0:2], bank[2:4], bank[4:6], bank[6:8]
    wq, wk, wgate = v["B.wq"], v["B.wk"], v["B.gate"]
    GS, U, T, DK = A.group_units, A.units, A.tiles, A.dk
    headmask, gate = m["cst"][:, 8:10], m["gates"][:, 2:3]
    take, wide = carve(m), carve(m, "wc")
    NS, PTR, NG = 3, 2 * A.group, 3
    w_val = carve(m, "big1")(KC, HB * EB * DK)
    w_out = carve(m, "big2")(HB * EB // 2, D)
    vtok, otok = wide(QT, A.width), wide(QT, A.width)
    xstage, xnT = take(QT, D), take(KC, S)
    qT, kT, kz = take(2, S), take(S), take(2 * A.per_tile, S)
    prob, sneg, pT = take(NS, S), take(NS, S), take(PTR, QT * P)
    low, rowsum, rinv = take(U), take(U), take(U)
    oT = take(S)
    gates, hit, gm, gmr = (take(QT * HB, EB) for _ in range(4))
    best, rev = take(QT * HB), take(EB)
    scaled, spread, spreadT = take(NG, EB * DK), take(NG, EB * DK), take(NG, EB * DK)
    cneg = take(S)
    VU = QT * HB
    VALUES = [(h, t) for h in range(HB) for t in range(QT)]

    with ExitStack() as ctx:
        def sig(what, per):
            return Signal(nc, ctx, f"B_{what}", per)

        turn_done = sig("x_updated", QT)
        val_loaded = [ctx.enter_context(nc.semaphore(f"B_val_loaded_{h}")) for h in range(HB)]
        out_loaded = ctx.enter_context(nc.semaphore("B_out_loaded"))
        consts = ctx.enter_context(nc.semaphore("B_consts_made"))
        xt_made, xt_ready = sig("xn_transposed", KC), sig("xnT_ready", KC)
        gate_made, gate_ready, pick = sig("gate_made", 1), sig("gate_ready", 1), sig("pick_step", 6)
        val_made, val_scaled, v_ready = sig("val_made", VU), sig("val_scaled", VU), sig("v_ready", VU)
        qk_made, q_ready, k_ready = sig("qk_made", 2 * T), sig("q_ready", T), sig("k_ready", T)
        kz_ready = sig("kz_ready", T)
        s_made, low_ready, p_ready = sig("scores_made", U), sig("low_ready", U), sig("probs_ready", U)
        t_made = sig("probs_transposed", U)
        pt_even, pt_odd = sig("pT_even_ready", U // 2), sig("pT_odd_ready", U // 2)
        av_done, rinv_ready, gmr_ready = sig("av_done", A.groups * QT), sig("rinv_ready", A.groups), sig("gmr_ready", A.groups)
        ot_ready, heads_made, otok_ready = sig("oT_ready", A.groups), sig("heads_made", A.groups), sig("otok_ready", A.groups)
        sp_ready, spt_made, spt_ready = sig("spread_ready", VU), sig("spread_transposed", VU), sig("spreadT_ready", VU)
        sp_used = sig("spread_used", VU)
        norm = Norm(nc, ctx, m, "B", ("ln",), take, xstage, lambda eng, b: xt_made.wait(eng, b - 1, KC))

        STEPS = U + 8
        TURN = U - 9

        def closes_pass(u):
            return 0 <= u < U and u % A.group == A.group - 1

        def closes_group(u):
            return 0 <= u < U and u % GS == GS - 1

        def tile_at(step):
            u = step + 5
            return u // A.tile_units if 5 < u <= U and u % A.tile_units == 0 else None

        def groups_before(step):
            return sum(closes_group(z - 7) for z in range(step))

        def tiles_until(step, more):
            return 1 + sum(tile_at(z) is not None and (more or tile_at(z) < T) for z in range(step + 1))

        def norm_parts(step):
            first = TURN - 3 - norm.parts
            return [step - first] if 0 <= step - first < norm.parts else []

        def each_tile(step, b, more, do):
            t = tile_at(step)
            if t is not None and t < T:
                do(b, t)
            elif t is not None and more:
                do(b + 1, 0)

        with nc.Block() as block:
            @block.sync
            def _(eng):
                for h in range(HB):
                    eng.dma_start(w_val[:, :, h * EB * DK:(h + 1) * EB * DK],
                                  a["B.val"].rearrange("(c p) n -> p c n", p=P)[:, :, h * EB * DK:(h + 1) * EB * DK]
                                  ).then_inc(val_loaded[h], 16)
                eng.dma_start(w_out, a["B.out"]).then_inc(out_loaded, 16)

            @block.gpsimd
            def _(eng):
                eng.memset(cneg, 0.0).then_inc(consts, 1)
                eng.wait_ge(consts, 1)
                eng.affine_select(out=cneg, in_=cneg, compare_op=ALU.is_ge, fill=CAUSAL, base=S - P,
                                  pattern=[[-1, S]], channel_multiplier=1).then_inc(consts, 1)
                eng.iota(rev, pattern=[[-1, EB]], base=EB, channel_multiplier=0,
                         allow_small_or_imprecise_dtypes=True).then_inc(consts, 1)

                def spread_heads(b, t):
                    k_ready.wait(eng, b, t + 1)
                    s_made.wait(eng, b if t >= 2 else b - 1, (t - 1) * A.tile_units + (0 if t >= 2 else U))
                    apart(eng, m)
                    for j in range(A.per_tile):
                        last = eng.tensor_scalar(kz[:, (t % 2) * A.per_tile + j, :], kT, headmask[:, j:j + 1],
                                                 None, ALU.mult)
                    last.then_inc(kz_ready.sem, 1)

                spread_heads(0, 0)

                def turn(b, more):
                    for step in range(STEPS):
                        each_tile(step, b, more, spread_heads)

                turns(eng, turn)

            @block.tensor
            def _(eng):
                def turn_x(b):
                    norm.wait(eng, b)
                    k_ready.wait(eng, b - 1, T)
                    otok_ready.wait(eng, b - 1, groups_before(TURN))
                    for c in range(KC):
                        for t in range(QT):
                            last = eng.transpose(MB[c][:, t * P:(t + 1) * P], xstage[:, t, c * P:(c + 1) * P], ident[:, :])
                        last.then_inc(xt_made.sem, 1)

                def project(b, t, step):
                    if t == 0:
                        xt_ready.wait(eng, b, KC)
                    else:
                        k_ready.wait(eng, b, t)
                        if groups_before(step):
                            otok_ready.wait(eng, b, groups_before(step))
                        else:
                            otok_ready.wait(eng, b - 1, A.groups)
                    for kc in range(KC):
                        last = eng.matmul(MB[0][:, :], wq[:, kc, t * P:(t + 1) * P], xnT[:, kc, :],
                                          start=(kc == 0), stop=(kc == KC - 1))
                    last.then_inc(qk_made.sem, 1)
                    for kc in range(KC):
                        last = eng.matmul(MB[1][:, :], wk[:, kc, t * P:(t + 1) * P], xnT[:, kc, :],
                                          start=(kc == 0), stop=(kc == KC - 1))
                    last.then_inc(qk_made.sem, 1)

                def gate_logits(b):
                    ot_ready.wait(eng, b - 1, A.groups - 1)
                    xt_ready.wait(eng, b, KC)
                    for t in range(QT):
                        for kc in range(KC):
                            last = eng.matmul(OB[0][:, t * 64:(t + 1) * 64], xnT[:, kc, t * P:(t + 1) * P],
                                              wgate[:, kc, :], start=(kc == 0), stop=(kc == KC - 1))
                    last.then_inc(gate_made.sem, 1)

                def values(b):
                    for n, (h, t) in enumerate(VALUES):
                        if n >= 2:
                            val_scaled.wait(eng, b, n - 1)
                        else:
                            low_ready.wait(eng, b - 1, U)
                        if isinstance(b, int) and b == 0 and t == 0:
                            eng.wait_ge(val_loaded[h], 16)
                        for kc in range(KC):
                            last = eng.matmul(SB[n % 2][:, :], xnT[:, kc, t * P:(t + 1) * P],
                                              w_val[:, kc, h * EB * DK:(h + 1) * EB * DK],
                                              start=(kc == 0), stop=(kc == KC - 1))
                        last.then_inc(val_made.sem, 1)

                eng.wait_ge(s["wb_loaded"], 48)
                turn_x(0)
                gate_logits(0)
                project(0, 0, 0)
                values(0)

                def turn(b, more):
                    for step in range(STEPS):
                        if step == TURN and more:
                            turn_x(b + 1)
                        each_tile(step, b, more, lambda b, t: project(b, t, step))
                        if step < U:
                            g, qt, j, h = A.unit(step)
                            tl, hj = divmod(h, A.per_tile)
                            L = P * A.keys(qt)
                            if A.first_of_tile(step):
                                kz_ready.wait(eng, b, tl + 1)
                                q_ready.wait(eng, b, tl + 1)
                            if step >= 2:
                                low_ready.wait(eng, b, step - 1)
                            else:
                                val_scaled.wait(eng, b, VU)
                            eng.matmul(SB[step % 2][:, 0:L], qT[:, tl % 2, qt * P:(qt + 1) * P],
                                       kz[:, (tl % 2) * A.per_tile + hj, 0:L], start=True, stop=True
                                       ).then_inc(s_made.sem, 1)
                        u = step - 2
                        if 0 <= u < U:
                            qt = A.unit(u)[1]
                            p_ready.wait(eng, b, u + 1)
                            if u >= 2:
                                (pt_even if u % 2 == 0 else pt_odd).wait(eng, b, u // 2)
                            else:
                                spt_ready.wait(eng, b - 1, VU)
                            for kt in range(A.keys(qt)):
                                last = eng.transpose(TB[u % 2][:, kt * P:(kt + 1) * P],
                                                     prob[:, u % NS, kt * P:(kt + 1) * P], ident[:, :])
                            last.then_inc(t_made.sem, 1)
                        u = step - 4
                        if closes_pass(u):
                            g, qt, _, _ = A.unit(u)
                            pt_even.wait(eng, b, (u + 1) // 2)
                            pt_odd.wait(eng, b, (u + 1) // 2)
                            if u < A.group:
                                v_ready.wait(eng, b, VU)
                            if qt == 0 and g >= 2:
                                ot_ready.wait(eng, b, g - 1)
                            elif qt == 0:
                                turn_done.wait(eng, b - 1, QT)
                            for kt in range(A.keys(qt)):
                                for j in range(A.group):
                                    h = g * A.group + j
                                    r = A.strip * j
                                    last = eng.matmul(OB[g % 2][r:r + DK, qt * P:(qt + 1) * P],
                                                      vtok[:, kt, h * DK:(h + 1) * DK],
                                                      pT[:, (u - A.group + 1 + j) % PTR, kt * P:(kt + 1) * P],
                                                      start=(kt == 0), stop=(kt == A.keys(qt) - 1))
                            last.then_inc(av_done.sem, 1)
                        if step == U + 4 and more:
                            gate_logits(b + 1)
                        u = step - 7
                        if closes_group(u):
                            g = u // GS
                            ot_ready.wait(eng, b, g + 1)
                            k_ready.wait(eng, b, tiles_until(step, more))
                            if g >= 1:
                                otok_ready.wait(eng, b, g)
                            for qt in range(QT):
                                last = eng.transpose(MB[1][:, qt * P:(qt + 1) * P], oT[:, qt * P:(qt + 1) * P], ident[:, :])
                            last.then_inc(heads_made.sem, 1)
                    if more:
                        values(b + 1)
                        gate_ready.wait(eng, b + 1, 1)
                    otok_ready.wait(eng, b, A.groups)
                    eng.wait_ge(out_loaded, 16)
                    for n in range(VU + 2):
                        if n < VU:
                            sp_ready.wait(eng, b, n + 1)
                            if n >= 2:
                                spt_ready.wait(eng, b, n - 1)
                            for c in range(4):
                                last = eng.transpose(TB[n % 2][:, c * P:(c + 1) * P],
                                                     spread[:, n % NG, c * P:(c + 1) * P], ident[:, :])
                            last.then_inc(spt_made.sem, 1)
                        w = n - 2
                        if w >= 0:
                            qt, h = divmod(w, HB)
                            spt_ready.wait(eng, b, w + 1)
                            if qt >= 2 and h == 0:
                                turn_done.wait(eng, b, qt - 1)
                            for c in range(4):
                                last = eng.matmul(OB[qt % 2][:, 0:D], spreadT[:, w % NG, c * P:(c + 1) * P],
                                                  w_out[:, h * 4 + c, :], start=(h == 0 and c == 0),
                                                  stop=(h == HB - 1 and c == 3))
                            last.then_inc(sp_used.sem, 1)

                turns(eng, turn)

            @block.scalar
            def _(eng):
                def squash_gates(b):
                    gate_made.wait(eng, b, 1)
                    pick.wait(eng, b - 1, 6)
                    eng.activation(gates, OB[0][:, 0:QT * 64].rearrange("p (a e) -> p a e", e=EB), ACT.Sigmoid
                                   ).then_inc(gate_ready.sem, 1)

                norm.all_parts(eng, 0, norm.on_scalar)
                squash_gates(0)

                def turn(b, more):
                    for step in range(STEPS):
                        if more:
                            for part in norm_parts(step):
                                norm.on_scalar(eng, b + 1, part)
                        if step < U:
                            L = P * A.keys(A.unit(step)[1])
                            if step == 0:
                                rinv_ready.wait(eng, b - 1, A.groups)
                            low_ready.wait(eng, b, step + 1)
                            if step >= NS:
                                t_made.wait(eng, b, step - NS + 1)
                            else:
                                t_made.wait(eng, b - 1, U)
                            eng.activation(prob[:, step % NS, 0:L], sneg[:, step % NS, 0:L], ACT.Exp,
                                           bias=low[:, step:step + 1], scale=-1.0,
                                           accum_out=rowsum[:, step:step + 1]).then_inc(p_ready.sem, 1)
                        u = step - 2
                        if 0 <= u < U and u % 2 == 1:
                            L = P * A.keys(A.unit(u)[1])
                            t_made.wait(eng, b, u + 1)
                            if u >= PTR:
                                av_done.wait(eng, b, u // A.group - 1)
                            else:
                                av_done.wait(eng, b - 1, A.groups * QT)
                            eng.activation(pT[:, u % PTR, 0:L], TB[u % 2][:, 0:L], ACT.Copy).then_inc(pt_odd.sem, 1)
                        u = step - 5
                        if closes_group(u):
                            g = u // GS
                            av_done.wait(eng, b, (g + 1) * QT)
                            heads_made.wait(eng, b if g >= 1 else b - 1, g if g >= 1 else A.groups)
                            eng.activation(oT, OB[g % 2][:, :], ACT.Copy).then_inc(ot_ready.sem, 1)
                    if more:
                        squash_gates(b + 1)
                    for n in range(VU):
                        spt_made.wait(eng, b, n + 1)
                        if n >= NG:
                            sp_used.wait(eng, b, n - NG + 1)
                        else:
                            sp_used.wait(eng, b - 1, VU)
                        eng.activation(spreadT[:, n % NG, :], TB[n % 2][:, :], ACT.Copy).then_inc(spt_ready.sem, 1)

                turns(eng, turn)

            @block.vector
            def _(eng):
                def turn_x(b):
                    for c in range(KC):
                        xt_made.wait(eng, b, c + 1)
                        eng.tensor_copy(xnT[:, c, :], MB[c][:, :]).then_inc(xt_ready.sem, 1)

                def take_qk(b, t):
                    qk_made.wait(eng, b, 2 * t + 1)
                    s_made.wait(eng, b if t >= 2 else b - 1, (t - 1) * A.tile_units + (0 if t >= 2 else U))
                    eng.tensor_scalar(qT[:, t % 2, :], MB[0][:, :], -(DK ** -0.5), None, ALU.mult).then_inc(q_ready.sem, 1)
                    qk_made.wait(eng, b, 2 * t + 2)
                    kz_ready.wait(eng, b if t >= 1 else b - 1, t if t >= 1 else T)
                    eng.tensor_copy(kT, MB[1][:, :]).then_inc(k_ready.sem, 1)

                def pick_experts(b):
                    wide_best = best.unsqueeze(2).to_broadcast([P, VU, EB])
                    wide_rev = rev.unsqueeze(1).to_broadcast([P, VU, EB])
                    gate_ready.wait(eng, b, 1)
                    gmr_ready.wait(eng, b - 1, A.groups)
                    eng.tensor_reduce(best, gates, AX.X, ALU.max).then_inc(pick.sem, 1)
                    pick.wait(eng, b, 1)
                    eng.tensor_tensor(hit, gates, wide_best, ALU.is_equal).then_inc(pick.sem, 1)
                    pick.wait(eng, b, 2)
                    eng.tensor_tensor(gm, hit, wide_rev, ALU.mult).then_inc(pick.sem, 1)
                    pick.wait(eng, b, 3)
                    eng.tensor_reduce(best, gm, AX.X, ALU.max).then_inc(pick.sem, 1)
                    pick.wait(eng, b, 4)
                    eng.tensor_tensor(hit, gm, wide_best, ALU.is_equal).then_inc(pick.sem, 1)
                    pick.wait(eng, b, 5)
                    eng.tensor_tensor(gm, hit, gates, ALU.mult).then_inc(pick.sem, 1)
                    pick.wait(eng, b, 6)

                def values(b):
                    for n in range(VU + 1):
                        if n < VU:
                            h, t = VALUES[n]
                            val_made.wait(eng, b, n + 1)
                            if n >= NG:
                                v_ready.wait(eng, b, n - NG + 1)
                            else:
                                v_ready.wait(eng, b - 1, VU)
                            eng.tensor_tensor(scaled[:, n % NG, :].rearrange("p (e k) -> p e k", e=EB),
                                              SB[n % 2][:, :].rearrange("p (e k) -> p e k", e=EB),
                                              gm[:, t * HB + h, :].unsqueeze(2).to_broadcast([P, EB, DK]), ALU.mult
                                              ).then_inc(val_scaled.sem, 1)
                        w = n - 1
                        if w >= 0:
                            h, t = VALUES[w]
                            val_scaled.wait(eng, b, w + 1)
                            eng.tensor_reduce(vtok[:, t, h * DK:(h + 1) * DK],
                                              scaled[:, w % NG, :].rearrange("p (e k) -> p k e", e=EB), AX.X, ALU.add
                                              ).then_inc(v_ready.sem, 1)

                eng.wait_ge(consts, 3)
                norm.all_parts(eng, 0, norm.on_vector)
                turn_x(0)
                pick_experts(0)
                take_qk(0, 0)
                values(0)

                def turn(b, more):
                    for step in range(STEPS):
                        if more:
                            for part in norm_parts(step):
                                norm.on_vector(eng, b + 1, part)
                            if step == TURN:
                                turn_x(b + 1)
                        each_tile(step, b, more, take_qk)
                        if step < U:
                            g, qt, j, h = A.unit(step)
                            L = P * A.keys(qt)
                            s_made.wait(eng, b, step + 1)
                            if step >= NS:
                                p_ready.wait(eng, b, step - NS + 1)
                            else:
                                p_ready.wait(eng, b - 1, U)
                            apart(eng, m)
                            eng.tensor_tensor_reduce(sneg[:, step % NS, 0:L], SB[step % 2][:, 0:L], cneg[:, S - L:S],
                                                     1.0, 3.0e38, ALU.add, ALU.min, low[:, step:step + 1]
                                                     ).then_inc(low_ready.sem, 1)
                        u = step - 2
                        if 0 <= u < U and u % 2 == 0:
                            L = P * A.keys(A.unit(u)[1])
                            t_made.wait(eng, b, u + 1)
                            if u >= PTR:
                                av_done.wait(eng, b, u // A.group - 1)
                            else:
                                av_done.wait(eng, b - 1, A.groups * QT)
                            eng.tensor_copy(pT[:, u % PTR, 0:L], TB[u % 2][:, 0:L]).then_inc(pt_even.sem, 1)
                        u = step - 4
                        if closes_group(u):
                            g = u // GS
                            p_ready.wait(eng, b, (g + 1) * GS)
                            eng.reciprocal(rinv[:, g * GS:(g + 1) * GS], rowsum[:, g * GS:(g + 1) * GS]
                                           ).then_inc(rinv_ready.sem, 1)
                            rinv_ready.wait(eng, b, g + 1)

                            def of_group(z):
                                return z.rearrange("p (t h) e -> p t h e", h=HB)[:, :, 2 * g:2 * g + 2, :]

                            eng.tensor_tensor(of_group(gmr), of_group(gm),
                                              rinv[:, g * GS:(g + 1) * GS].rearrange("p (t j) -> p t j", j=2)
                                              .unsqueeze(3).to_broadcast([P, QT, 2, EB]), ALU.mult
                                              ).then_inc(gmr_ready.sem, 1)
                        u = step - 7
                        if closes_group(u):
                            g = u // GS
                            heads_made.wait(eng, b, g + 1)
                            sp_ready.wait(eng, b - 1, VU)
                            eng.tensor_copy(otok[:, :, g * P:(g + 1) * P],
                                            MB[1][:, :].rearrange("p (t c) -> p t c", t=QT)).then_inc(otok_ready.sem, 1)
                    gmr_ready.wait(eng, b, A.groups)
                    otok_ready.wait(eng, b, A.groups)
                    if more:
                        pick_experts(b + 1)
                        values(b + 1)
                    for n in range(VU + 3):
                        if n < VU:
                            qt, h = divmod(n, HB)
                            if n >= NG:
                                spt_made.wait(eng, b, n - NG + 1)
                            else:
                                spt_made.wait(eng, b - 1, VU)
                            eng.tensor_tensor(spread[:, n % NG, :].rearrange("p (e k) -> p e k", e=EB),
                                              otok[:, qt, h * DK:(h + 1) * DK].unsqueeze(1).to_broadcast([P, EB, DK]),
                                              gmr[:, n, :].unsqueeze(2).to_broadcast([P, EB, DK]), ALU.mult
                                              ).then_inc(sp_ready.sem, 1)
                        w = n - 3
                        if w >= 0 and w % HB == HB - 1:
                            qt = w // HB
                            sp_used.wait(eng, b, w + 1)
                            xt = x[:, b * QT + qt, :]
                            eng.scalar_tensor_tensor(out=xt, in0=OB[qt % 2][:, 0:D], scalar=gate, in1=xt,
                                                     op0=ALU.mult, op1=ALU.add).then_inc(turn_done.sem, 1)

                turns(eng, turn)


def product_key_experts(nc, a, m):
    s = m["s"]
    bank, ident, x = m["bank"], m["ident"], m["x"]
    HP, WP, UPP, XP, SP = bank[0:2], bank[2:5], bank[5], bank[6], bank[7]
    take, wide, wab = carve(m), carve(m, "wc"), carve(m, "wab")
    down = carve(m, "big1")(KC * ELO, EHI)
    up = carve(m, "big2")(ELO, D)
    hot = wide(8192).bitcast(BF16).rearrange("p (m t) -> p m t", t=P)
    wq, keysT = wab(2 * HD, D), wab(2 * HD, NK)
    simw = take(KC, 2 * HD * NK)
    xstage, xnT = take(D), take(KC, P)
    sims = take(2 * HD, NK)
    Hg = take(ELO, P)
    xn = Hg.rearrange("p (t a) b -> p t (a b)", a=D // P)
    G = carve(m, "wab")(ELO, P)
    scale, shift = take(B * QT), take(B * QT)
    elo = take(ELO * P // 2).bitcast(BF16).rearrange("p (j t) -> p j t", t=P)
    b12 = take(ELO * P // 2).bitcast(BF16).rearrange("p (j t) -> p j t", t=P)
    b3 = take(ELO * P // 2).bitcast(BF16).rearrange("p (j t) -> p j t", t=P)
    sel = take(4, P)
    selT = take(4 * P // 2).bitcast(BF16).rearrange("p (f t) -> p f t", t=P)
    top, topi = take(2 * HD, TOP), take(2 * HD, TOP).bitcast(U32)
    topf = take(2 * HD, TOP)
    pairs, eq = take(HD, TOP * TOP), take(HD * TOP, TOP)
    score, pk, pa, pb = take(HD, TOP), take(NSEL).bitcast(U32), take(NSEL).bitcast(U32), take(NSEL).bitcast(U32)
    paf, pbf, i1, i2, over = take(NSEL), take(NSEL), take(NSEL), take(NSEL), take(NSEL)
    part, rest = take(NSEL // 2).bitcast(BF16), take(NSEL)
    iota = take(TOP)
    NT, NJ = B * QT, 4
    gate = m["gates"][:, 3:4]
    TW = 16
    BJ = 4

    with ExitStack() as ctx:
        def sig(what, per):
            return Signal(nc, ctx, f"D_{what}", per)

        def sem(what):
            return ctx.enter_context(nc.semaphore("D_" + what))

        w_loaded, down_loaded, up_loaded = sem("w_loaded"), sem("down_loaded"), sem("up_loaded")
        fold_made, fold_ready, consts = sem("fold_made"), sem("fold_ready"), sem("consts")
        staged, xt_made, xt_ready = sig("staged", 1), sig("xn_transposed", 1), sig("xnT_ready", 1)
        sim_made, sim_ready = sig("sims_made", 2), sig("sims_ready", 2)
        STEPS = 52
        step = sig("pick_step", STEPS)
        selt_made, selt_ready = sig("sel_transposed", 1), sig("selT_ready", 1)
        h_made, h_ready = sig("hidden_made", ELO // NJ), sig("hidden_ready", ELO // NJ)
        hot_ready, elo_ready = sig("hot_ready", 1), sig("elo_ready", 1)
        b_ready, pool_b_ready = sig("b_ready", 1), sig("pool_b_ready", 2)
        w_made, g_ready = sig("weights_made", P // TW), sig("weighted", P // TW)
        up_made, turn_done = sig("up_made", 1), sig("x_updated", 1)
        ln_act, ln_dve, xn_done, xn_count = layer_norm(nc, ctx, m, "D", 2, x, xn, take, (scale, shift))

        def scored(eng, f, dst, j0, j1):
            return eng.tensor_tensor(dst[:, j0:j1, :], elo[:, j0:j1, :],
                                     selT[:, f, :].unsqueeze(1).to_broadcast([P, j1 - j0, P]), ALU.mult)

        def turns(eng, turn):
            turn(0, 2)
            with eng.Fori(1, NT - 2) as i:
                turn(i, 2)
            turn(NT - 2, 1)
            turn(NT - 1, 0)

        with nc.Block() as block:
            @block.sync
            def _(eng):
                eng.wait_ge(s["wa_loaded"], 16 * 9)
                eng.wait_ge(s["wb_loaded"], 48)
                eng.dma_start(wq, a["L1_ffn_w_q"].rearrange("(n p) d -> p n d", p=P)).then_inc(w_loaded, 16)
                eng.dma_start(keysT, a["D.keysT"]).then_inc(w_loaded, 16)
                eng.dma_start(down, a["D.downT"]).then_inc(down_loaded, 16)
                eng.dma_start(up, a["D.up"]).then_inc(up_loaded, 16)

            @block.gpsimd
            def _(eng):
                eng.iota(iota, pattern=[[1, TOP]], base=0, channel_multiplier=0,
                         allow_small_or_imprecise_dtypes=True).then_inc(consts, 1)
                eng.memset(sel, 0.0).then_inc(consts, 1)

                def scores(i):
                    elo_ready.wait(eng, i, 1)
                    selt_ready.wait(eng, i, 1)
                    w_made.wait(eng, i - 1, P // TW)
                    scored(eng, 3, b3, 0, ELO).then_inc(pool_b_ready.sem, 1)
                    scored(eng, 2, b12, BJ, ELO).then_inc(pool_b_ready.sem, 1)

                scores(0)

                def turn(i, ahead):
                    if ahead >= 1:
                        scores(i + 1)

                turns(eng, turn)

            @block.tensor
            def _(eng):
                eng.wait_ge(w_loaded, 32)
                for n in range(4):
                    kc, c = divmod(n, 2)
                    for q in range(HD):
                        hc = c * HD + q
                        last = eng.matmul(bank[n][:, q * NK:(q + 1) * NK], wq[:, hc, kc * P:(kc + 1) * P],
                                          keysT[:, hc, :], start=True, stop=True)
                    last.then_inc(fold_made, 1)

                def select(i):
                    h_ready.wait(eng, i - 1, ELO // NJ)
                    staged.wait(eng, i, 1)
                    for c in range(KC):
                        last = eng.transpose(XP[:, c * P:(c + 1) * P], xstage[:, c * P:(c + 1) * P], ident[:, :])
                    last.then_inc(xt_made.sem, 1)
                    xt_ready.wait(eng, i, 1)
                    for n in range(2):
                        for kc in range(KC):
                            last = eng.matmul(HP[n][:, :], xnT[:, kc, :], simw[:, kc, n * 512:(n + 1) * 512],
                                              start=(kc == 0), stop=(kc == KC - 1))
                        last.then_inc(sim_made.sem, 1)

                def turn_picks(i):
                    step.wait(eng, i, STEPS)
                    selt_ready.wait(eng, i - 1, 1)
                    for f in range(4):
                        last = eng.transpose(SP[:, f * P:(f + 1) * P], sel[:, f, :], ident[:, :])
                    last.then_inc(selt_made.sem, 1)

                def hidden(i):
                    for n in range(ELO // NJ):
                        if n >= 2:
                            h_ready.wait(eng, i, n - 1)
                        else:
                            sim_ready.wait(eng, i, 2)
                        for q in range(NJ):
                            for kc in range(KC):
                                last = eng.matmul(HP[n % 2][:, q * P:(q + 1) * P], down[:, kc * ELO + n * NJ + q, :],
                                                  xnT[:, kc, :], start=(kc == 0), stop=(kc == KC - 1))
                        last.then_inc(h_made.sem, 1)

                eng.wait_ge(fold_ready, 4)
                select(0)
                eng.wait_ge(down_loaded, 16)
                hidden(0)
                select(1)
                turn_picks(0)
                eng.wait_ge(up_loaded, 16)

                def turn(i, ahead):
                    hot_ready.wait(eng, i, 1)
                    b_ready.wait(eng, i, 1)
                    pool_b_ready.wait(eng, i, 2)
                    for n in range(P // TW):
                        g_ready.wait(eng, i, n - 2)
                        for q in range(TW):
                            t = n * TW + q
                            dst = WP[n % 3][:, q * ELO:(q + 1) * ELO]
                            eng.matmul(dst, hot[:, :, t], b12[:, :, t], start=True, stop=False)
                            last = eng.matmul(dst, hot[:, :, t], b3[:, :, t], start=False, stop=True)
                        last.then_inc(w_made.sem, 1)
                    if ahead >= 1:
                        turn_picks(i + 1)
                        hidden(i + 1)
                    if ahead >= 2:
                        select(i + 2)
                    g_ready.wait(eng, i, P // TW)
                    turn_done.wait(eng, i - 1, 1)
                    for j in range(ELO):
                        last = eng.matmul(UPP[:, 0:D], G[:, j, :], up[:, j, :], start=(j == 0), stop=(j == ELO - 1))
                    last.then_inc(up_made.sem, 1)

                turns(eng, turn)

            @block.scalar
            def _(eng):
                ln_act(eng)
                for n in range(4):
                    kc, c = divmod(n, 2)
                    eng.wait_ge(fold_made, n + 1)
                    eng.activation(simw[:, kc, c * 512:(c + 1) * 512], bank[n][:, :], ACT.Copy).then_inc(fold_ready, 1)
                eng.wait_ge(xn_done, xn_count)

                def stage(i):
                    xt_made.wait(eng, i, 0)
                    eng.activation(xstage, x[:, i, :], ACT.Identity, scale=scale[:, bass.ds(i, 1)],
                                   bias=shift[:, bass.ds(i, 1)]).then_inc(staged.sem, 1)

                def select(i):
                    xt_made.wait(eng, i, 1)
                    for c in range(KC):
                        last = eng.activation(xnT[:, c, :], XP[:, c * P:(c + 1) * P], ACT.Copy,
                                              scale=m["cols"][:, 8 + c:9 + c])
                    last.then_inc(xt_ready.sem, 1)
                    for n in range(2):
                        sim_made.wait(eng, i, n + 1)
                        if n == 0:
                            step.wait(eng, i, 0)
                        eng.activation(sims[:, n * HD:(n + 1) * HD, :],
                                       HP[n][:, :].rearrange("p (a b) -> p a b", b=NK), ACT.Copy).then_inc(sim_ready.sem, 1)

                def picks(i):
                    selt_made.wait(eng, i, 1)
                    hot_ready.wait(eng, i - 1, 1)
                    b_ready.wait(eng, i - 1, 1)
                    pool_b_ready.wait(eng, i - 1, 2)
                    eng.activation(selT, SP[:, :].rearrange("p (f t) -> p f t", t=P), ACT.Copy).then_inc(selt_ready.sem, 1)

                def hidden(i):
                    g_ready.wait(eng, i - 1, P // TW)
                    for n in range(ELO // NJ):
                        h_made.wait(eng, i, n + 1)
                        eng.activation(Hg[:, n * NJ:(n + 1) * NJ, :], HP[n % 2][:, :].rearrange("p (j t) -> p j t", t=P),
                                       ACT.Gelu).then_inc(h_ready.sem, 1)

                stage(0)
                select(0)
                stage(1)
                hidden(0)
                select(1)
                picks(0)

                def turn(i, ahead):
                    if ahead >= 2:
                        stage(i + 2)
                    if ahead >= 1:
                        picks(i + 1)
                        hidden(i + 1)
                    if ahead >= 2:
                        select(i + 2)

                turns(eng, turn)

            @block.vector
            def _(eng):
                eng.wait_ge(consts, 2)
                ln_dve(eng)

                def topk(i):
                    n = [0]

                    def mark(ins):
                        ins.then_inc(step.sem, 1)
                        n[0] += 1

                    def reach():
                        step.wait(eng, i, n[0])

                    sim_ready.wait(eng, i, 2)
                    apart(eng, m)
                    for hc in range(2 * HD):
                        mark(eng.max(top[:, hc, :], sims[:, hc, :]))
                    reach()
                    apart(eng, m)
                    for hc in range(2 * HD):
                        last = eng.max_index(topi[:, hc, :], top[:, hc, :], sims[:, hc, :])
                    mark(last)
                    halves = top.rearrange("p (h c) k -> p h c k", c=2)
                    mark(eng.tensor_tensor(pairs.rearrange("p h (a b) -> p h a b", b=TOP),
                                           halves[:, :, 0, :].unsqueeze(3).to_broadcast([P, HD, TOP, TOP]),
                                           halves[:, :, 1, :].unsqueeze(2).to_broadcast([P, HD, TOP, TOP]), ALU.add))
                    reach()
                    apart(eng, m)
                    for h in range(HD):
                        mark(eng.max(score[:, h, :], pairs[:, h, :]))
                    mark(eng.tensor_copy(topf, topi))
                    reach()
                    apart(eng, m)
                    for h in range(HD):
                        last = eng.max_index(pk[:, h * TOP:(h + 1) * TOP], score[:, h, :], pairs[:, h, :])
                    mark(last)
                    reach()
                    mark(eng.tensor_scalar(pa, pk, 3, None, ALU.logical_shift_right))
                    mark(eng.tensor_scalar(pb, pk, TOP - 1, None, ALU.bitwise_and))
                    reach()
                    mark(eng.tensor_copy(paf, pa))
                    mark(eng.tensor_copy(pbf, pb))
                    reach()
                    numbers = topf.rearrange("p (h c) k -> p h c k", c=2)
                    for c, place, key in ((0, paf, i1), (1, pbf, i2)):
                        mark(eng.tensor_tensor(eq, place.unsqueeze(2).to_broadcast([P, NSEL, TOP]),
                                               iota.unsqueeze(1).to_broadcast([P, NSEL, TOP]), ALU.is_equal))
                        reach()
                        e4 = eq.rearrange("p (h k) a -> p h k a", k=TOP)
                        mark(eng.tensor_tensor(e4, e4, numbers[:, :, c, :].unsqueeze(2).to_broadcast([P, HD, TOP, TOP]),
                                               ALU.mult))
                        reach()
                        mark(eng.tensor_reduce(key, eq, AX.X, ALU.add))
                        reach()
                    mark(eng.tensor_scalar(over, i2, float(ELO), None, ALU.is_ge))
                    reach()
                    selt_made.wait(eng, i, 0)
                    for d in range(2):
                        mark(eng.scalar_tensor_tensor(out=sel[:, 0, d * NSEL:(d + 1) * NSEL], in0=i1, scalar=2.0, in1=over,
                                                      op0=ALU.mult, op1=ALU.add))
                        mark(eng.scalar_tensor_tensor(out=sel[:, 1, d * NSEL:(d + 1) * NSEL], in0=over,
                                                      scalar=-float(ELO), in1=i2, op0=ALU.mult, op1=ALU.add))
                    flat = score.rearrange("p h k -> p (h k)")
                    mark(eng.tensor_scalar(rest, flat, 0.0, None, ALU.max))
                    reach()
                    for q in range(3):
                        dst = sel[:, 2, q * NSEL:(q + 1) * NSEL] if q < 2 else sel[:, 3, 0:NSEL]
                        mark(eng.tensor_copy(part, rest))
                        reach()
                        mark(eng.tensor_copy(dst, part))
                        if q < 2:
                            mark(eng.tensor_tensor(rest, rest, part, ALU.subtract))
                            reach()
                    assert n[0] == STEPS, n[0]

                def onehots(i):
                    selt_ready.wait(eng, i, 1)
                    pool_b_ready.wait(eng, i - 1, 2)
                    for j in range(ELO):
                        last = eng.tensor_scalar(elo[:, j, :], selT[:, 1, :], float(j), None, ALU.is_equal)
                    last.then_inc(elo_ready.sem, 1)
                    for mm in range(EHI):
                        last = eng.tensor_scalar(hot[:, mm, :], selT[:, 0, :], float(mm), None, ALU.is_equal)
                    last.then_inc(hot_ready.sem, 1)
                    elo_ready.wait(eng, i, 1)
                    scored(eng, 2, b12, 0, BJ).then_inc(b_ready.sem, 1)

                def update(i):
                    up_made.wait(eng, i, 1)
                    xt = x[:, i, :]
                    eng.scalar_tensor_tensor(out=xt, in0=UPP[:, 0:D], scalar=gate, in1=xt, op0=ALU.mult, op1=ALU.add
                                             ).then_inc(turn_done.sem, 1)

                topk(0)
                onehots(0)
                topk(1)

                def turn(i, ahead):
                    h_ready.wait(eng, i, ELO // NJ)
                    for n in range(P // TW):
                        w_made.wait(eng, i, n + 1)
                        if n == 0:
                            up_made.wait(eng, i - 1, 1)
                        eng.tensor_tensor(G[:, :, n * TW:(n + 1) * TW],
                                          WP[n % 3][:, :].rearrange("p (t j) -> p j t", j=ELO),
                                          Hg[:, :, n * TW:(n + 1) * TW], ALU.mult).then_inc(g_ready.sem, 1)
                    if not isinstance(i, int) or i > 0:
                        update(i - 1)
                    if ahead >= 1:
                        onehots(i + 1)
                    if ahead >= 2:
                        topk(i + 2)

                turns(eng, turn)
                update(NT - 1)


def layouts(i):
    c = np.ascontiguousarray
    r = {"x": c(i["x"]), "bias": c(i["fside_BxSxS2_0"]), "mask": c(i["mask_BxS2_ik0"])}
    r["ctxT"] = c(np.transpose(i["ctx_1024"], (2, 0, 1)).reshape(D, B * S))
    for n, k in (("A.wqT", "WQ"), ("A.wkT", "WK"), ("A.wvT", "WV"), ("A.woT", "WO")):
        r[n] = c(i[f"L0_xattn_{k}_w"].T)
    r["B.val"] = c(i["L0_ffn_value_experts"].transpose(2, 1, 0, 3).reshape(D, -1))
    r["B.out"] = c(i["L0_ffn_output_experts"].reshape(4, 2, HB, 64, D).transpose(1, 3, 2, 0, 4).reshape(P, 32, D))
    r["D.keysT"] = c(i["L1_ffn_keys"].transpose(3, 0, 2, 1).reshape(P, 2 * HD, NK))
    r["D.downT"] = c(i["L1_ffn_expert_down"].reshape(EHI, ELO, KC, P).transpose(3, 2, 1, 0).reshape(P, KC * ELO, EHI))
    r["D.up"] = c(i["L1_ffn_expert_up"].reshape(EHI, ELO, D))
    r["C.wk"] = c(i["L1_xattn_w_kv"][:, :1024])
    r["C.wv"] = c(i["L1_xattn_w_kv"][:, 1024:])
    r["mask.cols"] = c(i["mask_BxS2_ik0"].reshape(B, QT, P).transpose(0, 2, 1))
    for k in ("L0_xattn_WQ_b", "L0_xattn_WK_b", "L1_xattn_ln_gamma", "L1_xattn_ln_beta", "L1_ffn_norm_w"):
        r[k + ".cols"] = c(i[k].reshape(KC, P).T)
    for k in ("L0_ffn_w_gate", "L0_ffn_w_q", "L0_ffn_w_k", "L1_ffn_w_q", "g_xattn", "g_ffn", "L1_xattn_gate", "L0_xattn_WV_b", "L0_xattn_WO_b", "L1_xattn_b_out", "L1_xattn_w_q",
              "L1_xattn_w_out"):
        r[k] = c(i[k])
    return r


def kernel(**inputs):
    import concourse.bacc as bacc
    from concourse.bass_utils import run_bass_kernel_spmd

    arrays = layouts({name: np.asarray(value) for name, value in inputs.items()})
    nc = bacc.Bacc("TRN2", target_bir_lowering=False, num_devices=1)
    names = {key: "in_" + key.replace(".", "_") for key in arrays}
    views = {key: nc.dram_tensor(names[key], value.shape, mybir.dt.from_np(value.dtype), kind="ExternalInput").ap()
             for key, value in arrays.items()}
    out = nc.dram_tensor("out_0", (B, S, D), F32, kind="ExternalOutput").ap()
    build(nc, views, out)
    result = run_bass_kernel_spmd(nc, [{names[key]: value for key, value in arrays.items()}], core_ids=[0])
    return result.results[0]["out_0"]
```

```python
from contextlib import ExitStack

import numpy as np

import concourse.bass as bass
from concourse import mybir

F32 = mybir.dt.float32
BF16 = mybir.dt.bfloat16
I32 = mybir.dt.int32
U32 = mybir.dt.uint32
ALU = mybir.AluOpType
ACT = mybir.ActivationFunctionType
AX = mybir.AxisListType

P = 128
B, S, D = 4, 512, 256
QT = S // P
KC = D // P
EPS = 1e-5
MASKED = 1e9
CAUSAL = 3.0e38


class Signal:

    def __init__(self, nc, ctx, name, per):
        self.sem = ctx.enter_context(nc.semaphore(name))
        self.per = per

    def at(self, turn, n):
        return turn * self.per + n

    def due(self, turn, n):
        return not isinstance(turn, int) or turn * self.per + n > 0


TICKS = 16


def apart(eng, m):
    m["ticks"] += 1
    n = m["ticks"] % TICKS
    if eng is m["pool"]:
        eng.tensor_tensor(m["tick"][:, n:n + 1], m["cst"][:, 0:1], m["cst"][:, 1:2], ALU.mult)
    else:
        eng.memset(m["tick"][:, TICKS + n:TICKS + n + 1], 0.0)


ORDER = (0, 3, 1, 2)


class Attention:

    def __init__(self, heads, dk, group, causal=False):
        self.heads, self.dk, self.group, self.causal = heads, dk, group, causal
        self.width = heads * dk
        self.per_tile = P // dk
        self.tiles = heads // self.per_tile
        self.groups = heads // group
        self.strip = P // group
        self.units = heads * QT
        self.tile_units = self.per_tile * QT
        self.group_units = group * QT
        self.order = ORDER if causal else tuple(range(QT))

    def unit(self, u):
        g, r = divmod(u, self.group_units)
        n, j = divmod(r, self.group)
        return g, self.order[n], j, g * self.group + j

    def column(self, u):
        g, qt, j, _ = self.unit(u)
        return g * self.group_units + qt * self.group + j

    def opens_group(self, u):
        return u % self.group_units == self.group - 1

    def keys(self, qt):
        return qt + 1 if self.causal else QT

    def first_of_tile(self, s):
        return s % self.tile_units == 0 and 0 <= s < self.units


A_ = Attention(16, 16, 4)
B_ = Attention(8, 64, 2, causal=True)
C_ = Attention(16, 64, 2)

EB, HB = 8, 8
HD, NK, TOP = 8, 64, 8
NSEL = HD * TOP
EHI, ELO = 128, 32


def build(nc, a, out, phases="ABCD"):
    with ExitStack() as ctx:
        def sb(name, shape, dt=F32):
            return ctx.enter_context(nc.sbuf_tensor(name, shape, dt))

        def sem(name):
            return ctx.enter_context(nc.semaphore(name))

        bank = [ctx.enter_context(nc.psum_tensor(f"bank{i}", [P, 512], F32)) for i in range(8)]
        m = {"phases": phases, "out": out, "stored_tiles": 0, "stores": 0}
        m["bank"] = bank
        m["x"] = sb("x", [P, B * QT, D])
        m["ident"] = sb("ident", [P, P])
        m["cst"] = sb("cst", [P, 64])
        m["gates"] = sb("gates", [P, 8])
        m["cols"] = sb("cols", [P, 32])
        m["tick"], m["ticks"] = sb("tick", [P, 2 * TICKS]), 0
        m["pool"] = nc.gpsimd
        m["big1"] = sb("big1", [P, 8192])
        m["big2"] = sb("big2", [P, 8192])
        m["wab"] = sb("wab", [P, 5248])
        m["wc"] = sb("wc", [P, 8192])
        m["work"] = sb("work", [P, 18800])
        s = {n: sem(n) for n in ("x_loaded", "identity_made", "wa_loaded", "wb_loaded",
                                 "wc_loaded", "c_ctx_loaded", "stored", "dq_loaded", "up_loaded", "x_first_loaded", "scalars_loaded", "scalars_ready")}
        m["s"] = s
        prologue(nc, a, m)
        if "A" in phases:
            cross_attention(nc, a, m, A_, "A")
        if "B" in phases:
            moe_attention(nc, a, m)
        if "C" in phases:
            cross_attention(nc, a, m, C_, "C")
        if "D" in phases:
            product_key_experts(nc, a, m)
        epilogue(nc, out, m)


def carve(m, key="work"):
    at = [0]
    region = m[key]

    def take(*shape):
        n = int(np.prod(shape))
        v = region[:, at[0]:at[0] + n]
        at[0] += n
        if len(shape) == 2:
            v = v.rearrange("p (a b) -> p a b", b=shape[1])
        elif len(shape) == 3:
            v = v.rearrange("p (a b c) -> p a b c", b=shape[1], c=shape[2])
        return v
    return take


def weight_views(m):
    ta = carve(m, "wab")
    v = {}
    v["A.wq"], v["A.wk"], v["A.wv"] = ta(KC, 256), ta(KC, 256), ta(KC, 256)
    v["A.wo"] = ta(4, 256)
    v["A.bv"], v["A.bo"] = ta(256), ta(256)
    v["B.gate"], v["B.wq"], v["B.wk"] = ta(KC, HB * EB), ta(KC, 512), ta(KC, 512)
    tc = carve(m, "big1")
    v["C.wq"], v["C.wk"], v["C.wv"] = tc(KC, 1024), tc(KC, 1024), tc(KC, 1024)
    v["C.wo"] = tc(8, 256)
    return v


def fetch_rest(eng, a, m):
    tokens = a["x"].rearrange("b (t p) d -> p (b t) d", p=P)
    eng.dma_start(m["x"][:, QT:, :], tokens[:, QT:, :]).then_inc(m["s"]["x_loaded"], 16)


def prologue(nc, a, m):
    s, v = m["s"], weight_views(m)
    with nc.Block() as block:
        @block.sync
        def _(eng):
            tokens = a["x"].rearrange("b (t p) d -> p (b t) d", p=P)
            eng.dma_start(m["x"][:, 0:QT, :], tokens[:, 0:QT, :]).then_inc(s["x_first_loaded"], 16)
            for n, name in enumerate(("g_xattn", "g_ffn")):
                eng.dma_start(m["gates"][:, 2 * n:2 * n + 2],
                              a[name].rearrange("(a n) -> a n", a=1).to_broadcast([P, 2])
                              ).then_inc(s["scalars_loaded"], 16)
            eng.dma_start(m["gates"][:, 4:5], a["L1_xattn_gate"].rearrange("(a n) -> a n", a=1).to_broadcast([P, 1])
                          ).then_inc(s["scalars_loaded"], 16)
            for n, name in enumerate(("L0_xattn_WQ_b", "L0_xattn_WK_b", "L1_xattn_ln_gamma", "L1_xattn_ln_beta",
                                      "L1_ffn_norm_w")):
                eng.dma_start(m["cols"][:, 2 * n:2 * n + 2], a[name + ".cols"]).then_inc(s["scalars_loaded"], 16)
            for name, key in (("A.wq", "A.wqT"), ("A.wk", "A.wkT"), ("A.wv", "A.wvT")):
                eng.dma_start(v[name], a[key].rearrange("(c p) n -> p c n", p=P)).then_inc(s["wa_loaded"], 16)
            for name, key in (("A.bv", "L0_xattn_WV_b"), ("A.bo", "L0_xattn_WO_b")):
                eng.dma_start(v[name], a[key].rearrange("(a n) -> a n", a=1).to_broadcast([P, 256])
                              ).then_inc(s["wa_loaded"], 16)
            for name, key in (("B.gate", "L0_ffn_w_gate"), ("B.wq", "L0_ffn_w_q"), ("B.wk", "L0_ffn_w_k")):
                eng.dma_start(v[name], a[key].rearrange("(c p) n -> p c n", p=P)).then_inc(s["wb_loaded"], 16)
            if "A" not in m["phases"]:
                fetch_rest(eng, a, m)
            eng.wait_ge(s["identity_made"], 4)
            for j in range(4):
                eng.dma_start(v["A.wo"][32 * j:32 * j + 16, :, :],
                              a["A.woT"].rearrange("(g j r) n -> j r g n", j=4, r=16)[j]).then_inc(s["wa_loaded"], 16)

        @block.gpsimd
        def _(eng):
            eng.memset(m["ident"][:, :], 0.0).then_inc(s["identity_made"], 1)
            eng.wait_ge(s["identity_made"], 1)
            eng.affine_select(out=m["ident"][:, :], in_=m["ident"][:, :], compare_op=ALU.not_equal, fill=1.0,
                              base=0, pattern=[[-1, P]], channel_multiplier=1).then_inc(s["identity_made"], 1)
            eng.memset(m["cst"][:, :], 1.0).then_inc(s["identity_made"], 1)
            eng.memset(v["A.wo"], 0.0).then_inc(s["identity_made"], 1)
            eng.wait_ge(s["identity_made"], 4)
            n = 4
            for at, count, rows in ((0, 8, 16), (8, 2, 64)):
                part = m["cst"][:, at:at + count]
                eng.affine_select(out=part, in_=part, compare_op=ALU.is_ge, fill=0.0, base=0,
                                  pattern=[[-rows, count]], channel_multiplier=1).then_inc(s["identity_made"], 1)
                n += 1
                eng.wait_ge(s["identity_made"], n)
                eng.affine_select(out=part, in_=part, compare_op=ALU.is_ge, fill=0.0, base=rows - 1,
                                  pattern=[[rows, count]], channel_multiplier=-1).then_inc(s["identity_made"], 1)
                n += 1

        @block.scalar
        def _(eng):
            eng.wait_ge(s["scalars_loaded"], 8 * 16)
            eng.activation(m["gates"][:, 0:5], m["gates"][:, 0:5], ACT.Tanh).then_inc(s["scalars_ready"], 1)

        @block.vector
        def _(eng):
            eng.wait_ge(s["scalars_ready"], 1)
            eng.tensor_tensor(m["gates"][:, 5:6], m["gates"][:, 1:2], m["gates"][:, 4:5], ALU.mult
                              ).then_inc(s["scalars_ready"], 1)


def fetch_c(eng, a, m):
    s, v = m["s"], weight_views(m)
    eng.dma_start(c_context(m), a["ctxT"].rearrange("(c p) n -> p c n", p=P)).then_inc(s["c_ctx_loaded"], 16)
    for w, key in (("C.wq", "L1_xattn_w_q"), ("C.wk", "C.wk"), ("C.wv", "C.wv"), ("C.wo", "L1_xattn_w_out")):
        eng.dma_start(v[w], a[key].rearrange("(c p) n -> p c n", p=P)).then_inc(s["wc_loaded"], 16)
    m["c_fetched"] = True


def c_context(m):
    return m["wc"][:, 4096:8192].rearrange("p (c n) -> p c n", c=KC)


def d_views(m):
    wab = carve(m, "wab")
    return wab(2 * HD, D), wab(2 * HD, NK), carve(m, "big2")(ELO, D)


def fetch_d(eng, a, m):
    s = m["s"]
    wq, keysT, up = d_views(m)
    eng.wait_ge(s["wa_loaded"], 16 * 9)
    eng.wait_ge(s["wb_loaded"], 48)
    eng.dma_start(wq, a["L1_ffn_w_q"].rearrange("(n p) d -> p n d", p=P)).then_inc(s["dq_loaded"], 16)
    eng.dma_start(keysT, a["D.keysT"]).then_inc(s["dq_loaded"], 16)
    eng.dma_start(up, a["D.up"]).then_inc(s["up_loaded"], 16)
    m["d_fetched"] = True


def epilogue(nc, out, m):
    tiles = out.rearrange("b (t p) d -> p (b t) d", p=P)
    stored, first = m["s"]["stored"], m["stored_tiles"]
    with nc.Block() as block:
        @block.sync
        def _(eng):
            eng.dma_start(tiles[:, first:, :], m["x"][:, first:, :]).then_inc(stored, 16)
            eng.wait_ge(stored, 16 * (m["stores"] + 1))


class Norm:

    def __init__(self, nc, ctx, m, name, take, second=None, tiles=QT, xstage=None, staged_used=None):
        self.m, self.x, self.xn, self.tiles = m, m["x"], xstage, tiles
        self.eps = [EPS] + ([] if second is None else [second])
        self.staged_used = staged_used
        self.kinds = [("stats", 0), ("stats", 1)]
        for r in range(len(self.eps)):
            self.kinds += [("add eps", r), ("root", r)]
        self.kinds += [("write", 0), ("write", 1)]
        self.parts = len(self.kinds)
        self.stats, self.mv = take(tiles, 6), take(tiles, 2)
        self.rstd, self.shift = take(tiles), take(tiles)
        self.std, self.ve, self.r2, self.t1, self.t2 = (take(tiles) for _ in range(5))
        self.eps_added = Signal(nc, ctx, name + "_eps_added", len(self.eps))
        self.root_ready = Signal(nc, ctx, name + "_root_ready", len(self.eps))
        self.step = Signal(nc, ctx, name + "_stat_step", 2 * tiles + (5 if second is None else 13))
        self.done = Signal(nc, ctx, name + "_xn_ready", tiles if xstage is not None else 1)

    def on_scalar(self, eng, b, part):
        kind, r = self.kinds[part]
        if kind == "add eps":
            eng.wait_ge(self.eps_added.sem, self.eps_added.at(b, r + 1))
            eng.activation(self.std, self.ve, ACT.Sqrt).then_inc(self.root_ready.sem, 1)

    def on_vector(self, eng, b, part):
        kind, r = self.kinds[part]
        mean, var = self.mv[:, :, 0], self.mv[:, :, 1]
        half, base = self.tiles // 2, 2 * self.tiles
        mine = range(r * half, (r + 1) * half)
        if kind == "stats":
            for t in mine:
                eng.bn_stats(self.stats[:, t, :], self.x[:, b * QT + t, :]).then_inc(self.step.sem, 1)
            eng.wait_ge(self.step.sem, self.step.at(b, 2 * half * r + half))
            apart(eng, self.m)
            for t in mine:
                eng.bn_aggr(self.mv[:, t, :], self.stats[:, t, :]).then_inc(self.step.sem, 1)
        if kind == "add eps" and r == 0:
            eng.wait_ge(self.step.sem, self.step.at(b, base))
            eng.tensor_scalar(self.ve, var, self.eps[0], None, ALU.add).then_inc(self.eps_added.sem, 1)
        if kind == "add eps" and r == 1:
            eng.tensor_tensor(self.t1, self.rstd, self.rstd, ALU.mult).then_inc(self.step.sem, 1)
            eng.wait_ge(self.step.sem, self.step.at(b, base + 6))
            eng.tensor_tensor(self.t2, self.t1, var, ALU.mult).then_inc(self.step.sem, 1)
            eng.wait_ge(self.step.sem, self.step.at(b, base + 7))
            eng.tensor_scalar(self.ve, self.t2, self.eps[1], None, ALU.add).then_inc(self.eps_added.sem, 1)
        if kind == "root":
            n, root = (base, self.rstd) if r == 0 else (base + 7, self.r2)
            eng.wait_ge(self.root_ready.sem, self.root_ready.at(b, r + 1))
            eng.reciprocal(root, self.std).then_inc(self.step.sem, 1)
            eng.wait_ge(self.step.sem, self.step.at(b, n + 1))
            eng.tensor_tensor(self.t1, root, root, ALU.mult).then_inc(self.step.sem, 1)
            eng.wait_ge(self.step.sem, self.step.at(b, n + 2))
            eng.tensor_tensor(self.t2, self.t1, self.ve, ALU.mult).then_inc(self.step.sem, 1)
            eng.wait_ge(self.step.sem, self.step.at(b, n + 3))
            eng.tensor_scalar(self.t1, self.t2, -0.5, 1.5, ALU.mult, ALU.add).then_inc(self.step.sem, 1)
            eng.wait_ge(self.step.sem, self.step.at(b, n + 4))
            eng.tensor_tensor(root, root, self.t1, ALU.mult).then_inc(self.step.sem, 1)
            eng.wait_ge(self.step.sem, self.step.at(b, n + 5))
            if r == 1:
                eng.tensor_tensor(self.rstd, self.rstd, root, ALU.mult).then_inc(self.step.sem, 1)
                eng.wait_ge(self.step.sem, self.step.at(b, n + 6))
        if kind == "write" and self.xn is None and r == 0:
            eng.scalar_tensor_tensor(out=self.shift, in0=mean, scalar=-1.0, in1=self.rstd, op0=ALU.mult, op1=ALU.mult
                                     ).then_inc(self.done.sem, 1)
        if kind == "write" and self.xn is not None:
            if r == 0:
                used, count = self.staged_used
                if used.due(b - 1, count):
                    eng.wait_ge(used.sem, used.at(b - 1, count))
            for t in mine:
                eng.tensor_scalar(self.xn[:, t, :], self.x[:, b * QT + t, :], mean[:, t:t + 1], self.rstd[:, t:t + 1],
                                  ALU.subtract, ALU.mult).then_inc(self.done.sem, 1)

    def all_parts(self, eng, b, on):
        for part in range(self.parts):
            on(eng, b, part)


def turns(eng, turn):
    turn(0, True)
    with eng.Fori(1, B - 1) as b:
        turn(b, True)
    turn(B - 1, False)


def cross_attention(nc, a, m, A, name):
    masked = name == "A"
    s, v = m["s"], weight_views(m)
    bank, ident, x = m["bank"], m["ident"], m["x"]
    SB, TB, OB, MB = bank[0:2], bank[2:4], bank[4:6], bank[6:8]
    wq, wk, wv, wo = (v[f"{name}.{w}"] for w in ("wq", "wk", "wv", "wo"))
    GS, U, T = A.group_units, A.units, A.tiles
    headmask = m["cst"][:, 0:8] if name == "A" else m["cst"][:, 8:10]
    gate = m["gates"][:, 0:1] if name == "A" else m["gates"][:, 5:6]
    take, big1, big2 = carve(m), carve(m, "big1"), carve(m, "big2")
    NS, PTR = 3, 2 * A.group
    if masked:
        ctxT, vtok = big2(KC, B * S), big1(QT, A.width)
    else:
        ctxT, vtok = c_context(m), carve(m, "wc")(QT, A.width)
    xstage = take(QT, D)
    xnT, ctxb = take(KC, S), take(KC, S)
    qT, kT = take(2, S), take(S)
    prob = take(NS, S)
    pT = take(PTR, QT * P)
    low, rowsum, rinv = take(U), take(U), take(U)
    y = take(2, D)
    if masked:
        blocks = carve(m, "wc")(2, A.per_tile * S).bitcast(BF16)
        blocks = [[blocks[:, slot, w * A.per_tile * S:(w + 1) * A.per_tile * S].rearrange("p (h n) -> p h n", n=S)
                   for w in range(2)] for slot in range(2)]
        parts = big1(2, 3 * S // 2).bitcast(BF16).rearrange("p w (i n) -> p w i n", n=S)
        rest = take(2, S)
        scratch = nc.dram_tensor("parts", [2, 2, 3, P, S], BF16).ap()
        onorm, braw = big2(A.groups, S), big2(QT, S)
        rbs, rmat = take(S), take(2 * GS, A.dk)
        sneg = take(NS, S)
        bneg, bnext = big1(QT, S), big1(QT, S)
        rows, rnext = take(2, S), big1(2, S)
        mm, bt = take(S), take(S)
        mraw, mcraw, mcol = take(S).bitcast(I32), take(QT).bitcast(I32), take(QT)
    else:
        kz, onorm, bo = take(2 * A.per_tile, S), take(A.groups, S), take(D)

    PAIRS = [(i, j) for i in range(3) for j in range(3)][:8]
    NBLOCKS = 2 * len(PAIRS)

    with ExitStack() as ctx:
        def sig(what, per):
            return Signal(nc, ctx, f"{name}_{what}", per)

        turn_done = sig("x_updated", QT)
        ctx_staged = sig("ctx_staged", 1)
        xt_made = sig("xn_transposed", KC)
        xt_ready = sig("xnT_ready", KC)
        v_made, v_ready = sig("v_made", QT * max(1, A.width // 512)), sig("v_ready", QT * max(1, A.width // 512))
        qk_made, q_ready, k_ready = sig("qk_made", 2 * T), sig("q_ready", T), sig("k_ready", T)
        if masked:
            bias_loaded, bias_step, bias_ready = sig("bias_loaded", 48), sig("bias_step", 5 + 4 * QT), sig("bias_ready", 2)
            cleared = ctx.enter_context(nc.semaphore(f"{name}_cleared"))
            split_step, parts_stored = sig("split_step", 10 * T), sig("parts_stored", 32 * T)
            blocks_loaded = [sig(f"blocks_loaded_{slot}", 16 * NBLOCKS) for slot in range(2)]
        else:
            kz_ready = sig("kz_ready", T)
            bo_loaded = ctx.enter_context(nc.semaphore(f"{name}_bo_loaded"))
        if masked:
            ctx_first = ctx.enter_context(nc.semaphore("A_ctx_first_loaded"))
            ctx_loaded = ctx.enter_context(nc.semaphore("A_ctx_loaded"))
        else:
            ctx_first = ctx_loaded = s["c_ctx_loaded"]
        s_made, low_ready = sig("scores_made", U), sig("low_ready", U)
        p_ready = sig("probs_ready", U)
        t_made = sig("probs_transposed", U)
        pt_even, pt_odd = sig("pT_even_ready", U // 2), sig("pT_odd_ready", U // 2)
        av_done = sig("av_done", A.groups * QT)
        rinv_ready = sig("rinv_ready", A.groups if masked else U)
        if masked:
            rmat_ready = sig("rmat_ready", A.groups)
            rb_made, rb_copied = sig("rb_made", A.groups), sig("rb_copied", A.groups)
        else:
            normed = sig("probs_normalised", U)
        on_ready = sig("onorm_ready", A.groups)
        out_made, y_ready = sig("out_made", QT), sig("y_ready", QT)
        norm = Norm(nc, ctx, m, name, take, None if masked else EPS, QT, xstage,
                    (xt_made, KC))

        STEPS = U + 9
        STAGE, TURN = (8, 20) if masked else (U - 11, U - 8)
        VW = min(512, A.width)
        VCHUNKS = [(kt, c) for kt in range(QT) for c in range(A.width // VW)]

        def closes_pass(u):
            return 0 <= u < U and u % A.group == A.group - 1

        def closes_group(u):
            return 0 <= u < U and u % GS == GS - 1

        def tile_at(step):
            if masked:
                return {2: 1, A.tile_units + 2: T}.get(step)
            u = step + 5
            return u // A.tile_units if 5 < u <= U and u % A.tile_units == 0 else None

        def groups_before(step):
            return sum(closes_group(z - 7) for z in range(step)) if masked else 0

        def tiles_until(step, more):
            return 1 + sum(tile_at(z) is not None and (more or tile_at(z) < T) for z in range(step + 1))

        def norm_parts(step):
            first = TURN - 5 - norm.parts
            return [step - first] if 0 <= step - first < norm.parts else []

        def each_tile(step, b, more, do):
            t = tile_at(step)
            if t is not None and t < T:
                do(b, t)
            elif t is not None and more:
                do(b + 1, 0)

        def split(eng, b, t):
            for w, (full, ready) in enumerate(((qT[:, 0, :], q_ready), (kT, k_ready))):
                n = 10 * t + 5 * w
                eng.wait_ge(ready.sem, ready.at(b, t + 1))
                if w == 0:
                    if parts_stored.due(b if t else b - 1, 32 * (t if t else T)):
                        eng.wait_ge(parts_stored.sem, parts_stored.at(b if t else b - 1, 32 * (t if t else T)))
                apart(eng, m)
                eng.tensor_copy(parts[:, w, 0], full).then_inc(split_step.sem, 1)
                for i in range(1, 3):
                    eng.wait_ge(split_step.sem, split_step.at(b, n + 2 * i - 1))
                    eng.tensor_tensor(rest[:, w], full if i == 1 else rest[:, w], parts[:, w, i - 1], ALU.subtract
                                      ).then_inc(split_step.sem, 1)
                    eng.wait_ge(split_step.sem, split_step.at(b, n + 2 * i))
                    apart(eng, m)
                    eng.tensor_copy(parts[:, w, i], rest[:, w]).then_inc(split_step.sem, 1)

        def spread_sums(eng, b, g):
            eng.wait_ge(rinv_ready.sem, rinv_ready.at(b, g + 1))
            if rb_made.due(b if g >= 2 else b - 1, g - 1 if g >= 2 else A.groups - 1 + g):
                eng.wait_ge(rb_made.sem, rb_made.at(b if g >= 2 else b - 1, g - 1 if g >= 2 else A.groups - 1 + g))
            eng.tensor_copy(rmat[:, (g % 2) * GS:(g % 2 + 1) * GS, :],
                            rinv[:, g * GS:(g + 1) * GS].unsqueeze(2).to_broadcast([P, GS, A.dk])
                            ).then_inc(rmat_ready.sem, 1)

        def fold_bias(eng, b, t):
            n = 5 + 4 * t
            eng.wait_ge(bias_step.sem, bias_step.at(b, n))
            if eng is m["pool"]:
                apart(eng, m)
            eng.tensor_scalar(mm, rnext[:, 0, :], mcol[:, t:t + 1], None, ALU.mult).then_inc(bias_step.sem, 1)
            eng.wait_ge(bias_step.sem, bias_step.at(b, n + 1))
            eng.tensor_tensor(bt, braw[:, t, :], mm, ALU.mult).then_inc(bias_step.sem, 1)
            eng.wait_ge(bias_step.sem, bias_step.at(b, n + 2))
            if eng is m["pool"]:
                apart(eng, m)
            eng.tensor_scalar(mm, mm, -MASKED, MASKED, ALU.mult, ALU.add).then_inc(bias_step.sem, 1)
            eng.wait_ge(bias_step.sem, bias_step.at(b, n + 3))
            eng.tensor_tensor(bnext[:, t, :], mm, bt, ALU.subtract).then_inc(bias_step.sem, 1)

        with nc.Block() as block:
            @block.sync
            def _(eng):
                context = a["ctxT"].rearrange("(c p) n -> p c n", p=P)
                if masked:
                    eng.dma_start(ctxT[:, :, 0:S], context[:, :, 0:S]).then_inc(ctx_first, 16)
                if not masked:
                    eng.dma_start(bo, a["L1_xattn_b_out"].rearrange("(a n) -> a n", a=1).to_broadcast([P, D])
                                  ).then_inc(bo_loaded, 16)
                    if "c_fetched" not in m:
                        fetch_c(eng, a, m)
                    fetch_d(eng, a, m)
                def load_bias(b):
                    if bias_step.due(b - 1, 5 + 4 * QT):
                        eng.wait_ge(bias_step.sem, bias_step.at(b - 1, 5 + 4 * QT))
                    eng.dma_start(mraw, a["mask"][b].rearrange("(a k) -> a k", a=1).to_broadcast([P, S])).then_inc(bias_loaded.sem, 16)
                    eng.dma_start(mcraw, a["mask.cols"][b]).then_inc(bias_loaded.sem, 16)
                    eng.dma_start(braw, a["bias"][b].rearrange("(t p) k -> p t k", p=P)).then_inc(bias_loaded.sem, 16)

                def move_parts(b, t):
                    if s_made.due(b - 1, (t + 1) * A.tile_units):
                        eng.wait_ge(s_made.sem, s_made.at(b - 1, (t + 1) * A.tile_units))
                    for w in range(2):
                        eng.wait_ge(split_step.sem, split_step.at(b, 10 * t + 5 * (w + 1)))
                        eng.dma_start(scratch[t % 2, w].rearrange("i p n -> p i n"), parts[:, w]).then_inc(parts_stored.sem, 16)
                    eng.wait_ge(parts_stored.sem, parts_stored.at(b, 32 * (t + 1)))
                    for w in range(2):
                        for n, pair in enumerate(PAIRS):
                            eng.dma_start(blocks[t % 2][w][n * A.dk:(n + 1) * A.dk],
                                          scratch[t % 2, w, pair[w]].rearrange("(h r) n -> r h n", r=A.dk)
                                          ).then_inc(blocks_loaded[t % 2].sem, 16)

                if masked:
                    load_bias(0)
                    fetch_rest(eng, a, m)
                    eng.dma_start(ctxT[:, :, S:], context[:, :, S:]).then_inc(ctx_loaded, 16)
                    move_parts(0, 0)

                    def later(b):
                        load_bias(b)
                        move_parts(b - 1, 1)
                        move_parts(b, 0)

                    later(1)
                    with eng.Fori(2, B) as b:
                        later(b)
                    move_parts(B - 1, 1)

            @block.gpsimd
            def _(eng):
                def fold_rows(b):
                    eng.wait_ge(bias_loaded.sem, bias_loaded.at(b, 48))
                    if bias_ready.due(b - 1, 2):
                        eng.wait_ge(bias_ready.sem, bias_ready.at(b - 1, 2))
                    apart(eng, m)
                    eng.tensor_scalar(mm, mraw, 0.0, None, ALU.is_equal).then_inc(bias_step.sem, 1)
                    eng.tensor_scalar(mcol, mcraw, 0.0, None, ALU.is_equal).then_inc(bias_step.sem, 1)
                    eng.wait_ge(bias_step.sem, bias_step.at(b, 2))
                    apart(eng, m)
                    eng.tensor_scalar(rnext[:, 1, :], mm, A.dk ** -0.5, -(A.dk ** -0.5), ALU.mult, ALU.add
                                      ).then_inc(bias_step.sem, 1)
                    eng.tensor_scalar(mcol, mcol, -1.0, 1.0, ALU.mult, ALU.add).then_inc(bias_step.sem, 1)
                    eng.tensor_scalar(rnext[:, 0, :], mm, -1.0, 1.0, ALU.mult, ALU.add).then_inc(bias_step.sem, 1)

                def spread_heads(b, t):
                    eng.wait_ge(k_ready.sem, k_ready.at(b, t + 1))
                    if s_made.due(b if t >= 2 else b - 1, (t - 1) * A.tile_units + (0 if t >= 2 else U)):
                        eng.wait_ge(s_made.sem, s_made.at(b if t >= 2 else b - 1, (t - 1) * A.tile_units + (0 if t >= 2 else U)))
                    apart(eng, m)
                    for j in range(A.per_tile):
                        last = eng.tensor_scalar(kz[:, (t % 2) * A.per_tile + j, :], kT, headmask[:, j:j + 1],
                                                 None, ALU.mult)
                    last.then_inc(kz_ready.sem, 1)

                prepare = (lambda b, t: split(eng, b, t)) if masked else spread_heads
                if masked:
                    fold_rows(0)
                else:
                    spread_heads(0, 0)
                fold_at = {8: -1, 10: 0, 14: 1, 22: 2, 28: 3}

                def turn(b, more):
                    for step in range(STEPS):
                        if masked and more and step in fold_at:
                            if fold_at[step] < 0:
                                fold_rows(b + 1)
                            else:
                                fold_bias(eng, b + 1, fold_at[step])
                        each_tile(step, b, more, prepare)

                turns(eng, turn)

            @block.tensor
            def _(eng):
                def turn_x(b):
                    eng.wait_ge(norm.done.sem, norm.done.at(b, norm.done.per))
                    if k_ready.due(b - 1, T):
                        eng.wait_ge(k_ready.sem, k_ready.at(b - 1, T))
                    if groups_before(TURN):
                        if rb_copied.due(b - 1, groups_before(TURN)):
                            eng.wait_ge(rb_copied.sem, rb_copied.at(b - 1, groups_before(TURN)))
                    for c in range(KC):
                        for t in range(QT):
                            last = eng.transpose(MB[c][:, t * P:(t + 1) * P], xstage[:, t, c * P:(c + 1) * P], ident[:, :])
                        last.then_inc(xt_made.sem, 1)

                def project(b, t, step):
                    if t == 0:
                        eng.wait_ge(xt_ready.sem, xt_ready.at(b, KC))
                        eng.wait_ge(ctx_staged.sem, ctx_staged.at(b, 1))
                    else:
                        eng.wait_ge(k_ready.sem, k_ready.at(b, t))
                        if groups_before(step):
                            eng.wait_ge(rb_copied.sem, rb_copied.at(b, groups_before(step)))
                        else:
                            if y_ready.due(b - 1, QT):
                                eng.wait_ge(y_ready.sem, y_ready.at(b - 1, QT))
                    for kc in range(KC):
                        last = eng.matmul(MB[0][:, :], wq[:, kc, t * P:(t + 1) * P], xnT[:, kc, :],
                                          start=(kc == 0), stop=(kc == KC - 1))
                    last.then_inc(qk_made.sem, 1)
                    for kc in range(KC):
                        last = eng.matmul(MB[1][:, :], wk[:, kc, t * P:(t + 1) * P], ctxb[:, kc, :],
                                          start=(kc == 0), stop=(kc == KC - 1))
                    last.then_inc(qk_made.sem, 1)

                def values(b):
                    for n, (kt, c) in enumerate(VCHUNKS):
                        if n >= 2:
                            eng.wait_ge(v_ready.sem, v_ready.at(b, n - 1))
                        else:
                            if (low_ready if masked else p_ready).due(b - 1, U):
                                eng.wait_ge((low_ready if masked else p_ready).sem, (low_ready if masked else p_ready).at(b - 1, U))
                        for kc in range(KC):
                            last = eng.matmul(SB[n % 2][:, 0:VW], ctxb[:, kc, kt * P:(kt + 1) * P],
                                              wv[:, kc, c * VW:(c + 1) * VW], start=(kc == 0), stop=(kc == KC - 1))
                        last.then_inc(v_made.sem, 1)

                eng.wait_ge(s["identity_made"], 8)
                if masked:
                    eng.wait_ge(cleared, 2)
                eng.wait_ge(s["wa_loaded" if masked else "wc_loaded"], 16 * (9 if masked else 4))
                turn_x(0)
                project(0, 0, 0)
                values(0)

                def turn(b, more):
                    for step in range(STEPS):
                        if step == TURN and more:
                            turn_x(b + 1)
                        each_tile(step, b, more, lambda b, t: project(b, t, step))
                        if step < U:
                            g, qt, j, h = A.unit(step)
                            tl, hj = divmod(h, A.per_tile)
                            if A.first_of_tile(step):
                                if masked:
                                    eng.wait_ge(blocks_loaded[tl % 2].sem, blocks_loaded[tl % 2].at(b, 16 * NBLOCKS))
                                else:
                                    eng.wait_ge(kz_ready.sem, kz_ready.at(b, tl + 1))
                                    eng.wait_ge(q_ready.sem, q_ready.at(b, tl + 1))
                            if step >= 2:
                                eng.wait_ge((low_ready if masked else p_ready).sem, (low_ready if masked else p_ready).at(b, step - 1))
                            else:
                                eng.wait_ge(v_ready.sem, v_ready.at(b, len(VCHUNKS)))
                            if masked:
                                left = blocks[tl % 2][0][:, hj, qt * P:(qt + 1) * P]
                                right = blocks[tl % 2][1][:, hj, :]
                            else:
                                left, right = qT[:, tl % 2, qt * P:(qt + 1) * P], kz[:, (tl % 2) * A.per_tile + hj, :]
                            eng.matmul(SB[step % 2][:, :], left, right, start=True, stop=True).then_inc(s_made.sem, 1)
                        u = step - 2
                        if 0 <= u < U:
                            eng.wait_ge((p_ready if masked else normed).sem, (p_ready if masked else normed).at(b, u + 1))
                            if u >= 2:
                                eng.wait_ge((pt_even if u % 2 == 0 else pt_odd).sem, (pt_even if u % 2 == 0 else pt_odd).at(b, u // 2))
                            else:
                                if (pt_even if u % 2 == 0 else pt_odd).due(b - 1, U // 2):
                                    eng.wait_ge((pt_even if u % 2 == 0 else pt_odd).sem, (pt_even if u % 2 == 0 else pt_odd).at(b - 1, U // 2))
                            for kt in range(QT):
                                last = eng.transpose(TB[u % 2][:, kt * P:(kt + 1) * P],
                                                     prob[:, u % NS, kt * P:(kt + 1) * P], ident[:, :])
                            last.then_inc(t_made.sem, 1)
                        u = step - 4
                        if closes_pass(u):
                            g, qt, _, _ = A.unit(u)
                            eng.wait_ge(pt_even.sem, pt_even.at(b, (u + 1) // 2))
                            eng.wait_ge(pt_odd.sem, pt_odd.at(b, (u + 1) // 2))
                            if qt == 0:
                                if on_ready.due(b if g >= 2 else b - 1, g - 1 if g >= 2 else A.groups - 1 + g):
                                    eng.wait_ge(on_ready.sem, on_ready.at(b if g >= 2 else b - 1, g - 1 if g >= 2 else A.groups - 1 + g))
                        kts = range(QT) if closes_pass(u) else ()
                        if masked:
                            kts = range(2) if closes_pass(u) else range(2, QT) if closes_pass(u - 1) else ()
                            u = u if closes_pass(u) else u - 1
                        if kts:
                            g, qt, _, _ = A.unit(u)
                            for kt in kts:
                                for j in range(A.group):
                                    h = g * A.group + j
                                    un = u - A.group + 1 + j
                                    r = A.strip * j
                                    last = eng.matmul(OB[g % 2][r:r + A.dk, qt * P:(qt + 1) * P],
                                                      vtok[:, kt, h * A.dk:(h + 1) * A.dk],
                                                      pT[:, un % PTR, kt * P:(kt + 1) * P],
                                                      start=(kt == 0), stop=(kt == QT - 1))
                            if QT - 1 in kts:
                                last.then_inc(av_done.sem, 1)
                        if step == U + 4 and more:
                            values(b + 1)
                        u = step - 7
                        if closes_group(u) and masked:
                            g = u // GS
                            eng.wait_ge(rmat_ready.sem, rmat_ready.at(b, g + 1))
                            eng.wait_ge(k_ready.sem, k_ready.at(b, tiles_until(step, more)))
                            if g >= 1:
                                eng.wait_ge(rb_copied.sem, rb_copied.at(b, g))
                            else:
                                if y_ready.due(b - 1, QT):
                                    eng.wait_ge(y_ready.sem, y_ready.at(b - 1, QT))
                            for qt in range(QT):
                                for j in range(A.group):
                                    r = A.strip * j
                                    last = eng.matmul(MB[1][r:r + A.dk, qt * P:(qt + 1) * P],
                                                      rmat[:, (g % 2) * GS + qt * A.group + j, 0:A.dk], ident[:, :],
                                                      start=True, stop=True)
                            last.then_inc(rb_made.sem, 1)
                    eng.wait_ge(on_ready.sem, on_ready.at(b, A.groups))
                    if masked:
                        eng.wait_ge(rb_copied.sem, rb_copied.at(b, A.groups))
                    elif more:
                        eng.wait_ge(k_ready.sem, k_ready.at(b + 1, 1))
                    for t in range(QT):
                        if t >= 2:
                            eng.wait_ge(y_ready.sem, y_ready.at(b, t - 1))
                        NG = A.groups
                        for g in range(NG):
                            last = eng.matmul(MB[t % 2][:, 0:D], onorm[:, g, t * P:(t + 1) * P], wo[:, g, :],
                                              start=(g == 0), stop=(g == NG - 1))
                        last.then_inc(out_made.sem, 1)

                turns(eng, turn)

            @block.scalar
            def _(eng):
                def stage_ctx(b):
                    if qk_made.due(b - 1, 2 * T):
                        eng.wait_ge(qk_made.sem, qk_made.at(b - 1, 2 * T))
                    eng.activation(ctxb, ctxT[:, :, bass.ts(b, S)], ACT.Copy).then_inc(ctx_staged.sem, 1)

                def values(b):
                    if not masked:
                        for n, (kt, c) in enumerate(VCHUNKS):
                            eng.wait_ge(v_made.sem, v_made.at(b, n + 1))
                            eng.activation(vtok[:, kt, c * VW:(c + 1) * VW], SB[n % 2][:, 0:VW], ACT.Copy
                                           ).then_inc(v_ready.sem, 1)

                norm.all_parts(eng, 0, norm.on_scalar)
                eng.wait_ge(ctx_first, 16)
                stage_ctx(0)
                values(0)
                eng.wait_ge(ctx_loaded, 16)

                def turn(b, more):
                    for step in range(STEPS):
                        if more:
                            for part in norm_parts(step):
                                norm.on_scalar(eng, b + 1, part)
                            if step == STAGE:
                                stage_ctx(b + 1)
                        u = step - 2
                        if 0 <= u < U and u % 2 == 1:
                            eng.wait_ge(t_made.sem, t_made.at(b, u + 1))
                            if u >= PTR:
                                eng.wait_ge(av_done.sem, av_done.at(b, u // A.group - 1))
                            else:
                                if av_done.due(b - 1, A.groups * QT):
                                    eng.wait_ge(av_done.sem, av_done.at(b - 1, A.groups * QT))
                            eng.activation(pT[:, u % PTR, :], TB[u % 2][:, :], ACT.Copy).then_inc(pt_odd.sem, 1)
                        if step < U:
                            if step == 0:
                                if rinv_ready.due(b - 1, rinv_ready.per):
                                    eng.wait_ge(rinv_ready.sem, rinv_ready.at(b - 1, rinv_ready.per))
                            eng.wait_ge(low_ready.sem, low_ready.at(b, step + 1))
                            if step >= NS:
                                eng.wait_ge(t_made.sem, t_made.at(b, step - NS + 1))
                            else:
                                if t_made.due(b - 1, U):
                                    eng.wait_ge(t_made.sem, t_made.at(b - 1, U))
                            src = sneg[:, step % NS, :] if masked else SB[step % 2][:, :]
                            done = eng.activation(prob[:, step % NS, :], src, ACT.Exp, bias=low[:, step:step + 1],
                                                  scale=-1.0 if masked else 1.0, accum_out=rowsum[:, step:step + 1])
                            done.then_inc(p_ready.sem, 1)
                        u = step - 5
                        if closes_group(u) and not masked:
                            g = u // GS
                            eng.wait_ge(av_done.sem, av_done.at(b, (g + 1) * QT))
                            if g == 0:
                                if out_made.due(b - 1, QT):
                                    eng.wait_ge(out_made.sem, out_made.at(b - 1, QT))
                            eng.activation(onorm[:, g, :], OB[g % 2][:, :], ACT.Copy).then_inc(on_ready.sem, 1)
                        if step == U + 5 and more:
                            values(b + 1)
                        u = step - 7
                        if closes_group(u) and masked:
                            g = u // GS
                            eng.wait_ge(rb_made.sem, rb_made.at(b, g + 1))
                            if on_ready.due(b if g >= 1 else b - 1, g if g >= 1 else A.groups):
                                eng.wait_ge(on_ready.sem, on_ready.at(b if g >= 1 else b - 1, g if g >= 1 else A.groups))
                            eng.activation(rbs, MB[1][:, :], ACT.Copy).then_inc(rb_copied.sem, 1)

                turns(eng, turn)

            @block.vector
            def _(eng):
                def turn_x(b):
                    for c in range(KC):
                        eng.wait_ge(xt_made.sem, xt_made.at(b, c + 1))
                        if masked:
                            eng.tensor_copy(xnT[:, c, :], MB[c][:, :]).then_inc(xt_ready.sem, 1)
                        else:
                            eng.tensor_scalar(xnT[:, c, :], MB[c][:, :], m["cols"][:, 4 + c:5 + c],
                                              m["cols"][:, 6 + c:7 + c], ALU.mult, ALU.add).then_inc(xt_ready.sem, 1)

                def take_bias(b):
                    eng.wait_ge(bias_step.sem, bias_step.at(b, 5))
                    eng.tensor_copy(rows, rnext).then_inc(bias_ready.sem, 1)

                def take_bias_tiles(b):
                    eng.wait_ge(bias_step.sem, bias_step.at(b, 5 + 4 * QT))
                    eng.tensor_copy(bneg, bnext).then_inc(bias_ready.sem, 1)

                def take_qk(b, t):
                    if t == 0 and masked:
                        take_bias(b)
                        eng.wait_ge(bias_ready.sem, bias_ready.at(b, 1))
                    eng.wait_ge(qk_made.sem, qk_made.at(b, 2 * t + 1))
                    if masked:
                        if split_step.due(b if t else b - 1, 10 * (t if t else T)):
                            eng.wait_ge(split_step.sem, split_step.at(b if t else b - 1, 10 * (t if t else T)))
                    else:
                        if s_made.due(b if t >= 2 else b - 1, (t - 1) * A.tile_units + (0 if t >= 2 else U)):
                            eng.wait_ge(s_made.sem, s_made.at(b if t >= 2 else b - 1, (t - 1) * A.tile_units + (0 if t >= 2 else U)))
                    if masked:
                        eng.scalar_tensor_tensor(out=qT[:, 0, :], in0=MB[0][:, :],
                                                 scalar=m["cols"][:, t:t + 1], in1=rows[:, 1, :],
                                                 op0=ALU.add, op1=ALU.mult).then_inc(q_ready.sem, 1)
                    else:
                        eng.tensor_scalar(qT[:, t % 2, :], MB[0][:, :], A.dk ** -0.5, None, ALU.mult
                                          ).then_inc(q_ready.sem, 1)
                    eng.wait_ge(qk_made.sem, qk_made.at(b, 2 * t + 2))
                    if not masked:
                        if kz_ready.due(b if t >= 1 else b - 1, t if t >= 1 else T):
                            eng.wait_ge(kz_ready.sem, kz_ready.at(b if t >= 1 else b - 1, t if t >= 1 else T))
                    if masked:
                        eng.scalar_tensor_tensor(out=kT, in0=MB[1][:, :], scalar=m["cols"][:, 2 + t:3 + t],
                                                 in1=rows[:, 0, :], op0=ALU.add, op1=ALU.mult).then_inc(k_ready.sem, 1)
                    else:
                        eng.tensor_copy(kT, MB[1][:, :]).then_inc(k_ready.sem, 1)

                def values(b):
                    if masked:
                        for n, (kt, c) in enumerate(VCHUNKS):
                            eng.wait_ge(v_made.sem, v_made.at(b, n + 1))
                            eng.tensor_tensor(vtok[:, kt, :], SB[n % 2][:, 0:VW], v["A.bv"], ALU.add
                                              ).then_inc(v_ready.sem, 1)

                eng.wait_ge(s["x_first_loaded"], 16)
                eng.wait_ge(s["scalars_ready"], 2)
                eng.wait_ge(s["identity_made"], 8)
                if masked:
                    for k in OB:
                        eng.memset(k[:, :], 0.0).then_inc(cleared, 1)
                norm.all_parts(eng, 0, norm.on_vector)
                if masked:
                    eng.wait_ge(s["wa_loaded"], 16 * 9)
                else:
                    eng.wait_ge(bo_loaded, 16)
                turn_x(0)
                take_qk(0, 0)
                if masked:
                    split(eng, 0, 0)
                values(0)
                if masked:
                    for t in range(QT):
                        fold_bias(eng, 0, t)
                eng.wait_ge(s["x_loaded"], 16)

                def turn(b, more):
                    if masked:
                        take_bias_tiles(b)
                    for step in range(STEPS):
                        if more:
                            for part in norm_parts(step):
                                norm.on_vector(eng, b + 1, part)
                            if step == TURN:
                                turn_x(b + 1)
                        each_tile(step, b, more, take_qk)
                        u = step - 1
                        if 0 <= u < U and not masked:
                            eng.wait_ge(p_ready.sem, p_ready.at(b, u + 1))
                            if u == 0:
                                if normed.due(b - 1, U):
                                    eng.wait_ge(normed.sem, normed.at(b - 1, U))
                            eng.reciprocal(rinv[:, u:u + 1], rowsum[:, u:u + 1]).then_inc(rinv_ready.sem, 1)
                            eng.wait_ge(rinv_ready.sem, rinv_ready.at(b, u + 1))
                            eng.tensor_scalar(prob[:, u % NS, :], prob[:, u % NS, :], rinv[:, u:u + 1], None, ALU.mult
                                              ).then_inc(normed.sem, 1)
                        if step < U:
                            g, qt, j, h = A.unit(step)
                            eng.wait_ge(s_made.sem, s_made.at(b, step + 1))
                            if masked:
                                if step == 0:
                                    eng.wait_ge(bias_ready.sem, bias_ready.at(b, 2))
                                if step >= NS:
                                    eng.wait_ge(p_ready.sem, p_ready.at(b, step - NS + 1))
                                else:
                                    if p_ready.due(b - 1, U):
                                        eng.wait_ge(p_ready.sem, p_ready.at(b - 1, U))
                                apart(eng, m)
                                eng.tensor_tensor_reduce(sneg[:, step % NS, :], SB[step % 2][:, :], bneg[:, qt, :],
                                                         1.0, 3.0e38, ALU.add, ALU.min, low[:, step:step + 1]
                                                         ).then_inc(low_ready.sem, 1)
                            else:
                                if step == 0:
                                    if p_ready.due(b - 1, U):
                                        eng.wait_ge(p_ready.sem, p_ready.at(b - 1, U))
                                eng.tensor_reduce(low[:, step:step + 1], SB[step % 2][:, :], AX.X, ALU.max,
                                                  negate=True).then_inc(low_ready.sem, 1)
                        u = step - 2
                        if 0 <= u < U and u % 2 == 0:
                            eng.wait_ge(t_made.sem, t_made.at(b, u + 1))
                            if u >= PTR:
                                eng.wait_ge(av_done.sem, av_done.at(b, u // A.group - 1))
                            else:
                                if av_done.due(b - 1, A.groups * QT):
                                    eng.wait_ge(av_done.sem, av_done.at(b - 1, A.groups * QT))
                            eng.tensor_copy(pT[:, u % PTR, :], TB[u % 2][:, :]).then_inc(pt_even.sem, 1)
                        u = step - 4
                        if closes_group(u) and masked:
                            g = u // GS
                            eng.wait_ge(p_ready.sem, p_ready.at(b, (g + 1) * GS))
                            if rmat_ready.due(b - 1, A.groups):
                                eng.wait_ge(rmat_ready.sem, rmat_ready.at(b - 1, A.groups))
                            eng.reciprocal(rinv[:, g * GS:(g + 1) * GS], rowsum[:, g * GS:(g + 1) * GS]
                                           ).then_inc(rinv_ready.sem, 1)
                            spread_sums(eng, b, g)
                        if step == U + 4 and more:
                            values(b + 1)
                        u = step - 8
                        if closes_group(u) and masked:
                            g = u // GS
                            eng.wait_ge(rb_copied.sem, rb_copied.at(b, g + 1))
                            eng.wait_ge(av_done.sem, av_done.at(b, (g + 1) * QT))
                            eng.tensor_tensor(onorm[:, g, :], OB[g % 2][:, :], rbs, ALU.mult).then_inc(on_ready.sem, 1)
                    for t in range(QT):
                        eng.wait_ge(out_made.sem, out_made.at(b, t + 1))
                        eng.tensor_tensor(y[:, t % 2, :], MB[t % 2][:, 0:D], v["A.bo"] if masked else bo, ALU.add
                                          ).then_inc(y_ready.sem, 1)
                        eng.wait_ge(y_ready.sem, y_ready.at(b, t + 1))
                        xt = x[:, b * QT + t, :]
                        eng.scalar_tensor_tensor(out=xt, in0=y[:, t % 2, :], scalar=gate, in1=xt,
                                                 op0=ALU.mult, op1=ALU.add).then_inc(turn_done.sem, 1)

                turns(eng, turn)


def moe_attention(nc, a, m):
    A = B_
    s, v = m["s"], weight_views(m)
    bank, ident, x = m["bank"], m["ident"], m["x"]
    SB, TB, OB, MB = bank[0:2], bank[2:4], bank[4:6], bank[6:8]
    wq, wk, wgate = v["B.wq"], v["B.wk"], v["B.gate"]
    GS, U, T, DK = A.group_units, A.units, A.tiles, A.dk
    headmask, gate = m["cst"][:, 8:10], m["gates"][:, 2:3]
    take, wide = carve(m), carve(m, "wc")
    NS, PTR, NG = 3, 2 * A.group, 3
    w_val = carve(m, "big1")(KC, HB * EB * DK)
    w_out = carve(m, "big2")(HB * EB // 2, D)
    vtok, otok = wide(QT, A.width), wide(QT, A.width)
    xstage, xnT = take(QT, D), take(KC, S)
    qT, kT, kz = take(2, S), take(S), take(2 * A.per_tile, S)
    prob, sneg, pT = take(NS, S), take(NS, S), take(PTR, QT * P)
    low, rowsum, rinv = take(U), take(U), take(U)
    oT = take(S)
    gates, hit, gm, gmr = (take(QT * HB, EB) for _ in range(4))
    best, rev = take(QT * HB), take(EB)
    scaled, spread, spreadT = take(NG, EB * DK), take(NG, EB * DK), take(NG, EB * DK)
    cneg = take(S)
    VU = QT * HB
    VALUES = [(h, t) for h in range(HB) for t in range(QT)]

    with ExitStack() as ctx:
        def sig(what, per):
            return Signal(nc, ctx, f"B_{what}", per)

        turn_done = sig("x_updated", QT)
        val_loaded = [ctx.enter_context(nc.semaphore(f"B_val_loaded_{h}")) for h in range(HB)]
        out_loaded = ctx.enter_context(nc.semaphore("B_out_loaded"))
        consts = ctx.enter_context(nc.semaphore("B_consts_made"))
        xt_made, xt_ready = sig("xn_transposed", KC), sig("xnT_ready", KC)
        gate_made, gate_ready, pick = sig("gate_made", 1), sig("gate_ready", 1), sig("pick_step", 6)
        val_made, val_scaled, v_ready = sig("val_made", VU), sig("val_scaled", VU), sig("v_ready", VU)
        qk_made, q_ready, k_ready = sig("qk_made", 2 * T), sig("q_ready", T), sig("k_ready", T)
        kz_ready = sig("kz_ready", T)
        s_made, low_ready, p_ready = sig("scores_made", U), sig("low_ready", U), sig("probs_ready", U)
        t_made = sig("probs_transposed", U)
        pt_even, pt_odd = sig("pT_even_ready", U // 2), sig("pT_odd_ready", U // 2)
        av_done, rinv_ready, gmr_ready = sig("av_done", A.groups * QT), sig("rinv_ready", A.groups), sig("gmr_ready", A.groups)
        ot_ready, heads_made, otok_ready = sig("oT_ready", A.groups), sig("heads_made", A.groups), sig("otok_ready", A.groups)
        sp_ready, spt_made, spt_ready = sig("spread_ready", VU), sig("spread_transposed", VU), sig("spreadT_ready", VU)
        sp_used = sig("spread_used", VU)
        norm = Norm(nc, ctx, m, "B", take, None, QT, xstage, (xt_made, KC))

        STEPS = U + 8
        TURN = U - 9

        def closes_pass(u):
            return 0 <= u < U and u % A.group == A.group - 1

        def closes_group(u):
            return 0 <= u < U and u % GS == GS - 1

        def tile_at(step):
            u = step + 5
            return u // A.tile_units if 5 < u <= U and u % A.tile_units == 0 else None

        def groups_before(step):
            return sum(closes_group(z - 7) for z in range(step))

        def tiles_until(step, more):
            return 1 + sum(tile_at(z) is not None and (more or tile_at(z) < T) for z in range(step + 1))

        def norm_parts(step):
            first = TURN - 3 - norm.parts
            return [step - first] if 0 <= step - first < norm.parts else []

        def each_tile(step, b, more, do):
            t = tile_at(step)
            if t is not None and t < T:
                do(b, t)
            elif t is not None and more:
                do(b + 1, 0)

        with nc.Block() as block:
            @block.sync
            def _(eng):
                for h in range(HB):
                    eng.dma_start(w_val[:, :, h * EB * DK:(h + 1) * EB * DK],
                                  a["B.val"].rearrange("(c p) n -> p c n", p=P)[:, :, h * EB * DK:(h + 1) * EB * DK]
                                  ).then_inc(val_loaded[h], 16)
                eng.dma_start(w_out, a["B.out"]).then_inc(out_loaded, 16)
                if "C" in m["phases"]:
                    if val_made.due(B - 1, VU):
                        eng.wait_ge(val_made.sem, val_made.at(B - 1, VU))
                    fetch_c(eng, a, m)

            @block.gpsimd
            def _(eng):
                eng.memset(cneg, 0.0).then_inc(consts, 1)
                eng.wait_ge(consts, 1)
                eng.affine_select(out=cneg, in_=cneg, compare_op=ALU.is_ge, fill=CAUSAL, base=S - P,
                                  pattern=[[-1, S]], channel_multiplier=1).then_inc(consts, 1)
                eng.iota(rev, pattern=[[-1, EB]], base=EB, channel_multiplier=0,
                         allow_small_or_imprecise_dtypes=True).then_inc(consts, 1)

                def spread_heads(b, t):
                    eng.wait_ge(k_ready.sem, k_ready.at(b, t + 1))
                    if s_made.due(b if t >= 2 else b - 1, (t - 1) * A.tile_units + (0 if t >= 2 else U)):
                        eng.wait_ge(s_made.sem, s_made.at(b if t >= 2 else b - 1, (t - 1) * A.tile_units + (0 if t >= 2 else U)))
                    apart(eng, m)
                    for j in range(A.per_tile):
                        last = eng.tensor_scalar(kz[:, (t % 2) * A.per_tile + j, :], kT, headmask[:, j:j + 1],
                                                 None, ALU.mult)
                    last.then_inc(kz_ready.sem, 1)

                spread_heads(0, 0)

                def turn(b, more):
                    for step in range(STEPS):
                        each_tile(step, b, more, spread_heads)

                turns(eng, turn)

            @block.tensor
            def _(eng):
                def turn_x(b):
                    eng.wait_ge(norm.done.sem, norm.done.at(b, norm.done.per))
                    if k_ready.due(b - 1, T):
                        eng.wait_ge(k_ready.sem, k_ready.at(b - 1, T))
                    if otok_ready.due(b - 1, groups_before(TURN)):
                        eng.wait_ge(otok_ready.sem, otok_ready.at(b - 1, groups_before(TURN)))
                    for c in range(KC):
                        for t in range(QT):
                            last = eng.transpose(MB[c][:, t * P:(t + 1) * P], xstage[:, t, c * P:(c + 1) * P], ident[:, :])
                        last.then_inc(xt_made.sem, 1)

                def project(b, t, step):
                    if t == 0:
                        eng.wait_ge(xt_ready.sem, xt_ready.at(b, KC))
                    else:
                        eng.wait_ge(k_ready.sem, k_ready.at(b, t))
                        if groups_before(step):
                            eng.wait_ge(otok_ready.sem, otok_ready.at(b, groups_before(step)))
                        else:
                            if otok_ready.due(b - 1, A.groups):
                                eng.wait_ge(otok_ready.sem, otok_ready.at(b - 1, A.groups))
                    for kc in range(KC):
                        last = eng.matmul(MB[0][:, :], wq[:, kc, t * P:(t + 1) * P], xnT[:, kc, :],
                                          start=(kc == 0), stop=(kc == KC - 1))
                    last.then_inc(qk_made.sem, 1)
                    for kc in range(KC):
                        last = eng.matmul(MB[1][:, :], wk[:, kc, t * P:(t + 1) * P], xnT[:, kc, :],
                                          start=(kc == 0), stop=(kc == KC - 1))
                    last.then_inc(qk_made.sem, 1)

                def gate_logits(b):
                    if ot_ready.due(b - 1, A.groups - 1):
                        eng.wait_ge(ot_ready.sem, ot_ready.at(b - 1, A.groups - 1))
                    eng.wait_ge(xt_ready.sem, xt_ready.at(b, KC))
                    for t in range(QT):
                        for kc in range(KC):
                            last = eng.matmul(OB[0][:, t * 64:(t + 1) * 64], xnT[:, kc, t * P:(t + 1) * P],
                                              wgate[:, kc, :], start=(kc == 0), stop=(kc == KC - 1))
                    last.then_inc(gate_made.sem, 1)

                def values(b):
                    for n, (h, t) in enumerate(VALUES):
                        if n >= 2:
                            eng.wait_ge(val_scaled.sem, val_scaled.at(b, n - 1))
                        else:
                            if low_ready.due(b - 1, U):
                                eng.wait_ge(low_ready.sem, low_ready.at(b - 1, U))
                        if isinstance(b, int) and b == 0 and t == 0:
                            eng.wait_ge(val_loaded[h], 16)
                        for kc in range(KC):
                            last = eng.matmul(SB[n % 2][:, :], xnT[:, kc, t * P:(t + 1) * P],
                                              w_val[:, kc, h * EB * DK:(h + 1) * EB * DK],
                                              start=(kc == 0), stop=(kc == KC - 1))
                        last.then_inc(val_made.sem, 1)

                eng.wait_ge(s["wb_loaded"], 48)
                turn_x(0)
                gate_logits(0)
                project(0, 0, 0)
                values(0)

                def turn(b, more):
                    for step in range(STEPS):
                        if step == TURN and more:
                            turn_x(b + 1)
                        each_tile(step, b, more, lambda b, t: project(b, t, step))
                        if step < U:
                            g, qt, j, h = A.unit(step)
                            tl, hj = divmod(h, A.per_tile)
                            L = P * A.keys(qt)
                            if A.first_of_tile(step):
                                eng.wait_ge(kz_ready.sem, kz_ready.at(b, tl + 1))
                                eng.wait_ge(q_ready.sem, q_ready.at(b, tl + 1))
                            if step >= 2:
                                eng.wait_ge(low_ready.sem, low_ready.at(b, step - 1))
                            else:
                                eng.wait_ge(val_scaled.sem, val_scaled.at(b, VU))
                            eng.matmul(SB[step % 2][:, 0:L], qT[:, tl % 2, qt * P:(qt + 1) * P],
                                       kz[:, (tl % 2) * A.per_tile + hj, 0:L], start=True, stop=True
                                       ).then_inc(s_made.sem, 1)
                        u = step - 2
                        if 0 <= u < U:
                            qt = A.unit(u)[1]
                            eng.wait_ge(p_ready.sem, p_ready.at(b, u + 1))
                            if u >= 2:
                                eng.wait_ge((pt_even if u % 2 == 0 else pt_odd).sem, (pt_even if u % 2 == 0 else pt_odd).at(b, u // 2))
                            else:
                                if spt_ready.due(b - 1, VU):
                                    eng.wait_ge(spt_ready.sem, spt_ready.at(b - 1, VU))
                            for kt in range(A.keys(qt)):
                                last = eng.transpose(TB[u % 2][:, kt * P:(kt + 1) * P],
                                                     prob[:, u % NS, kt * P:(kt + 1) * P], ident[:, :])
                            last.then_inc(t_made.sem, 1)
                        u = step - 4
                        if closes_pass(u):
                            g, qt, _, _ = A.unit(u)
                            eng.wait_ge(pt_even.sem, pt_even.at(b, (u + 1) // 2))
                            eng.wait_ge(pt_odd.sem, pt_odd.at(b, (u + 1) // 2))
                            if u < A.group:
                                eng.wait_ge(v_ready.sem, v_ready.at(b, VU))
                            if A.opens_group(u) and g >= 2:
                                eng.wait_ge(ot_ready.sem, ot_ready.at(b, g - 1))
                            elif A.opens_group(u):
                                if turn_done.due(b - 1, QT):
                                    eng.wait_ge(turn_done.sem, turn_done.at(b - 1, QT))
                            for kt in range(A.keys(qt)):
                                for j in range(A.group):
                                    h = g * A.group + j
                                    r = A.strip * j
                                    last = eng.matmul(OB[g % 2][r:r + DK, qt * P:(qt + 1) * P],
                                                      vtok[:, kt, h * DK:(h + 1) * DK],
                                                      pT[:, (u - A.group + 1 + j) % PTR, kt * P:(kt + 1) * P],
                                                      start=(kt == 0), stop=(kt == A.keys(qt) - 1))
                            last.then_inc(av_done.sem, 1)
                        if step == U + 4 and more:
                            gate_logits(b + 1)
                        u = step - 7
                        if closes_group(u):
                            g = u // GS
                            eng.wait_ge(ot_ready.sem, ot_ready.at(b, g + 1))
                            eng.wait_ge(k_ready.sem, k_ready.at(b, tiles_until(step, more)))
                            if g >= 1:
                                eng.wait_ge(otok_ready.sem, otok_ready.at(b, g))
                            for qt in range(QT):
                                last = eng.transpose(MB[1][:, qt * P:(qt + 1) * P], oT[:, qt * P:(qt + 1) * P], ident[:, :])
                            last.then_inc(heads_made.sem, 1)
                    if more:
                        values(b + 1)
                        eng.wait_ge(gate_ready.sem, gate_ready.at(b + 1, 1))
                    eng.wait_ge(otok_ready.sem, otok_ready.at(b, A.groups))
                    eng.wait_ge(out_loaded, 16)
                    for n in range(VU + 2):
                        if n < VU:
                            eng.wait_ge(sp_ready.sem, sp_ready.at(b, n + 1))
                            if n >= 2:
                                eng.wait_ge(spt_ready.sem, spt_ready.at(b, n - 1))
                            for c in range(4):
                                last = eng.transpose(TB[n % 2][:, c * P:(c + 1) * P],
                                                     spread[:, n % NG, c * P:(c + 1) * P], ident[:, :])
                            last.then_inc(spt_made.sem, 1)
                        w = n - 2
                        if w >= 0:
                            qt, h = divmod(w, HB)
                            eng.wait_ge(spt_ready.sem, spt_ready.at(b, w + 1))
                            if qt >= 2 and h == 0:
                                eng.wait_ge(turn_done.sem, turn_done.at(b, qt - 1))
                            for c in range(4):
                                last = eng.matmul(OB[qt % 2][:, 0:D], spreadT[:, w % NG, c * P:(c + 1) * P],
                                                  w_out[:, h * 4 + c, :], start=(h == 0 and c == 0),
                                                  stop=(h == HB - 1 and c == 3))
                            last.then_inc(sp_used.sem, 1)

                turns(eng, turn)

            @block.scalar
            def _(eng):
                def squash_gates(b):
                    eng.wait_ge(gate_made.sem, gate_made.at(b, 1))
                    if pick.due(b - 1, 6):
                        eng.wait_ge(pick.sem, pick.at(b - 1, 6))
                    eng.activation(gates, OB[0][:, 0:QT * 64].rearrange("p (a e) -> p a e", e=EB), ACT.Sigmoid
                                   ).then_inc(gate_ready.sem, 1)

                norm.all_parts(eng, 0, norm.on_scalar)
                squash_gates(0)

                def turn(b, more):
                    for step in range(STEPS):
                        if more:
                            for part in norm_parts(step):
                                norm.on_scalar(eng, b + 1, part)
                        u = step - 2
                        if 0 <= u < U and u % 2 == 1:
                            L = P * A.keys(A.unit(u)[1])
                            eng.wait_ge(t_made.sem, t_made.at(b, u + 1))
                            if u >= PTR:
                                eng.wait_ge(av_done.sem, av_done.at(b, u // A.group - 1))
                            else:
                                if av_done.due(b - 1, A.groups * QT):
                                    eng.wait_ge(av_done.sem, av_done.at(b - 1, A.groups * QT))
                            eng.activation(pT[:, u % PTR, 0:L], TB[u % 2][:, 0:L], ACT.Copy).then_inc(pt_odd.sem, 1)
                        if step < U:
                            L, col = P * A.keys(A.unit(step)[1]), A.column(step)
                            if step == 0:
                                if rinv_ready.due(b - 1, A.groups):
                                    eng.wait_ge(rinv_ready.sem, rinv_ready.at(b - 1, A.groups))
                            eng.wait_ge(low_ready.sem, low_ready.at(b, step + 1))
                            if step >= NS:
                                eng.wait_ge(t_made.sem, t_made.at(b, step - NS + 1))
                            else:
                                if t_made.due(b - 1, U):
                                    eng.wait_ge(t_made.sem, t_made.at(b - 1, U))
                            eng.activation(prob[:, step % NS, 0:L], sneg[:, step % NS, 0:L], ACT.Exp,
                                           bias=low[:, col:col + 1], scale=-1.0,
                                           accum_out=rowsum[:, col:col + 1]).then_inc(p_ready.sem, 1)
                        u = step - 5
                        if closes_group(u):
                            g = u // GS
                            eng.wait_ge(av_done.sem, av_done.at(b, (g + 1) * QT))
                            if heads_made.due(b if g >= 1 else b - 1, g if g >= 1 else A.groups):
                                eng.wait_ge(heads_made.sem, heads_made.at(b if g >= 1 else b - 1, g if g >= 1 else A.groups))
                            eng.activation(oT, OB[g % 2][:, :], ACT.Copy).then_inc(ot_ready.sem, 1)
                    if more:
                        squash_gates(b + 1)
                    for n in range(VU):
                        eng.wait_ge(spt_made.sem, spt_made.at(b, n + 1))
                        if n >= NG:
                            eng.wait_ge(sp_used.sem, sp_used.at(b, n - NG + 1))
                        else:
                            if sp_used.due(b - 1, VU):
                                eng.wait_ge(sp_used.sem, sp_used.at(b - 1, VU))
                        eng.activation(spreadT[:, n % NG, :], TB[n % 2][:, :], ACT.Copy).then_inc(spt_ready.sem, 1)

                turns(eng, turn)

            @block.vector
            def _(eng):
                def turn_x(b):
                    for c in range(KC):
                        eng.wait_ge(xt_made.sem, xt_made.at(b, c + 1))
                        eng.tensor_copy(xnT[:, c, :], MB[c][:, :]).then_inc(xt_ready.sem, 1)

                def take_qk(b, t):
                    eng.wait_ge(qk_made.sem, qk_made.at(b, 2 * t + 1))
                    if s_made.due(b if t >= 2 else b - 1, (t - 1) * A.tile_units + (0 if t >= 2 else U)):
                        eng.wait_ge(s_made.sem, s_made.at(b if t >= 2 else b - 1, (t - 1) * A.tile_units + (0 if t >= 2 else U)))
                    eng.tensor_scalar(qT[:, t % 2, :], MB[0][:, :], -(DK ** -0.5), None, ALU.mult).then_inc(q_ready.sem, 1)
                    eng.wait_ge(qk_made.sem, qk_made.at(b, 2 * t + 2))
                    if kz_ready.due(b if t >= 1 else b - 1, t if t >= 1 else T):
                        eng.wait_ge(kz_ready.sem, kz_ready.at(b if t >= 1 else b - 1, t if t >= 1 else T))
                    eng.tensor_copy(kT, MB[1][:, :]).then_inc(k_ready.sem, 1)

                def pick_experts(b):
                    wide_best = best.unsqueeze(2).to_broadcast([P, VU, EB])
                    wide_rev = rev.unsqueeze(1).to_broadcast([P, VU, EB])
                    eng.wait_ge(gate_ready.sem, gate_ready.at(b, 1))
                    if gmr_ready.due(b - 1, A.groups):
                        eng.wait_ge(gmr_ready.sem, gmr_ready.at(b - 1, A.groups))
                    eng.tensor_reduce(best, gates, AX.X, ALU.max).then_inc(pick.sem, 1)
                    eng.wait_ge(pick.sem, pick.at(b, 1))
                    eng.tensor_tensor(hit, gates, wide_best, ALU.is_equal).then_inc(pick.sem, 1)
                    eng.wait_ge(pick.sem, pick.at(b, 2))
                    eng.tensor_tensor(gm, hit, wide_rev, ALU.mult).then_inc(pick.sem, 1)
                    eng.wait_ge(pick.sem, pick.at(b, 3))
                    eng.tensor_reduce(best, gm, AX.X, ALU.max).then_inc(pick.sem, 1)
                    eng.wait_ge(pick.sem, pick.at(b, 4))
                    eng.tensor_tensor(hit, gm, wide_best, ALU.is_equal).then_inc(pick.sem, 1)
                    eng.wait_ge(pick.sem, pick.at(b, 5))
                    eng.tensor_tensor(gm, hit, gates, ALU.mult).then_inc(pick.sem, 1)
                    eng.wait_ge(pick.sem, pick.at(b, 6))

                def values(b):
                    for n in range(VU + 1):
                        if n < VU:
                            h, t = VALUES[n]
                            eng.wait_ge(val_made.sem, val_made.at(b, n + 1))
                            if n >= NG:
                                eng.wait_ge(v_ready.sem, v_ready.at(b, n - NG + 1))
                            else:
                                if v_ready.due(b - 1, VU):
                                    eng.wait_ge(v_ready.sem, v_ready.at(b - 1, VU))
                            eng.tensor_tensor(scaled[:, n % NG, :].rearrange("p (e k) -> p e k", e=EB),
                                              SB[n % 2][:, :].rearrange("p (e k) -> p e k", e=EB),
                                              gm[:, t * HB + h, :].unsqueeze(2).to_broadcast([P, EB, DK]), ALU.mult
                                              ).then_inc(val_scaled.sem, 1)
                        w = n - 1
                        if w >= 0:
                            h, t = VALUES[w]
                            eng.wait_ge(val_scaled.sem, val_scaled.at(b, w + 1))
                            eng.tensor_reduce(vtok[:, t, h * DK:(h + 1) * DK],
                                              scaled[:, w % NG, :].rearrange("p (e k) -> p k e", e=EB), AX.X, ALU.add
                                              ).then_inc(v_ready.sem, 1)

                eng.wait_ge(consts, 3)
                norm.all_parts(eng, 0, norm.on_vector)
                turn_x(0)
                pick_experts(0)
                take_qk(0, 0)
                values(0)

                def turn(b, more):
                    for step in range(STEPS):
                        if more:
                            for part in norm_parts(step):
                                norm.on_vector(eng, b + 1, part)
                            if step == TURN:
                                turn_x(b + 1)
                        each_tile(step, b, more, take_qk)
                        if step < U:
                            g, qt, j, h = A.unit(step)
                            L, col = P * A.keys(qt), A.column(step)
                            eng.wait_ge(s_made.sem, s_made.at(b, step + 1))
                            if step >= NS:
                                eng.wait_ge(p_ready.sem, p_ready.at(b, step - NS + 1))
                            else:
                                if p_ready.due(b - 1, U):
                                    eng.wait_ge(p_ready.sem, p_ready.at(b - 1, U))
                            apart(eng, m)
                            eng.tensor_tensor_reduce(sneg[:, step % NS, 0:L], SB[step % 2][:, 0:L], cneg[:, S - L:S],
                                                     1.0, 3.0e38, ALU.add, ALU.min, low[:, col:col + 1]
                                                     ).then_inc(low_ready.sem, 1)
                        u = step - 2
                        if 0 <= u < U and u % 2 == 0:
                            L = P * A.keys(A.unit(u)[1])
                            eng.wait_ge(t_made.sem, t_made.at(b, u + 1))
                            if u >= PTR:
                                eng.wait_ge(av_done.sem, av_done.at(b, u // A.group - 1))
                            else:
                                if av_done.due(b - 1, A.groups * QT):
                                    eng.wait_ge(av_done.sem, av_done.at(b - 1, A.groups * QT))
                            eng.tensor_copy(pT[:, u % PTR, 0:L], TB[u % 2][:, 0:L]).then_inc(pt_even.sem, 1)
                        u = step - 4
                        if closes_group(u):
                            g = u // GS
                            eng.wait_ge(p_ready.sem, p_ready.at(b, (g + 1) * GS))
                            eng.reciprocal(rinv[:, g * GS:(g + 1) * GS], rowsum[:, g * GS:(g + 1) * GS]
                                           ).then_inc(rinv_ready.sem, 1)
                            eng.wait_ge(rinv_ready.sem, rinv_ready.at(b, g + 1))

                            def of_group(z):
                                return z.rearrange("p (t h) e -> p t h e", h=HB)[:, :, 2 * g:2 * g + 2, :]

                            eng.tensor_tensor(of_group(gmr), of_group(gm),
                                              rinv[:, g * GS:(g + 1) * GS].rearrange("p (t j) -> p t j", j=2)
                                              .unsqueeze(3).to_broadcast([P, QT, 2, EB]), ALU.mult
                                              ).then_inc(gmr_ready.sem, 1)
                        u = step - 7
                        if closes_group(u):
                            g = u // GS
                            eng.wait_ge(heads_made.sem, heads_made.at(b, g + 1))
                            if sp_ready.due(b - 1, VU):
                                eng.wait_ge(sp_ready.sem, sp_ready.at(b - 1, VU))
                            eng.tensor_copy(otok[:, :, g * P:(g + 1) * P],
                                            MB[1][:, :].rearrange("p (t c) -> p t c", t=QT)).then_inc(otok_ready.sem, 1)
                    eng.wait_ge(gmr_ready.sem, gmr_ready.at(b, A.groups))
                    eng.wait_ge(otok_ready.sem, otok_ready.at(b, A.groups))
                    if more:
                        pick_experts(b + 1)
                        values(b + 1)
                    for n in range(VU + 3):
                        if n < VU:
                            qt, h = divmod(n, HB)
                            if n >= NG:
                                eng.wait_ge(spt_made.sem, spt_made.at(b, n - NG + 1))
                            else:
                                if spt_made.due(b - 1, VU):
                                    eng.wait_ge(spt_made.sem, spt_made.at(b - 1, VU))
                            eng.tensor_tensor(spread[:, n % NG, :].rearrange("p (e k) -> p e k", e=EB),
                                              otok[:, qt, h * DK:(h + 1) * DK].unsqueeze(1).to_broadcast([P, EB, DK]),
                                              gmr[:, n, :].unsqueeze(2).to_broadcast([P, EB, DK]), ALU.mult
                                              ).then_inc(sp_ready.sem, 1)
                        w = n - 3
                        if w >= 0 and w % HB == HB - 1:
                            qt = w // HB
                            eng.wait_ge(sp_used.sem, sp_used.at(b, w + 1))
                            xt = x[:, b * QT + qt, :]
                            eng.scalar_tensor_tensor(out=xt, in0=OB[qt % 2][:, 0:D], scalar=gate, in1=xt,
                                                     op0=ALU.mult, op1=ALU.add).then_inc(turn_done.sem, 1)

                turns(eng, turn)


def product_key_experts(nc, a, m):
    s = m["s"]
    bank, ident, x = m["bank"], m["ident"], m["x"]
    HP, WP, UPP, XP, SP = bank[0:2], bank[2:5], bank[5], bank[6], bank[7]
    take, wide = carve(m), carve(m, "wc")
    down = carve(m, "big1")(KC * ELO, EHI)
    wq, keysT, up = d_views(m)
    hot = wide(8192).bitcast(BF16).rearrange("p (m t) -> p m t", t=P)
    simw = take(KC, 2 * HD * NK)
    xstage, xnT = take(D), take(KC, P)
    sims = take(2 * HD, NK)
    Hg = take(ELO, P)
    G = carve(m, "wab")(ELO, P)
    elo = take(ELO * P // 2).bitcast(BF16).rearrange("p (j t) -> p j t", t=P)
    b12 = take(ELO * P // 2).bitcast(BF16).rearrange("p (j t) -> p j t", t=P)
    b3 = take(ELO * P // 2).bitcast(BF16).rearrange("p (j t) -> p j t", t=P)
    sel = take(4, P)
    selT = take(4 * P // 2).bitcast(BF16).rearrange("p (f t) -> p f t", t=P)
    top, topi = take(2 * HD, TOP), take(2 * HD, TOP).bitcast(U32)
    topf = take(2 * HD, TOP)
    pairs, eq = take(HD, TOP * TOP), take(HD * TOP, TOP)
    score, pk, pa, pb = take(HD, TOP), take(NSEL).bitcast(U32), take(NSEL).bitcast(U32), take(NSEL).bitcast(U32)
    paf, pbf, i1, i2, over = take(NSEL), take(NSEL), take(NSEL), take(NSEL), take(NSEL)
    part, rest = take(NSEL // 2).bitcast(BF16), take(NSEL)
    iota = take(TOP)
    NT, NJ = B * QT, 4
    gate = m["gates"][:, 3:4]
    TW = 16
    BJ = 4

    with ExitStack() as ctx:
        def sig(what, per):
            return Signal(nc, ctx, f"D_{what}", per)

        def sem(what):
            return ctx.enter_context(nc.semaphore("D_" + what))

        down_loaded = sem("down_loaded")
        fold_made, fold_ready, consts = sem("fold_made"), sem("fold_ready"), sem("consts")
        staged, xt_made, xt_ready = sig("staged", 1), sig("xn_transposed", 1), sig("xnT_ready", 1)
        sim_made, sim_ready = sig("sims_made", 2), sig("sims_ready", 2)
        STEPS = 52
        step = sig("pick_step", STEPS)
        selt_made, selt_ready = sig("sel_transposed", 1), sig("selT_ready", 1)
        h_made, h_ready = sig("hidden_made", ELO // NJ), sig("hidden_ready", ELO // NJ)
        hot_ready, elo_ready = sig("hot_ready", 1), sig("elo_ready", 1)
        b_ready, pool_b_ready = sig("b_ready", 1), sig("pool_b_ready", 2)
        w_made, g_ready = sig("weights_made", P // TW), sig("weighted", P // TW)
        up_made, turn_done = sig("up_made", 1), sig("x_updated", 1)
        norm = Norm(nc, ctx, m, "D", take, 1e-6, NT)

        def scored(eng, f, dst, j0, j1):
            return eng.tensor_tensor(dst[:, j0:j1, :], elo[:, j0:j1, :],
                                     selT[:, f, :].unsqueeze(1).to_broadcast([P, j1 - j0, P]), ALU.mult)

        def turns(eng, turn):
            turn(0, 2)
            with eng.Fori(1, NT - 2) as i:
                turn(i, 2)
            turn(NT - 2, 1)
            turn(NT - 1, 0)

        with nc.Block() as block:
            @block.sync
            def _(eng):
                if "d_fetched" not in m:
                    fetch_d(eng, a, m)
                eng.dma_start(down, a["D.downT"]).then_inc(down_loaded, 16)
                tiles = m["out"].rearrange("b (t p) d -> p (b t) d", p=P)
                for until in (QT, 2 * QT, 3 * QT, NT - 1):
                    first = m["stored_tiles"]
                    eng.wait_ge(turn_done.sem, turn_done.at(until - 1, 1))
                    eng.dma_start(tiles[:, first:until, :], x[:, first:until, :]).then_inc(s["stored"], 16)
                    m["stored_tiles"], m["stores"] = until, m["stores"] + 1

            @block.gpsimd
            def _(eng):
                eng.iota(iota, pattern=[[1, TOP]], base=0, channel_multiplier=0,
                         allow_small_or_imprecise_dtypes=True).then_inc(consts, 1)
                eng.memset(sel, 0.0).then_inc(consts, 1)

                def scores(i):
                    eng.wait_ge(elo_ready.sem, elo_ready.at(i, 1))
                    eng.wait_ge(selt_ready.sem, selt_ready.at(i, 1))
                    if w_made.due(i - 1, P // TW):
                        eng.wait_ge(w_made.sem, w_made.at(i - 1, P // TW))
                    scored(eng, 3, b3, 0, ELO).then_inc(pool_b_ready.sem, 1)
                    scored(eng, 2, b12, BJ, ELO).then_inc(pool_b_ready.sem, 1)

                scores(0)

                def turn(i, ahead):
                    if ahead >= 1:
                        scores(i + 1)

                turns(eng, turn)

            @block.tensor
            def _(eng):
                eng.wait_ge(s["dq_loaded"], 32)
                for n in range(4):
                    kc, c = divmod(n, 2)
                    for q in range(HD):
                        hc = c * HD + q
                        last = eng.matmul(bank[n][:, q * NK:(q + 1) * NK], wq[:, hc, kc * P:(kc + 1) * P],
                                          keysT[:, hc, :], start=True, stop=True)
                    last.then_inc(fold_made, 1)

                def select(i):
                    if h_ready.due(i - 1, ELO // NJ):
                        eng.wait_ge(h_ready.sem, h_ready.at(i - 1, ELO // NJ))
                    eng.wait_ge(staged.sem, staged.at(i, 1))
                    for c in range(KC):
                        last = eng.transpose(XP[:, c * P:(c + 1) * P], xstage[:, c * P:(c + 1) * P], ident[:, :])
                    last.then_inc(xt_made.sem, 1)
                    eng.wait_ge(xt_ready.sem, xt_ready.at(i, 1))
                    for n in range(2):
                        for kc in range(KC):
                            last = eng.matmul(HP[n][:, :], xnT[:, kc, :], simw[:, kc, n * 512:(n + 1) * 512],
                                              start=(kc == 0), stop=(kc == KC - 1))
                        last.then_inc(sim_made.sem, 1)

                def turn_picks(i):
                    eng.wait_ge(step.sem, step.at(i, STEPS))
                    if selt_ready.due(i - 1, 1):
                        eng.wait_ge(selt_ready.sem, selt_ready.at(i - 1, 1))
                    for f in range(4):
                        last = eng.transpose(SP[:, f * P:(f + 1) * P], sel[:, f, :], ident[:, :])
                    last.then_inc(selt_made.sem, 1)

                def hidden(i):
                    for n in range(ELO // NJ):
                        if n >= 2:
                            eng.wait_ge(h_ready.sem, h_ready.at(i, n - 1))
                        else:
                            eng.wait_ge(sim_ready.sem, sim_ready.at(i, 2))
                        for q in range(NJ):
                            for kc in range(KC):
                                last = eng.matmul(HP[n % 2][:, q * P:(q + 1) * P], down[:, kc * ELO + n * NJ + q, :],
                                                  xnT[:, kc, :], start=(kc == 0), stop=(kc == KC - 1))
                        last.then_inc(h_made.sem, 1)

                eng.wait_ge(fold_ready, 4)
                select(0)
                eng.wait_ge(down_loaded, 16)
                hidden(0)
                turn_picks(0)
                select(1)
                eng.wait_ge(s["up_loaded"], 16)

                def turn(i, ahead):
                    eng.wait_ge(hot_ready.sem, hot_ready.at(i, 1))
                    eng.wait_ge(b_ready.sem, b_ready.at(i, 1))
                    eng.wait_ge(pool_b_ready.sem, pool_b_ready.at(i, 2))
                    for n in range(P // TW):
                        if n >= 3:
                            eng.wait_ge(g_ready.sem, g_ready.at(i, n - 2))
                        for q in range(TW):
                            t = n * TW + q
                            dst = WP[n % 3][:, q * ELO:(q + 1) * ELO]
                            eng.matmul(dst, hot[:, :, t], b12[:, :, t], start=True, stop=False)
                            last = eng.matmul(dst, hot[:, :, t], b3[:, :, t], start=False, stop=True)
                        last.then_inc(w_made.sem, 1)
                    first = isinstance(i, int) and i == 0
                    if ahead >= 1 and not first:
                        turn_picks(i + 1)
                    if ahead >= 1:
                        hidden(i + 1)
                    if first:
                        turn_picks(i + 1)
                    if ahead >= 2:
                        select(i + 2)
                    eng.wait_ge(g_ready.sem, g_ready.at(i, P // TW))
                    if turn_done.due(i - 1, 1):
                        eng.wait_ge(turn_done.sem, turn_done.at(i - 1, 1))
                    for j in range(ELO):
                        last = eng.matmul(UPP[:, 0:D], G[:, j, :], up[:, j, :], start=(j == 0), stop=(j == ELO - 1))
                    last.then_inc(up_made.sem, 1)

                turns(eng, turn)

            @block.scalar
            def _(eng):
                norm.all_parts(eng, 0, norm.on_scalar)
                for n in range(4):
                    kc, c = divmod(n, 2)
                    eng.wait_ge(fold_made, n + 1)
                    eng.activation(simw[:, kc, c * 512:(c + 1) * 512], bank[n][:, :], ACT.Copy).then_inc(fold_ready, 1)
                eng.wait_ge(norm.done.sem, norm.done.at(0, norm.done.per))

                def stage(i):
                    if xt_made.due(i, 0):
                        eng.wait_ge(xt_made.sem, xt_made.at(i, 0))
                    eng.activation(xstage, x[:, i, :], ACT.Identity, scale=norm.rstd[:, bass.ds(i, 1)],
                                   bias=norm.shift[:, bass.ds(i, 1)]).then_inc(staged.sem, 1)

                def select(i):
                    eng.wait_ge(xt_made.sem, xt_made.at(i, 1))
                    for c in range(KC):
                        last = eng.activation(xnT[:, c, :], XP[:, c * P:(c + 1) * P], ACT.Copy,
                                              scale=m["cols"][:, 8 + c:9 + c])
                    last.then_inc(xt_ready.sem, 1)
                    for n in range(2):
                        eng.wait_ge(sim_made.sem, sim_made.at(i, n + 1))
                        if n == 0:
                            if step.due(i, 0):
                                eng.wait_ge(step.sem, step.at(i, 0))
                        eng.activation(sims[:, n * HD:(n + 1) * HD, :],
                                       HP[n][:, :].rearrange("p (a b) -> p a b", b=NK), ACT.Copy).then_inc(sim_ready.sem, 1)

                def picks(i):
                    eng.wait_ge(selt_made.sem, selt_made.at(i, 1))
                    if hot_ready.due(i - 1, 1):
                        eng.wait_ge(hot_ready.sem, hot_ready.at(i - 1, 1))
                    if b_ready.due(i - 1, 1):
                        eng.wait_ge(b_ready.sem, b_ready.at(i - 1, 1))
                    if pool_b_ready.due(i - 1, 2):
                        eng.wait_ge(pool_b_ready.sem, pool_b_ready.at(i - 1, 2))
                    eng.activation(selT, SP[:, :].rearrange("p (f t) -> p f t", t=P), ACT.Copy).then_inc(selt_ready.sem, 1)

                def hidden(i):
                    if g_ready.due(i - 1, P // TW):
                        eng.wait_ge(g_ready.sem, g_ready.at(i - 1, P // TW))
                    for n in range(ELO // NJ):
                        eng.wait_ge(h_made.sem, h_made.at(i, n + 1))
                        eng.activation(Hg[:, n * NJ:(n + 1) * NJ, :], HP[n % 2][:, :].rearrange("p (j t) -> p j t", t=P),
                                       ACT.Gelu).then_inc(h_ready.sem, 1)

                stage(0)
                select(0)
                stage(1)
                hidden(0)
                picks(0)
                select(1)

                def turn(i, ahead):
                    if ahead >= 2:
                        stage(i + 2)
                    first = isinstance(i, int) and i == 0
                    if ahead >= 1 and not first:
                        picks(i + 1)
                    if ahead >= 1:
                        hidden(i + 1)
                    if first:
                        picks(i + 1)
                    if ahead >= 2:
                        select(i + 2)

                turns(eng, turn)

            @block.vector
            def _(eng):
                eng.wait_ge(consts, 2)
                eng.wait_ge(s["x_first_loaded"], 16)
                eng.wait_ge(s["x_loaded"], 16)
                norm.all_parts(eng, 0, norm.on_vector)

                def topk(i):
                    n = [0]

                    def mark(ins):
                        ins.then_inc(step.sem, 1)
                        n[0] += 1

                    def reach():
                        eng.wait_ge(step.sem, step.at(i, n[0]))

                    eng.wait_ge(sim_ready.sem, sim_ready.at(i, 2))
                    apart(eng, m)
                    for hc in range(2 * HD):
                        mark(eng.max(top[:, hc, :], sims[:, hc, :]))
                    reach()
                    apart(eng, m)
                    for hc in range(2 * HD):
                        last = eng.max_index(topi[:, hc, :], top[:, hc, :], sims[:, hc, :])
                    mark(last)
                    halves = top.rearrange("p (h c) k -> p h c k", c=2)
                    mark(eng.tensor_tensor(pairs.rearrange("p h (a b) -> p h a b", b=TOP),
                                           halves[:, :, 0, :].unsqueeze(3).to_broadcast([P, HD, TOP, TOP]),
                                           halves[:, :, 1, :].unsqueeze(2).to_broadcast([P, HD, TOP, TOP]), ALU.add))
                    reach()
                    apart(eng, m)
                    for h in range(HD):
                        mark(eng.max(score[:, h, :], pairs[:, h, :]))
                    mark(eng.tensor_copy(topf, topi))
                    reach()
                    apart(eng, m)
                    for h in range(HD):
                        last = eng.max_index(pk[:, h * TOP:(h + 1) * TOP], score[:, h, :], pairs[:, h, :])
                    mark(last)
                    reach()
                    mark(eng.tensor_scalar(pa, pk, 3, None, ALU.logical_shift_right))
                    mark(eng.tensor_scalar(pb, pk, TOP - 1, None, ALU.bitwise_and))
                    reach()
                    mark(eng.tensor_copy(paf, pa))
                    mark(eng.tensor_copy(pbf, pb))
                    reach()
                    numbers = topf.rearrange("p (h c) k -> p h c k", c=2)
                    for c, place, key in ((0, paf, i1), (1, pbf, i2)):
                        mark(eng.tensor_tensor(eq, place.unsqueeze(2).to_broadcast([P, NSEL, TOP]),
                                               iota.unsqueeze(1).to_broadcast([P, NSEL, TOP]), ALU.is_equal))
                        reach()
                        e4 = eq.rearrange("p (h k) a -> p h k a", k=TOP)
                        mark(eng.tensor_tensor(e4, e4, numbers[:, :, c, :].unsqueeze(2).to_broadcast([P, HD, TOP, TOP]),
                                               ALU.mult))
                        reach()
                        mark(eng.tensor_reduce(key, eq, AX.X, ALU.add))
                        reach()
                    mark(eng.tensor_scalar(over, i2, float(ELO), None, ALU.is_ge))
                    reach()
                    if selt_made.due(i, 0):
                        eng.wait_ge(selt_made.sem, selt_made.at(i, 0))
                    for d in range(2):
                        mark(eng.scalar_tensor_tensor(out=sel[:, 0, d * NSEL:(d + 1) * NSEL], in0=i1, scalar=2.0, in1=over,
                                                      op0=ALU.mult, op1=ALU.add))
                        mark(eng.scalar_tensor_tensor(out=sel[:, 1, d * NSEL:(d + 1) * NSEL], in0=over,
                                                      scalar=-float(ELO), in1=i2, op0=ALU.mult, op1=ALU.add))
                    flat = score.rearrange("p h k -> p (h k)")
                    mark(eng.tensor_scalar(rest, flat, 0.0, None, ALU.max))
                    reach()
                    for q in range(3):
                        dst = sel[:, 2, q * NSEL:(q + 1) * NSEL] if q < 2 else sel[:, 3, 0:NSEL]
                        mark(eng.tensor_copy(part, rest))
                        reach()
                        mark(eng.tensor_copy(dst, part))
                        if q < 2:
                            mark(eng.tensor_tensor(rest, rest, part, ALU.subtract))
                            reach()
                    assert n[0] == STEPS, n[0]

                def onehots(i):
                    eng.wait_ge(selt_ready.sem, selt_ready.at(i, 1))
                    if pool_b_ready.due(i - 1, 2):
                        eng.wait_ge(pool_b_ready.sem, pool_b_ready.at(i - 1, 2))
                    for j in range(ELO):
                        last = eng.tensor_scalar(elo[:, j, :], selT[:, 1, :], float(j), None, ALU.is_equal)
                    last.then_inc(elo_ready.sem, 1)
                    for mm in range(EHI):
                        last = eng.tensor_scalar(hot[:, mm, :], selT[:, 0, :], float(mm), None, ALU.is_equal)
                    last.then_inc(hot_ready.sem, 1)
                    eng.wait_ge(elo_ready.sem, elo_ready.at(i, 1))
                    scored(eng, 2, b12, 0, BJ).then_inc(b_ready.sem, 1)

                def update(i):
                    eng.wait_ge(up_made.sem, up_made.at(i, 1))
                    xt = x[:, i, :]
                    eng.scalar_tensor_tensor(out=xt, in0=UPP[:, 0:D], scalar=gate, in1=xt, op0=ALU.mult, op1=ALU.add
                                             ).then_inc(turn_done.sem, 1)

                topk(0)
                onehots(0)

                def turn(i, ahead):
                    eng.wait_ge(h_ready.sem, h_ready.at(i, ELO // NJ))
                    for n in range(P // TW):
                        eng.wait_ge(w_made.sem, w_made.at(i, n + 1))
                        if n == 0:
                            if up_made.due(i - 1, 1):
                                eng.wait_ge(up_made.sem, up_made.at(i - 1, 1))
                        eng.tensor_tensor(G[:, :, n * TW:(n + 1) * TW],
                                          WP[n % 3][:, :].rearrange("p (t j) -> p j t", j=ELO),
                                          Hg[:, :, n * TW:(n + 1) * TW], ALU.mult).then_inc(g_ready.sem, 1)
                    if isinstance(i, int) and i == 0:
                        topk(1)
                    else:
                        update(i - 1)
                    if ahead >= 1:
                        onehots(i + 1)
                    if ahead >= 2:
                        topk(i + 2)

                turns(eng, turn)
                update(NT - 1)


def layouts(i):
    c = np.ascontiguousarray
    r = {"x": c(i["x"]), "bias": c(i["fside_BxSxS2_0"]), "mask": c(i["mask_BxS2_ik0"])}
    r["ctxT"] = c(np.transpose(i["ctx_1024"], (2, 0, 1)).reshape(D, B * S))
    for n, k in (("A.wqT", "WQ"), ("A.wkT", "WK"), ("A.wvT", "WV"), ("A.woT", "WO")):
        r[n] = c(i[f"L0_xattn_{k}_w"].T)
    r["B.val"] = c(i["L0_ffn_value_experts"].transpose(2, 1, 0, 3).reshape(D, -1))
    r["B.out"] = c(i["L0_ffn_output_experts"].reshape(4, 2, HB, 64, D).transpose(1, 3, 2, 0, 4).reshape(P, 32, D))
    r["D.keysT"] = c(i["L1_ffn_keys"].transpose(3, 0, 2, 1).reshape(P, 2 * HD, NK))
    r["D.downT"] = c(i["L1_ffn_expert_down"].reshape(EHI, ELO, KC, P).transpose(3, 2, 1, 0).reshape(P, KC * ELO, EHI))
    r["D.up"] = c(i["L1_ffn_expert_up"].reshape(EHI, ELO, D))
    r["C.wk"] = c(i["L1_xattn_w_kv"][:, :1024])
    r["C.wv"] = c(i["L1_xattn_w_kv"][:, 1024:])
    r["mask.cols"] = c(i["mask_BxS2_ik0"].reshape(B, QT, P).transpose(0, 2, 1))
    for k in ("L0_xattn_WQ_b", "L0_xattn_WK_b", "L1_xattn_ln_gamma", "L1_xattn_ln_beta", "L1_ffn_norm_w"):
        r[k + ".cols"] = c(i[k].reshape(KC, P).T)
    for k in ("L0_ffn_w_gate", "L0_ffn_w_q", "L0_ffn_w_k", "L1_ffn_w_q", "g_xattn", "g_ffn", "L1_xattn_gate", "L0_xattn_WV_b", "L0_xattn_WO_b", "L1_xattn_b_out", "L1_xattn_w_q",
              "L1_xattn_w_out"):
        r[k] = c(i[k])
    return r


def kernel(**inputs):
    import concourse.bacc as bacc
    from concourse.bass_utils import run_bass_kernel_spmd

    arrays = layouts({name: np.asarray(value) for name, value in inputs.items()})
    nc = bacc.Bacc("TRN2", target_bir_lowering=False, num_devices=1)
    names = {key: "in_" + key.replace(".", "_") for key in arrays}
    views = {key: nc.dram_tensor(names[key], value.shape, mybir.dt.from_np(value.dtype), kind="ExternalInput").ap()
             for key, value in arrays.items()}
    out = nc.dram_tensor("out_0", (B, S, D), F32, kind="ExternalOutput").ap()
    build(nc, views, out)
    result = run_bass_kernel_spmd(nc, [{names[key]: value for key, value in arrays.items()}], core_ids=[0])
    return result.results[0]["out_0"]
```
